# Optimizing a Trainium2 kernel written in Bass

```python
import numpy as np
import jax
import jax.numpy as jnp

def _softmax(x, axis=-1):
    return jax.nn.softmax(x, axis=axis)

def _gelu(x):
    return jax.nn.gelu(x, approximate=True)

def _silu(x):
    return jax.nn.silu(x)

def _sigmoid(x):
    return jax.nn.sigmoid(x)

def _layernorm(x, axis=-1, eps=1e-05):
    m = jnp.mean(x, axis=axis, keepdims=True)
    v = jnp.var(x, axis=axis, keepdims=True)
    return (x - m) / jnp.sqrt(v + eps)

def _scatter_add(tgt, idx, src, axis=0):
    return tgt.at[idx].add(src)

def _segment_sum(src, seg, n):
    return jax.ops.segment_sum(src, seg, n)
kernel_name = 'mk_gnn_resnorm_d4_gnn_r8_800c17'

def setup_inputs(seed: int=0):
    np.random.seed(seed)
    _w = jnp.asarray

    def _rec_inputs():
        import jax
        import jax.numpy as jnp
        _gk = jax.random.key(seed)
        x = -0.0005121 + 1.001 * jax.random.normal(jax.random.fold_in(_gk, 1), (6250, 64), jnp.float32)
        _s = jax.random.randint(jax.random.fold_in(_gk, 2), (100000,), 0, 6250, jnp.int32)
        _d = jax.random.randint(jax.random.fold_in(_gk, 3), (100000,), 0, 6250, jnp.int32)
        _loop = jnp.arange(6250, dtype=jnp.int32)
        src = jnp.concatenate([_s, _d, _loop])
        dst = jnp.concatenate([_d, _s, _loop])
        _o = jnp.argsort(dst, stable=True)
        src = src[_o]
        dst = dst[_o]
        edge_attr_64 = -8.16379e-05 + 0.999858 * jax.random.normal(jax.random.fold_in(_gk, 12), (206250, 64), jnp.float32)
        edge_type_8 = jax.random.randint(jax.random.fold_in(_gk, 13), (206250,), 0, 8, jnp.int32)
        return (x, src, dst, edge_attr_64, edge_type_8)
    x, src, dst, edge_attr_64, edge_type_8 = _rec_inputs()

    def _L0_gnn_setup():
        import jax, jax.numpy as jnp
        import numpy as np
        N_NODES = 6250
        key = jax.random.key(seed)
        k = jax.random.split(key, 7)
        N, E, D = (N_NODES, 100000, 64)
        x = jax.random.normal(k[0], (N, D), dtype=jnp.float32)
        edge_src = jax.random.randint(k[1], (E,), 0, N, dtype=jnp.int32)
        edge_dst = jax.random.randint(k[2], (E,), 0, N, dtype=jnp.int32)
        s1 = 1.0 / np.sqrt(D)
        w1 = jax.random.uniform(k[3], (D, D), jnp.float32, -s1, s1)
        b1 = jax.random.uniform(k[4], (D,), jnp.float32, -s1, s1)
        w2 = jax.random.uniform(k[5], (D, D), jnp.float32, -s1, s1)
        b2 = jax.random.uniform(k[6], (D,), jnp.float32, -s1, s1)
        return {'x': x, 'edge_src': edge_src, 'edge_dst': edge_dst, 'w1': w1, 'b1': b1, 'w2': w2, 'b2': b2}
    _L0_gnn_all = _L0_gnn_setup()
    _L0_gnn_in = {k: v for k, v in _L0_gnn_all.items() if k in ('w1', 'b1', 'w2', 'b2')}
    del _L0_gnn_all

    def _L1_gnn_setup():
        import jax, jax.numpy as jnp
        import numpy as np
        N_NODES = 6250
        N_EDGES = 100000
        IN_DIM = 64
        OUT_DIM = 64
        NUM_RELS = 8
        key = jax.random.key(seed)
        k1, k2, k3, k4, k5, k6 = jax.random.split(key, 6)
        h = jax.random.normal(k1, (N_NODES, IN_DIM), dtype=jnp.float32)
        fc_weight = jax.random.normal(k2, (NUM_RELS, IN_DIM, OUT_DIM), dtype=jnp.float32) * 0.1
        attn_weight = jax.random.normal(k3, (NUM_RELS, 2 * OUT_DIM, 1), dtype=jnp.float32) * 0.1
        src = jax.random.randint(k4, (N_EDGES,), 0, N_NODES, dtype=jnp.int32)
        dst = jax.random.randint(k5, (N_EDGES,), 0, N_NODES, dtype=jnp.int32)
        etype = jax.random.randint(k6, (N_EDGES,), 0, NUM_RELS, dtype=jnp.int32)
        return {'h': h, 'fc_weight': fc_weight, 'attn_weight': attn_weight, 'src': src, 'dst': dst, 'etype': etype}
    _L1_gnn_all = _L1_gnn_setup()
    _L1_gnn_in = {k: v for k, v in _L1_gnn_all.items() if k in ('fc_weight', 'attn_weight')}
    del _L1_gnn_all

    def _L2_gnn_setup():
        import jax, jax.numpy as jnp
        import numpy as np
        N_NODES = 6250
        N_EDGES = 100000
        D_IN = 64
        D_HID = 128
        D_OUT = 64
        key = jax.random.key(seed)
        ks = jax.random.split(key, 6)
        feat = jax.random.normal(ks[0], (N_NODES, D_IN), dtype=jnp.float32)
        src = jax.random.randint(ks[1], (N_EDGES,), 0, N_NODES, dtype=jnp.int64 if jax.config.read('jax_enable_x64') else jnp.int32)
        dst = jax.random.randint(ks[2], (N_EDGES,), 0, N_NODES, dtype=jnp.int64 if jax.config.read('jax_enable_x64') else jnp.int32)
        eps = jnp.zeros((1,), dtype=jnp.float32)
        W1 = jax.random.normal(ks[3], (D_IN, D_HID), dtype=jnp.float32) * (1.0 / np.sqrt(D_IN))
        b1 = jnp.zeros((D_HID,), dtype=jnp.float32)
        W2 = jax.random.normal(ks[4], (D_HID, D_OUT), dtype=jnp.float32) * (1.0 / np.sqrt(D_HID))
        b2 = jnp.zeros((D_OUT,), dtype=jnp.float32)
        return {'feat': feat, 'src': src, 'dst': dst, 'eps': eps, 'W1': W1, 'b1': b1, 'W2': W2, 'b2': b2}
    _L2_gnn_all = _L2_gnn_setup()
    _L2_gnn_in = {k: v for k, v in _L2_gnn_all.items() if k in ('eps', 'W1', 'b1', 'W2', 'b2')}
    del _L2_gnn_all

    def _L3_gnn_setup():
        import jax, jax.numpy as jnp
        import numpy as np
        N_NODES = 12500
        N_EDGES = 200000
        H, D = (4, 16)
        DE = 16
        DIN_N = 64
        DIN_E = 64
        key = jax.random.key(seed)
        ks = jax.random.split(key, 9)
        return {'inputs_node': jax.random.normal(ks[0], (N_NODES, DIN_N), dtype=jnp.float32), 'inputs_edge': jax.random.normal(ks[1], (N_EDGES, DIN_E), dtype=jnp.float32), 'src': jax.random.randint(ks[2], (N_EDGES,), 0, N_NODES, dtype=jnp.int32), 'dst': jax.random.randint(ks[3], (N_EDGES,), 0, N_NODES, dtype=jnp.int32), 'W_node': jax.random.normal(ks[4], (DIN_N, H * D), dtype=jnp.float32) * (1.0 / np.sqrt(DIN_N)), 'W_edge': jax.random.normal(ks[5], (DIN_E, H * DE), dtype=jnp.float32) * (1.0 / np.sqrt(DIN_E)), 'attn_query': jax.random.normal(ks[6], (H, D), dtype=jnp.float32) * (1.0 / np.sqrt(D)), 'attn_key': jax.random.normal(ks[7], (H, D), dtype=jnp.float32) * (1.0 / np.sqrt(D)), 'attn_edge': jax.random.normal(ks[8], (H, DE), dtype=jnp.float32) * (1.0 / np.sqrt(DE)), 'bias': jnp.zeros((H * D,), dtype=jnp.float32)}
    _L3_gnn_all = _L3_gnn_setup()
    _L3_gnn_in = {k: v for k, v in _L3_gnn_all.items() if k in ('W_node', 'W_edge', 'attn_query', 'attn_key', 'attn_edge', 'bias')}
    del _L3_gnn_all
    return {'x': x, 'src': src, 'dst': dst, 'edge_attr_64': edge_attr_64, 'edge_type_8': edge_type_8, 'L0_gnn_w1': _L0_gnn_in['w1'], 'L0_gnn_b1': _L0_gnn_in['b1'], 'L0_gnn_w2': _L0_gnn_in['w2'], 'L0_gnn_b2': _L0_gnn_in['b2'], 'L1_gnn_fc_weight': _L1_gnn_in['fc_weight'], 'L1_gnn_attn_weight': _L1_gnn_in['attn_weight'], 'L2_gnn_eps': _L2_gnn_in['eps'], 'L2_gnn_W1': _L2_gnn_in['W1'], 'L2_gnn_b1': _L2_gnn_in['b1'], 'L2_gnn_W2': _L2_gnn_in['W2'], 'L2_gnn_b2': _L2_gnn_in['b2'], 'L3_gnn_W_node': _L3_gnn_in['W_node'], 'L3_gnn_W_edge': _L3_gnn_in['W_edge'], 'L3_gnn_attn_query': _L3_gnn_in['attn_query'], 'L3_gnn_attn_key': _L3_gnn_in['attn_key'], 'L3_gnn_attn_edge': _L3_gnn_in['attn_edge'], 'L3_gnn_bias': _L3_gnn_in['bias']}

def reference(x, src, dst, edge_attr_64, edge_type_8, L0_gnn_w1, L0_gnn_b1, L0_gnn_w2, L0_gnn_b2, L1_gnn_fc_weight, L1_gnn_attn_weight, L2_gnn_eps, L2_gnn_W1, L2_gnn_b1, L2_gnn_W2, L2_gnn_b2, L3_gnn_W_node, L3_gnn_W_edge, L3_gnn_attn_query, L3_gnn_attn_key, L3_gnn_attn_edge, L3_gnn_bias):
    import jax
    import jax.numpy as jnp

    def _L0_gnn_ref(x, edge_src, edge_dst, w1, b1, w2, b2):
        import jax, jax.numpy as jnp
        import numpy as np
        N_NODES = 6250
        N = N_NODES
        ones = jnp.ones(edge_src.shape[0], dtype=jnp.float32)
        out_deg = jax.ops.segment_sum(ones, edge_src, num_segments=N)
        in_deg = jax.ops.segment_sum(ones, edge_dst, num_segments=N)
        prod = out_deg[edge_src] * in_deg[edge_dst]
        prod = jnp.where(prod == 0, 1.0, prod)
        norm = jax.lax.rsqrt(prod)
        msg = x[edge_src] * norm[:, None]
        agg = jax.ops.segment_sum(msg, edge_dst, num_segments=N)
        h = jnp.einsum('nd,dh->nh', agg, w1) + b1
        h = jax.nn.gelu(h, approximate=False)
        out = jnp.einsum('nh,hd->nd', h, w2) + b2
        return out

    def _L1_gnn_ref(h, fc_weight, attn_weight, src, dst, etype):
        import jax, jax.numpy as jnp
        import numpy as np
        N_NODES = 6250
        N_EDGES = 100000
        IN_DIM = 64
        OUT_DIM = 64
        NUM_RELS = 8
        N = h.shape[0]
        Z = jnp.einsum('ni,rio->nro', h, fc_weight)
        z_s = Z[src, etype]
        z_d = Z[dst, etype]
        aw = attn_weight[etype, :, 0]
        z2 = jnp.concatenate([z_s, z_d], axis=1)
        e = jax.nn.relu(jnp.sum(z2 * aw, axis=1))
        m = jax.ops.segment_max(e, dst, num_segments=N)
        ex = jnp.exp(e - m[dst])
        denom = jax.ops.segment_sum(ex, dst, num_segments=N)
        alpha = ex / denom[dst]
        h_out = jax.ops.segment_sum(alpha[:, None] * z_s, dst, num_segments=N)
        return h_out

    def _L2_gnn_ref(feat, src, dst, eps, W1, b1, W2, b2):
        import jax, jax.numpy as jnp
        import numpy as np
        N_NODES = 6250
        N_EDGES = 100000
        D_IN = 64
        D_HID = 128
        D_OUT = 64
        msgs = feat[src]
        neigh = jax.ops.segment_sum(msgs, dst, num_segments=N_NODES)
        rst = (1.0 + eps) * feat + neigh
        h = jax.nn.relu(rst @ W1 + b1)
        out = h @ W2 + b2
        return out

    def _L3_gnn_ref(inputs_node, inputs_edge, src, dst, W_node, W_edge, attn_query, attn_key, attn_edge, bias):
        import jax, jax.numpy as jnp
        import numpy as np
        N_NODES = 12500
        N_EDGES = 200000
        H, D = (4, 16)
        DE = 16
        DIN_N = 64
        DIN_E = 64
        n = inputs_node.shape[0]
        hn = (inputs_node @ W_node).reshape(n, H, D)
        he = (inputs_edge @ W_edge).reshape(-1, H, DE)
        w_q = jnp.einsum('nhd,hd->nh', hn, attn_query)
        w_k = jnp.einsum('nhd,hd->nh', hn, attn_key)
        w_e = jnp.einsum('ehd,hd->eh', he, attn_edge)
        logits = jax.nn.leaky_relu(w_k[src] + w_q[dst] + w_e, negative_slope=0.01)
        seg_max = jax.ops.segment_max(logits, dst, num_segments=n)
        seg_max = jnp.where(jnp.isfinite(seg_max), seg_max, 0.0)
        ex = jnp.exp(logits - seg_max[dst])
        denom = jax.ops.segment_sum(ex, dst, num_segments=n)
        attn = ex / denom[dst]
        msg = hn[src] * attn[:, :, None]
        out = jax.ops.segment_sum(msg, dst, num_segments=n)
        out = out.reshape(n, H * D) + bias
        out = out + inputs_node
        return out
    x = _layernorm(x + _L0_gnn_ref(x, src, dst, L0_gnn_w1, L0_gnn_b1, L0_gnn_w2, L0_gnn_b2), axis=-1)
    x = _layernorm(x + _L1_gnn_ref(x, L1_gnn_fc_weight, L1_gnn_attn_weight, src, dst, edge_type_8), axis=-1)
    x = _layernorm(x + _L2_gnn_ref(x, src, dst, L2_gnn_eps, L2_gnn_W1, L2_gnn_b1, L2_gnn_W2, L2_gnn_b2), axis=-1)
    x = _layernorm(x + _L3_gnn_ref(x, edge_attr_64, src, dst, L3_gnn_W_node, L3_gnn_W_edge, L3_gnn_attn_query, L3_gnn_attn_key, L3_gnn_attn_edge, L3_gnn_bias), axis=-1)
    return x

_drawn_inputs = setup_inputs


def setup_inputs(seed=0):
    import zlib

    import numpy as np

    out = dict(_drawn_inputs(seed))
    spreads = {'L2_gnn_b1': (0.0, 0.588), 'L2_gnn_b2': (0.0, 0.366), 'L3_gnn_bias': (0.0, 0.1)}
    factors = {}
    for name, (base, spread) in spreads.items():
        noise = np.random.default_rng([zlib.crc32(name.encode()), seed]).standard_normal(out[name].shape)
        drawn = base * np.exp(spread * noise) if base else spread * noise
        out[name] = jnp.asarray(drawn.astype(out[name].dtype))
    for name, factor in factors.items():
        out[name] = (out[name] * factor).astype(out[name].dtype)
    return out
```

```python
from contextlib import ExitStack
import itertools

import concourse.bass as bass
from concourse import mybir

F32 = mybir.dt.float32
BF16 = mybir.dt.bfloat16
I32 = mybir.dt.int32
ALU = mybir.AluOpType
ACT = mybir.ActivationFunctionType
AX = mybir.AxisListType.X
PE_ONLY = (mybir.EngineType.PE,)

P = 128
N = 6250
NB = -(-N // P)
NLAST = N - (NB - 1) * P
E = 206250
T = -(-E // P)
EP = T * P
G = -(-T // P)
TP = G * P
D = 64
R = 8
H = 4
HD = D // H
CH = 13
SLOTS = 4
BODY = CH * SLOTS
ITERS = T // BODY
RING = 4
OFFS = 28
AW = 68
BANK = 512
BPB = BANK // AW
NG = NB // BPB
W1ROW = D + 1
W3ROW = H * (HD + 1) + H
EPS = 1e-5
LOW = -3.0e38
assert T == BODY * ITERS and NB == BPB * NG


class Count:

    def __init__(self, sem):
        self.sem, self.n = sem, 0

    def on(self, ins, k=1):
        ins.then_inc(self.sem, k)
        self.n += k
        return self.n


def fresh(nc, ctx):
    def sb(name, shape, dt=F32):
        return ctx.enter_context(nc.sbuf_tensor(name, shape, dt))

    def ps(name, shape, dt=F32):
        return ctx.enter_context(nc.psum_tensor(name, shape, dt))

    return sb, ps


def linked(engine, count):

    def link(ins):
        engine.wait_ge(count.sem, count.on(ins))

    return link


def along(ap, n):
    return ap.unsqueeze(2).broadcast_to([ap.shape[0], ap.shape[1], n])


def node_rows(table):
    return table.rearrange("(b p) f -> p b f", p=P)


def build(nc, x, src, dst, edge_attr, etype, w0a, b0a, w0b, b0b, fc, attn, eps2, w2a, b2a, w2b, b2b,
          wn, we, aq, ak, ae, bias3, out):
    with ExitStack() as whole:
        sb, _ = fresh(nc, whole)

        live = []

        def sem(name):
            live.append(nc.alloc_semaphore(name=name))
            return live[-1]

        def recycle():
            nc.all_engine_barrier()
            nc.clear_and_free_semaphores(live)
            nc.all_engine_barrier()
            live.clear()

        def dram(name, shape, dt=F32):
            return nc.dram_tensor(name, shape, dt, kind="Internal").ap()

        ident = sb("ident", [P, P])
        ones = sb("ones", [P, P])
        below = sb("below", [P, P])
        iota = sb("iota", [P, 2 * P])
        zeros16 = sb("zeros16", [P, BANK], BF16)
        src_tl = sb("src_tl", [P, TP], I32)
        idx1_tl = sb("idx1_tl", [P, TP], I32)
        rel_tl = sb("rel_tl", [P, TP])
        offs = sb("offs", [1, T // CH, OFFS], I32)
        mneg_f = sb("mneg_f", [P, T])
        mneg_b = sb("mneg_b", [P, T])
        whole_f = sb("whole_f", [H, P])
        whole_b = sb("whole_b", [H, P])
        first_dst = sb("first_dst", [P, 1], I32)
        rowstart = sb("rowstart", [P, NB], I32)
        xcur = sb("xcur", [P, NB, D])
        agg = sb("agg", [P, NB, AW])

        table0 = dram("table0", (NB * P, D))
        table1 = dram("table1", (NB * P * R, W1ROW))
        table2 = dram("table2", (NB * P, D))
        table3 = dram("table3", (NB * P, W3ROW))
        spill1 = dram("spill1", (T // CH, P, CH * (W1ROW + 1)))
        spill3 = dram("spill3", (T // CH, P, CH * W3ROW))
        offs_d = dram("offs_d", (TP * 2,), I32)
        spread1 = dram("spread1", (EP, R))
        spread3 = dram("spread3", (EP, H))
        nodes1 = dram("nodes1", (NB * P, R))
        nodes3 = dram("nodes3", (NB * P, H))
        score_d = dram("score_d", (H, TP * P))
        prob_d = dram("prob_d", (H, TP * P))
        we_d = dram("we_d", (P, T * H))

        def rows_of(flat):
            full = (G - 1) * P
            rest = E // P - full
            a = flat[0:full * P].rearrange("(g q c) -> q g c", q=P, c=P)
            b = flat[full * P:(full + rest) * P].rearrange("(q c) -> q c", c=P)
            return a, b, rest

        with ExitStack() as st:
            tsb, tps = fresh(nc, st)
            src_r = tsb("src_r", [P, G, P], I32)
            dst_r = tsb("dst_r", [P, G, P], I32)
            et_r = tsb("et_r", [P, G, P], I32)
            dst_s = tsb("dst_s", [P, T], I32)
            prev_s = tsb("prev_s", [P, T], I32)
            next_s = tsb("next_s", [P, T], I32)
            src_f = tsb("src_f", [P, G, P])
            dst_f = tsb("dst_f", [P, G, P])
            et_f = tsb("et_f", [P, G, P])
            rel_f = tsb("rel_f", [P, G, P])
            a_s = tsb("a_s", [P, T])
            base_f = tsb("base_f", [P, G])
            base_i = tsb("base_i", [P, G], I32)
            blk = tsb("blk", [P, G])
            q = tsb("q", [P, G])
            off_f = tsb("off_f", [P, G, 2])
            off_i = tsb("off_i", [P, G, 2], I32)
            edge4 = tsb("edge4", [P, 2, H])
            flag = tsb("flag", [P, 4])
            zero = tsb("zero", [P, 4 * T])
            iota_i = tsb("iota_i", [P, 2 * P], I32)
            turned = tps("turned", [P, 2, 4 * BANK])

            blank = sem("blank")
            loaded = sem("loaded")
            consts = sem("consts")
            iota_ready = sem("iota_ready")
            zero_ready = sem("zero_ready")
            zeroed = sem("zeroed")
            chain = Count(sem("prep_chain"))
            rows_ready = sem("rows_ready")
            turn_done = sem("turn_done")
            turn_used = sem("turn_used")
            off_ready = sem("off_ready")
            off_out = sem("off_out")
            off_in = sem("off_in")
            flags_ready = sem("flags_ready")
            flags_turned = sem("flags_turned")

            LAST = E - (P - 1) * T
            with nc.Block() as block:
                @block.gpsimd
                def _(pool):
                    nc.gpsimd.memset(src_r[:], N).then_inc(blank, 1)
                    nc.gpsimd.memset(dst_r[:], N).then_inc(blank, 1)
                    nc.gpsimd.memset(et_r[:], 0).then_inc(blank, 1)
                    nc.gpsimd.memset(dst_s[:], N).then_inc(blank, 1)
                    nc.gpsimd.memset(prev_s[:], N).then_inc(blank, 1)
                    nc.gpsimd.memset(next_s[:], N).then_inc(blank, 1)
                    nc.gpsimd.memset(xcur[:], 0.0).then_inc(blank, 1)
                    pool.wait_ge(blank, 7)
                    nc.gpsimd.memset(prev_s[0:1, 0:1], -1).then_inc(blank, 1)
                    nc.gpsimd.memset(offs[:], 0).then_inc(blank, 1)
                    nc.gpsimd.iota(iota_i[:], [[1, 2 * P]], base=0, channel_multiplier=0).then_inc(iota_ready, 1)
                    nc.gpsimd.memset(ident[:], 0.0).then_inc(consts, 1)
                    nc.gpsimd.memset(ones[:], 1.0).then_inc(consts, 1)
                    nc.gpsimd.memset(below[:], 1.0).then_inc(consts, 1)
                    pool.wait_ge(consts, 3)
                    nc.gpsimd.affine_select(out=ident[:], in_=ident[:], compare_op=ALU.not_equal, fill=1.0,
                                            base=0, pattern=[[-1, P]], channel_multiplier=1).then_inc(consts, 1)
                    nc.gpsimd.affine_select(out=below[:], in_=below[:], compare_op=ALU.is_gt, fill=0.0,
                                            base=0, pattern=[[1, P]], channel_multiplier=-1).then_inc(consts, 1)

                @block.sync
                def _(sp):
                    sp.wait_ge(blank, 9)
                    for flat, tile in ((src, src_r), (dst, dst_r), (etype, et_r)):
                        a, b, rest = rows_of(flat)
                        sp.dma_start(tile[:, 0:G - 1, :], a).then_inc(loaded, 16)
                        sp.dma_start(tile[0:rest, G - 1, :], b).then_inc(loaded, 16)
                        sp.dma_start(tile[rest:rest + 1, G - 1, 0:E % P], flat[E - E % P:E].unsqueeze(0)).then_inc(loaded, 16)
                    full = (P - 1) * T
                    sp.dma_start(dst_s[0:P - 1, :], dst[0:full].rearrange("(p j) -> p j", j=T)).then_inc(loaded, 16)
                    sp.dma_start(dst_s[P - 1:P, 0:LAST], dst[full:E].unsqueeze(0)).then_inc(loaded, 16)
                    sp.dma_start(prev_s[0:1, 1:T], dst[0:T - 1].unsqueeze(0)).then_inc(loaded, 16)
                    sp.dma_start(prev_s[1:P - 1, :], dst[T - 1:full - 1].rearrange("(p j) -> p j", j=T)).then_inc(loaded, 16)
                    sp.dma_start(prev_s[P - 1:P, 0:LAST + 1], dst[full - 1:E].unsqueeze(0)).then_inc(loaded, 16)
                    sp.dma_start(next_s[0:P - 1, :], dst[1:full + 1].rearrange("(p j) -> p j", j=T)).then_inc(loaded, 16)
                    sp.dma_start(next_s[P - 1:P, 0:LAST - 1], dst[full + 1:E].unsqueeze(0)).then_inc(loaded, 16)
                    sp.dma_start(xcur[:, 0:NB - 1, :], x[0:(NB - 1) * P, :].rearrange("(b p) f -> p b f", p=P)).then_inc(loaded, 16)
                    sp.dma_start(xcur[0:NLAST, NB - 1, :], x[(NB - 1) * P:N, :]).then_inc(loaded, 16)
                    sp.wait_ge(zero_ready, 2)
                    sp.dma_start(spread1.rearrange("(p j) r -> p (j r)", p=P)[:, 0:4 * T], zero[:]).then_inc(zeroed, 16)
                    sp.dma_start(spread1.rearrange("(p j) r -> p (j r)", p=P)[:, 4 * T:8 * T], zero[:]).then_inc(zeroed, 16)
                    sp.dma_start(spread3.rearrange("(p j) r -> p (j r)", p=P), zero[:]).then_inc(zeroed, 16)
                    sp.wait_ge(off_ready, 1)
                    sp.dma_start(offs_d.rearrange("(g q w) -> q g w", q=P, w=2), off_i[:]).then_inc(off_out, 16)
                    sp.wait_ge(off_out, 16)
                    sp.dma_start(offs[:, :, 0:2 * CH], offs_d[0:2 * T].rearrange("(o c k) -> o c k", o=1, k=2 * CH)).then_inc(off_in, 16)
                    sp.wait_ge(off_in, 16)
                    sp.wait_ge(zeroed, 48)
                    sp.wait_ge(loaded, 16 * 18)

                @block.vector
                def _(dve):
                    link = linked(dve, chain)
                    nc.vector.memset(zero[:], 0.0).then_inc(zero_ready, 1)
                    nc.vector.memset(zeros16[:], 0.0).then_inc(zero_ready, 1)
                    dve.wait_ge(iota_ready, 1)
                    link(nc.vector.tensor_copy(iota[:], iota_i[:]))
                    dve.wait_ge(loaded, 16 * 18)
                    nc.vector.tensor_copy(dst_f[:], dst_r[:]).then_inc(chain.sem, 1)
                    nc.vector.tensor_copy(et_f[:], et_r[:]).then_inc(chain.sem, 1)
                    chain.n += 2
                    link(nc.vector.tensor_copy(src_f[:], src_r[:]))
                    link(nc.vector.tensor_reduce(base_f[:], dst_f[:], AX, ALU.min))
                    link(nc.vector.tensor_copy(base_i[:], base_f[:]))
                    link(nc.vector.tensor_scalar(base_i[:], base_i[:], 7, None, ALU.arith_shift_right))
                    link(nc.vector.tensor_copy(base_f[:], base_i[:]))
                    link(nc.vector.tensor_scalar(blk[:], base_f[:], float(P), None, ALU.mult))
                    link(nc.vector.tensor_tensor(rel_f[:], dst_f[:], along(blk[:], P), ALU.subtract))
                    nc.vector.scalar_tensor_tensor(et_f[:], src_f[:], float(R), et_f[:], ALU.mult, ALU.add).then_inc(rows_ready, 1)
                    for w in range(2):
                        link(nc.vector.tensor_scalar(blk[:], base_f[:], float(w), float(NB - 1), ALU.add, ALU.min))
                        link(nc.vector.tensor_scalar(off_f[:, :, w], blk[:], float(AW), None, ALU.mult))
                        for k in range(1, NG):
                            link(nc.vector.tensor_scalar(q[:], blk[:], float(BPB * k), float(BANK - BPB * AW), ALU.is_ge, ALU.mult))
                            link(nc.vector.tensor_tensor(off_f[:, :, w], off_f[:, :, w], q[:], ALU.add))
                    nc.vector.tensor_copy(off_i[:], off_f[:]).then_inc(off_ready, 1)
                    link(nc.vector.tensor_tensor(a_s[:], dst_s[:], prev_s[:], ALU.is_equal))
                    link(nc.vector.tensor_copy(flag[:, 0:1], a_s[:, 0:1]))
                    link(nc.vector.tensor_scalar(mneg_f[:], a_s[:], 1.0, -LOW, ALU.subtract, ALU.mult))
                    link(nc.vector.tensor_tensor(a_s[:], dst_s[:], next_s[:], ALU.is_equal))
                    link(nc.vector.tensor_copy(flag[:, 1:2], a_s[:, T - 1:T]))
                    link(nc.vector.tensor_scalar(mneg_b[:], a_s[:], 1.0, -LOW, ALU.subtract, ALU.mult))
                    link(nc.vector.tensor_tensor(flag[:, 2:3], dst_s[:, 0:1], dst_s[:, T - 1:T], ALU.is_equal))
                    link(nc.vector.tensor_copy(first_dst[:], dst_s[:, 0:1]))
                    for w in range(2):
                        link(nc.vector.tensor_tensor(flag[:, w:w + 1], flag[:, w:w + 1], flag[:, 2:3], ALU.mult))
                        link(nc.vector.tensor_scalar(flag[:, w:w + 1], flag[:, w:w + 1], 1.0, -LOW, ALU.subtract, ALU.mult))
                        nc.vector.tensor_copy(edge4[:, w, :], flag[:, w:w + 1].broadcast_to([P, H])).then_inc(flags_ready, 1)
                    for n, tl in enumerate((src_tl, idx1_tl, rel_tl)):
                        dve.wait_ge(turn_done, n + 1)
                        nc.vector.tensor_copy(tl[:], turned[:, n % 2, 0:TP]).then_inc(turn_used, 1)
                    dve.wait_ge(flags_turned, 1)
                    nc.vector.tensor_copy(whole_f[:], turned[0:H, 1, 0:P]).then_inc(chain.sem, 1)
                    nc.vector.tensor_copy(whole_b[:], turned[0:H, 1, P:2 * P]).then_inc(chain.sem, 1)
                    chain.n += 2
                    dve.wait_ge(chain.sem, chain.n)

                @block.tensor
                def _(pe):
                    pe.wait_ge(consts, 5)
                    pe.wait_ge(rows_ready, 1)
                    for n, rows in enumerate((src_f, et_f, rel_f)):
                        if n >= 2:
                            pe.wait_ge(turn_used, n - 1)
                        for g in range(G):
                            last = nc.tensor.transpose(turned[:, n % 2, g * P:(g + 1) * P], rows[:, g, :], ident[:])
                        last.then_inc(turn_done, 1)
                    pe.wait_ge(flags_ready, 2)
                    pe.wait_ge(turn_used, 2)
                    for w in range(2):
                        last = nc.tensor.transpose(turned[0:H, 1, w * P:(w + 1) * P], edge4[:, w, :], ident[:])
                    last.then_inc(flags_turned, 1)


        serial = itertools.count()

        def held(engine, value):
            if isinstance(value, int):
                return value
            register = engine.alloc_register(f"held_{next(serial)}")
            engine.reg_mov(register, value)
            return engine.snap(register)

        def steps(engine, body):
            body(0, True)
            with engine.Fori(1, ITERS) as i:
                body(i, False)

        with ExitStack() as st:
            tsb, tps = fresh(nc, st)
            part_i = tsb("part_i", [P, TP], I32)
            lo_f = tsb("lo_f", [P, TP])
            hi_f = tsb("hi_f", [P, TP])
            lo_hot = tsb("lo_hot", [P, SLOTS, CH, P], BF16)
            hi_hot = tsb("hi_hot", [P, SLOTS, CH, NB], BF16)
            deg = tsb("deg", [P, NB])
            root = tsb("root", [P, NB])
            xs = tsb("xs", [P, NB, D])
            deg_ps = tps("deg_ps", [P, NB])
            chain = Count(sem("deg_chain"))
            hot_ready = sem("hot_ready")
            counted = sem("counted")
            deg_ready = sem("deg_ready")
            root_ready = sem("root_ready")
            xs_ready = sem("xs_ready")
            xs_out = sem("xs_out")
            with nc.Block() as block:
                @block.vector
                def _(dve):
                    link = linked(dve, chain)
                    link(nc.vector.tensor_scalar(part_i[:], src_tl[:], P - 1, None, ALU.bitwise_and))
                    link(nc.vector.tensor_copy(lo_f[:], part_i[:]))
                    link(nc.vector.tensor_scalar(part_i[:], src_tl[:], 7, None, ALU.arith_shift_right))
                    link(nc.vector.tensor_copy(hi_f[:], part_i[:]))

                    def body(i, first):
                        for s in range(SLOTS):
                            c = i * SLOTS + s
                            if not first:
                                dve.wait_ge(counted, c - SLOTS + 1)
                            nc.vector.tensor_tensor(
                                lo_hot[:, s], iota[:, 0:P].unsqueeze(1).broadcast_to([P, CH, P]),
                                along(lo_f[:, bass.ds(c * CH, CH)], P), ALU.is_equal).then_inc(hot_ready, 1)
                            nc.vector.tensor_tensor(
                                hi_hot[:, s], iota[:, 0:NB].unsqueeze(1).broadcast_to([P, CH, NB]),
                                along(hi_f[:, bass.ds(c * CH, CH)], NB), ALU.is_equal).then_inc(hot_ready, 1)

                    steps(dve, body)
                    dve.wait_ge(counted, T // CH)
                    nc.vector.tensor_scalar(deg[:], deg_ps[:], 1.0, None, ALU.max).then_inc(deg_ready, 1)
                    dve.wait_ge(root_ready, 1)
                    link(nc.vector.reciprocal(deg[:], root[:]))
                    nc.vector.tensor_tensor(xs[:], xcur[:], along(deg[:], D), ALU.mult).then_inc(xs_ready, 1)

                @block.tensor
                def _(pe):
                    nc.tensor.matmul(deg_ps[:], zeros16[:, 0:P], zeros16[:, 0:NB], start=True, stop=True, skip_group_check=True)

                    def body(i, first):
                        for s in range(SLOTS):
                            c = i * SLOTS + s
                            pe.wait_ge(hot_ready, 2 * (c + 1))
                            for k in range(CH):
                                last = nc.tensor.matmul(deg_ps[:], lo_hot[:, s, k], hi_hot[:, s, k], start=False, stop=True,
                                                        skip_group_check=True)
                            last.then_inc(counted, 1)

                    steps(pe, body)

                @block.scalar
                def _(act):
                    act.wait_ge(deg_ready, 1)
                    nc.scalar.sqrt(root[:], deg[:]).then_inc(root_ready, 1)

                @block.sync
                def _(sp):
                    sp.wait_ge(xs_ready, 1)
                    sp.dma_start(node_rows(table0), xs[:]).then_inc(xs_out, 16)
                    sp.wait_ge(xs_out, 16)

        def onehot_sums(pe, acc, hot, hot_ready, summed, arrived, rows_at, width):
            for b in range(NG):
                nc.tensor.matmul(acc[:, b * BANK:(b + 1) * BANK], zeros16[:, 0:P], zeros16[:], start=True, stop=True,
                                 skip_group_check=True)

            def body(i, first):
                for s in range(SLOTS):
                    c = i * SLOTS + s
                    _, at = nc.values_load_multi_w_load_instructions(
                        offs[0:1, bass.ds(c, 1), :], engines=PE_ONLY, min_val=0, max_val=(NG - 1) * BANK + (BPB - 1) * AW)
                    arrived(pe, i, s)
                    for k in range(CH):
                        n = i * BODY + s * CH + k
                        pe.wait_ge(hot_ready, n + 1)
                        for w in range(2):
                            last = nc.tensor.matmul(acc[:, bass.ds(at[2 * k + w], width)], hot[:, n_ring(s, k), w * P:(w + 1) * P],
                                                    rows_at(s, k), start=False, stop=True, skip_group_check=True)
                        last.then_inc(summed, 1)

            steps(pe, body)

        def n_ring(s, k):
            return (s * CH + k) % RING

        def make_onehots(dve, hot, hot_ready, summed, chunk_ready, per_chunk, rel_c, weight_c=None, before=None):

            def body(i, first):
                for s in range(SLOTS):
                    c = i * SLOTS + s
                    dve.wait_ge(chunk_ready, per_chunk * (c + 1))
                    if before is not None:
                        before(i, s, first)
                    for k in range(CH):
                        n = i * BODY + s * CH + k
                        if not (first and s * CH + k < RING):
                            dve.wait_ge(summed, n - RING + 1)
                        if weight_c is None:
                            ins = nc.vector.tensor_scalar(hot[:, n_ring(s, k)], iota[:], rel_c[:, s, k:k + 1], None, ALU.is_equal)
                        else:
                            ins = nc.vector.tensor_scalar(hot[:, n_ring(s, k)], iota[:], rel_c[:, s, k:k + 1],
                                                          weight_c[:, s, k:k + 1], ALU.is_equal, ALU.mult)
                        ins.then_inc(hot_ready, 1)

            steps(dve, body)

        def keep_sums(dve, acc, summed, kept, width):
            dve.wait_ge(summed, T)
            for b in range(NG):
                nc.vector.tensor_copy(agg[:, b * BPB:(b + 1) * BPB, 0:width],
                                      acc[:, b * BANK:b * BANK + BPB * AW].rearrange("p (b f) -> p b f", f=AW)[:, :, 0:width])\
                    .then_inc(kept, 1)
            dve.wait_ge(kept, NG)

        def gather_rows(pool, table, rows, row, idx_c, chunk_ready, per_chunk, one, gathered):

            def body(i, first):
                for s in range(SLOTS):
                    c = i * SLOTS + s
                    want = held(pool, per_chunk * (c + 1))
                    pool.wait_ge(one, 1)
                    pool.wait_ge(chunk_ready, want)
                    for k in range(CH):
                        pool.indirect_dma_start(rows[:, s, k, 0:row], None, table,
                                                bass.IndirectOffsetOnAxis(idx_c[:, s, k:k + 1], 0)).then_inc(gathered[s], 16)

            steps(pool, body)

        def gather_sum(tag, table):
            with ExitStack() as st:
                tsb, tps = fresh(nc, st)
                rows = tsb(f"rows_{tag}", [P, SLOTS, CH, D + 1])
                idx_c = tsb(f"idx_c_{tag}", [P, SLOTS, CH], I32)
                rel_c = tsb(f"rel_c_{tag}", [P, SLOTS, CH])
                hot = tsb(f"hot_{tag}", [P, RING, 2 * P])
                acc = tps(f"acc_{tag}", [P, NG * BANK])
                chunk_ready = sem(f"chunk_ready_{tag}")
                gathered = [sem(f"gathered_{tag}_{s}") for s in range(SLOTS)]
                hot_ready = sem(f"hot_ready_{tag}")
                summed = sem(f"summed_{tag}")
                kept = sem(f"kept_{tag}")
                one = sem(f"one_{tag}")
                with nc.Block() as block:
                    @block.scalar
                    def _(act):
                        def body(i, first):
                            for s in range(SLOTS):
                                c = i * SLOTS + s
                                if not first:
                                    act.wait_ge(summed, i * BODY + (s + 1 - SLOTS) * CH)
                                nc.scalar.copy(idx_c[:, s], src_tl[:, bass.ds(c * CH, CH)]).then_inc(chunk_ready, 1)
                                nc.scalar.copy(rel_c[:, s], rel_tl[:, bass.ds(c * CH, CH)]).then_inc(chunk_ready, 1)

                        steps(act, body)

                    @block.gpsimd
                    def _(pool):
                        gather_rows(pool, table, rows, D, idx_c, chunk_ready, 2, one, gathered)

                    @block.vector
                    def _(dve):
                        nc.vector.memset(rows[:, :, :, D:D + 1], 1.0).then_inc(one, 1)
                        make_onehots(dve, hot, hot_ready, summed, chunk_ready, 2, rel_c)
                        keep_sums(dve, acc, summed, kept, D + 1)

                    @block.tensor
                    def _(pe):
                        pe.wait_ge(one, 1)

                        def arrived(pe, i, s):
                            pe.wait_ge(gathered[s], 16 * CH * (i + 1))

                        onehot_sums(pe, acc, hot, hot_ready, summed, arrived, lambda s, k: rows[:, s, k, :], D + 1)

        def gather_spill(tag, table, idx_tl, row, width, spill, score_tl, score_at, heads):
            with ExitStack() as st:
                tsb, tps = fresh(nc, st)
                rows = tsb(f"rows_{tag}", [P, SLOTS, CH, width])
                idx_c = tsb(f"idx_c_{tag}", [P, SLOTS, CH], I32)
                chunk_ready = sem(f"chunk_ready_{tag}")
                gathered = [sem(f"gathered_{tag}_{s}") for s in range(SLOTS)]
                spilled = [sem(f"spilled_{tag}_{s}") for s in range(SLOTS)]
                scored = sem(f"scored_{tag}")
                one = sem(f"one_{tag}")
                with nc.Block() as block:
                    @block.scalar
                    def _(act):
                        def body(i, first):
                            for s in range(SLOTS):
                                c = i * SLOTS + s
                                if not first:
                                    act.wait_ge(spilled[s], 16 * i)
                                    act.wait_ge(scored, c - SLOTS + 1)
                                nc.scalar.copy(idx_c[:, s], idx_tl[:, bass.ds(c * CH, CH)]).then_inc(chunk_ready, 1)

                        steps(act, body)

                    @block.gpsimd
                    def _(pool):
                        gather_rows(pool, table, rows, row, idx_c, chunk_ready, 1, one, gathered)

                    @block.vector
                    def _(dve):
                        nc.vector.memset(rows[:, :, :, row % width:width], 1.0).then_inc(one, 1)

                        def body(i, first):
                            for s in range(SLOTS):
                                c = i * SLOTS + s
                                dve.wait_ge(gathered[s], 16 * CH * (i + 1))
                                nc.vector.tensor_copy(score_tl[:, :, bass.ds(c * CH, CH)],
                                                      rows[:, s, :, score_at:score_at + heads].rearrange("p k h -> p h k"))\
                                    .then_inc(scored, 1)

                        steps(dve, body)

                    @block.sync
                    def _(sp):
                        sp.wait_ge(one, 1)

                        def body(i, first):
                            for s in range(SLOTS):
                                c = i * SLOTS + s
                                sp.wait_ge(gathered[s], 16 * CH * (i + 1))
                                sp.dma_start(spill[bass.ds(c, 1)].rearrange("o p f -> (o p) f"),
                                             rows[:, s].rearrange("p k f -> p (k f)")).then_inc(spilled[s], 16)

                        steps(sp, body)
                        for s in range(SLOTS):
                            sp.wait_ge(spilled[s], 16 * ITERS)

        def spill_sum(tag, spill, width, heads, prob_tl):
            with ExitStack() as st:
                tsb, tps = fresh(nc, st)
                rows = tsb(f"rows_{tag}", [P, SLOTS, CH, width])
                rel_c = tsb(f"rel_c_{tag}", [P, SLOTS, CH])
                prob_c = tsb(f"prob_c_{tag}", [P, SLOTS, CH, heads])
                hot = tsb(f"hot_{tag}", [P, RING, 2 * P])
                acc = tps(f"acc_{tag}", [P, NG * BANK])
                sums = width if heads == 1 else heads * (HD + 1)
                msg = tsb(f"msg_{tag}", [P, SLOTS, CH, sums]) if heads > 1 else rows
                chunk_ready = sem(f"chunk_ready_{tag}")
                loaded_s = [sem(f"loaded_{tag}_{s}") for s in range(SLOTS)]
                hot_ready = sem(f"hot_ready_{tag}")
                msg_ready = sem(f"msg_ready_{tag}")
                summed = sem(f"summed_{tag}")
                kept = sem(f"kept_{tag}")
                with nc.Block() as block:
                    @block.sync
                    def _(sp):
                        def body(i, first):
                            for s in range(SLOTS):
                                c = i * SLOTS + s
                                if not first:
                                    sp.wait_ge(summed, i * BODY + (s + 1 - SLOTS) * CH)
                                sp.dma_start(rows[:, s].rearrange("p k f -> p (k f)"),
                                             spill[bass.ds(c, 1)].rearrange("o p f -> (o p) f")).then_inc(loaded_s[s], 16)

                        steps(sp, body)

                    @block.scalar
                    def _(act):
                        def body(i, first):
                            for s in range(SLOTS):
                                c = i * SLOTS + s
                                if not first:
                                    act.wait_ge(summed, i * BODY + (s + 1 - SLOTS) * CH)
                                nc.scalar.copy(rel_c[:, s], rel_tl[:, bass.ds(c * CH, CH)]).then_inc(chunk_ready, 1)
                                nc.scalar.copy(prob_c[:, s], prob_tl[:, :, bass.ds(c * CH, CH)].rearrange("p h k -> p k h"))\
                                    .then_inc(chunk_ready, 1)

                        steps(act, body)

                    @block.vector
                    def _(dve):
                        def weigh(i, s, first):
                            dve.wait_ge(loaded_s[s], 16 * (i + 1))
                            nc.vector.tensor_tensor(
                                msg[:, s].rearrange("p k (h d) -> p k h d", h=heads),
                                rows[:, s, :, 0:sums].rearrange("p k (h d) -> p k h d", h=heads),
                                prob_c[:, s].unsqueeze(3).broadcast_to([P, CH, heads, HD + 1]), ALU.mult).then_inc(msg_ready, 1)

                        if heads == 1:
                            make_onehots(dve, hot, hot_ready, summed, chunk_ready, 2, rel_c, weight_c=prob_c[:, :, :, 0])
                        else:
                            make_onehots(dve, hot, hot_ready, summed, chunk_ready, 2, rel_c, before=weigh)
                        keep_sums(dve, acc, summed, kept, sums)

                    @block.tensor
                    def _(pe):
                        def arrived(pe, i, s):
                            if heads == 1:
                                pe.wait_ge(loaded_s[s], 16 * (i + 1))
                            else:
                                pe.wait_ge(msg_ready, i * SLOTS + s + 1)

                        onehot_sums(pe, acc, hot, hot_ready, summed, arrived, lambda s, k: msg[:, s, k, :], sums)

        def normalise(tag, y, tmp, small, result_out=None):
            chain = Count(sem(f"norm_chain_{tag}"))
            var_ready = sem(f"var_ready_{tag}")
            std_ready = sem(f"std_ready_{tag}")
            x_ready = sem(f"x_ready_{tag}")
            x_out = sem(f"x_out_{tag}")
            mean, var, std, rstd = (small[:, n] for n in range(4))
            with nc.Block() as block:
                @block.vector
                def _(dve):
                    link = linked(dve, chain)
                    link(nc.vector.reduce_sum(mean, y[:], AX))
                    link(nc.vector.tensor_scalar(mean, mean, 1.0 / D, None, ALU.mult))
                    link(nc.vector.tensor_tensor(y[:], y[:], along(mean, D), ALU.subtract))
                    link(nc.vector.tensor_tensor(tmp[:], y[:], y[:], ALU.mult))
                    link(nc.vector.reduce_sum(var, tmp[:], AX))
                    nc.vector.tensor_scalar(var, var, 1.0 / D, EPS, ALU.mult, ALU.add).then_inc(var_ready, 1)
                    dve.wait_ge(std_ready, 1)
                    link(nc.vector.reciprocal(rstd, std))
                    nc.vector.tensor_tensor(xcur[:], y[:], along(rstd, D), ALU.mult).then_inc(x_ready, 1)

                @block.scalar
                def _(act):
                    act.wait_ge(var_ready, 1)
                    nc.scalar.sqrt(std, var).then_inc(std_ready, 1)

                @block.sync
                def _(sp):
                    if result_out is not None:
                        sp.wait_ge(x_ready, 1)
                        n = result_out(sp, x_out)
                        sp.wait_ge(x_out, n)

        def mlp(tag, w_in, b_in, w_out, b_out, hidden, func, y, prepare):
            with ExitStack() as st:
                tsb, tps = fresh(nc, st)
                wa = tsb(f"wa_{tag}", [D, hidden])
                ba = tsb(f"ba_{tag}", [hidden, 1])
                wb = tsb(f"wb_{tag}", [hidden, D])
                bb = tsb(f"bb_{tag}", [P, D])
                h = tsb(f"h_{tag}", [P, BPB, D])
                h_t = tsb(f"h_t_{tag}", [D, BPB * P])
                g_t = tsb(f"g_t_{tag}", [hidden, BPB * P])
                t_ps = tps(f"t_ps_{tag}", [D, 2 * BANK])
                g_ps = tps(f"g_ps_{tag}", [hidden, 2 * BANK])
                o_ps = tps(f"o_ps_{tag}", [P, BPB * D])
                loaded = sem(f"weights_{tag}")
                chain = Count(sem(f"mlp_chain_{tag}"))
                h_ready = sem(f"h_ready_{tag}")
                t_done = sem(f"t_done_{tag}")
                ht_ready = sem(f"ht_ready_{tag}")
                g_done = sem(f"g_done_{tag}")
                gt_ready = sem(f"gt_ready_{tag}")
                o_done = sem(f"o_done_{tag}")
                y_done = sem(f"y_done_{tag}")
                with nc.Block() as block:
                    @block.sync
                    def _(sp):
                        sp.dma_start(wa[:], w_in).then_inc(loaded, 16)
                        sp.dma_start(ba[:], b_in.unsqueeze(1)).then_inc(loaded, 16)
                        sp.dma_start(wb[:], w_out).then_inc(loaded, 16)
                        sp.dma_start(bb[:], b_out.partition_broadcast(P)).then_inc(loaded, 16)

                    @block.vector
                    def _(dve):
                        link = linked(dve, chain)
                        group = prepare(dve, link, h)
                        dve.wait_ge(loaded, 64)
                        link(nc.vector.tensor_tensor(y[:], xcur[:], bb[:].unsqueeze(1).broadcast_to([P, NB, D]), ALU.add))
                        with dve.Fori(0, NG) as g:
                            group(g).then_inc(h_ready, 1)
                            dve.wait_ge(t_done, g + 1)
                            nc.vector.tensor_copy(h_t[:], t_ps[:, 0:BPB * P]).then_inc(ht_ready, 1)
                            dve.wait_ge(o_done, g + 1)
                            yg = y[:, bass.ds(g * BPB, BPB), :]
                            nc.vector.tensor_tensor(yg, yg, o_ps[:].rearrange("p (b f) -> p b f", f=D), ALU.add).then_inc(y_done, 1)
                        dve.wait_ge(y_done, NG)

                    @block.tensor
                    def _(pe):
                        pe.wait_ge(loaded, 64)
                        with pe.Fori(0, NG) as g:
                            want = held(pe, g + 1)
                            pe.wait_ge(loaded, 64)
                            pe.wait_ge(h_ready, want)
                            for b in range(BPB):
                                last = nc.tensor.transpose(t_ps[:, b * P:(b + 1) * P], h[:, b], ident[:])
                            last.then_inc(t_done, 1)
                            want = held(pe, g + 1)
                            pe.wait_ge(loaded, 64)
                            pe.wait_ge(ht_ready, want)
                            for a, b in ((0, BANK), (BANK, BPB * P)):
                                last = nc.tensor.matmul(g_ps[:, a:b], wa[:], h_t[:, a:b], start=True, stop=True)
                            last.then_inc(g_done, 1)
                            want = held(pe, g + 1)
                            pe.wait_ge(loaded, 64)
                            pe.wait_ge(gt_ready, want)
                            for b in range(BPB):
                                last = nc.tensor.matmul(o_ps[:, b * D:(b + 1) * D], g_t[:, b * P:(b + 1) * P], wb[:], start=True, stop=True)
                            last.then_inc(o_done, 1)

                    @block.scalar
                    def _(act):
                        act.wait_ge(loaded, 64)
                        with act.Fori(0, NG) as g:
                            act.wait_ge(g_done, g + 1)
                            nc.scalar.activation(g_t[:], g_ps[:, 0:BPB * P], func, bias=ba[:, 0:1]).then_inc(gt_ready, 1)

        def project(tag, weights, cols, split, table, nodes, emit, make_weights):
            with ExitStack() as st:
                tsb, tps = fresh(nc, st)
                wsum = tsb(f"wsum_{tag}", [D, cols])
                h = tsb(f"ph_{tag}", [P, BPB, D])
                h_t = tsb(f"ph_t_{tag}", [D, BPB * P])
                stage, node = emit["buffers"](tsb)
                t_ps = tps(f"pt_ps_{tag}", [D, 2 * BANK])
                z_ps = tps(f"z_ps_{tag}", [P, 3, 2, BANK])
                chain = Count(sem(f"proj_chain_{tag}"))
                w_ready = sem(f"w_ready_{tag}")
                h_ready = sem(f"ph_ready_{tag}")
                t_done = sem(f"pt_done_{tag}")
                ht_ready = sem(f"pht_ready_{tag}")
                z_done = sem(f"z_done_{tag}")
                z_kept = sem(f"z_kept_{tag}")
                staged = sem(f"staged_{tag}")
                nodes_out = sem(f"nodes_out_{tag}")
                loaded = sem(f"pw_{tag}")

                with nc.Block() as block:
                    @block.sync
                    def _(sp):
                        make_weights["load"](sp, loaded)

                        def body(g, first):
                            for b in range(BPB):
                                sp.wait_ge(z_kept, g * BPB + b + 1)
                                emit["store"](sp, table, stage, g * BPB + b, b).then_inc(staged, 16)

                        body(0, True)
                        with sp.Fori(1, NG) as g:
                            body(g, False)
                        sp.dma_start(node_rows(nodes), node[:]).then_inc(nodes_out, 16)
                        sp.wait_ge(staged, 16 * NB)
                        sp.wait_ge(nodes_out, 16)

                    @block.vector
                    def _(dve):
                        link = linked(dve, chain)
                        make_weights["compute"](dve, link, loaded, tsb, wsum).then_inc(w_ready, 1)
                        emit["ones"](link, stage)

                        def body(g, first):
                            nc.vector.tensor_copy(h[:], xcur[:, bass.ds(g * BPB, BPB), :] if not first else xcur[:, 0:BPB, :])\
                                .then_inc(h_ready, 1)
                            dve.wait_ge(t_done, g + 1)
                            nc.vector.tensor_copy(h_t[:], t_ps[:, 0:BPB * P]).then_inc(ht_ready, 1)
                            if not first:
                                dve.wait_ge(staged, g * (16 * BPB))
                            for b in range(BPB):
                                dve.wait_ge(z_done, g * BPB + b + 1)
                                emit["keep"](z_ps[:, b % 3], stage, node, g * BPB + b, b).then_inc(z_kept, 1)

                        body(0, True)
                        with dve.Fori(1, NG) as g:
                            body(g, False)

                    @block.tensor
                    def _(pe):
                        pe.wait_ge(w_ready, 1)

                        def body(g, first):
                            want = held(pe, g + 1)
                            pe.wait_ge(w_ready, 1)
                            pe.wait_ge(h_ready, want)
                            for b in range(BPB):
                                last = nc.tensor.transpose(t_ps[:, b * P:(b + 1) * P], h[:, b], ident[:])
                            last.then_inc(t_done, 1)
                            want = held(pe, g + 1)
                            pe.wait_ge(w_ready, 1)
                            pe.wait_ge(ht_ready, want)
                            for b in range(BPB):
                                if b >= 3:
                                    pe.wait_ge(z_kept, g * BPB + b - 2)
                                elif not first:
                                    pe.wait_ge(z_kept, g * BPB)
                                for n, (lo, hi) in enumerate(split):
                                    last = nc.tensor.matmul(z_ps[:, b % 3, n, 0:hi - lo], h_t[:, b * P:(b + 1) * P], wsum[:, lo:hi],
                                                            start=True, stop=True)
                                last.then_inc(z_done, 1)

                        body(0, True)
                        with pe.Fori(1, NG) as g:
                            body(g, False)

        def spread(tag, cols, node, nodes, edges, values):
            scattered = sem(f"scattered_{tag}")
            first_in = sem(f"first_in_{tag}")
            loaded = sem(f"spread_in_{tag}")
            done = sem(f"spread_done_{tag}")
            with ExitStack() as st:
                tsb, _ = fresh(nc, st)
                first = tsb(f"first_{tag}", [P, cols])
                inside = tsb(f"inside_{tag}", [P, T])
                with nc.Block() as block:
                    @block.gpsimd
                    def _(pool):
                        pool.indirect_dma_start(first[:], None, nodes, bass.IndirectOffsetOnAxis(first_dst[:, 0:1], 0)).then_inc(first_in, 16)
                        for b in range(NB):
                            k = P if b < NB - 1 else NLAST + 1
                            pool.indirect_dma_start(edges, bass.IndirectOffsetOnAxis(rowstart[0:k, b:b + 1], 0), node[0:k, b, :], None)\
                                .then_inc(scattered, 16)

                    @block.sync
                    def _(sp):
                        sp.wait_ge(scattered, 16 * NB)
                        sp.dma_start(values[:], edges.rearrange("(p j) r -> p j r", p=P)).then_inc(loaded, 16)

                    @block.vector
                    def _(dve):
                        nc.vector.tensor_scalar(inside[:], mneg_f[:], 0.0, None, ALU.is_equal).then_inc(done, 1)
                        dve.wait_ge(done, 1)
                        dve.wait_ge(first_in, 16)
                        dve.wait_ge(loaded, 16)
                        for r in range(cols):
                            nc.vector.tensor_tensor_scan(values[:, :, r], inside[:], values[:, :, r], first[:, r:r + 1], ALU.mult, ALU.add)\
                                .then_inc(done, 1)
                        dve.wait_ge(done, 1 + cols)

        def tiles_to_scan(tag, heads, tl, scan):
            with ExitStack() as st:
                tsb, tps = fresh(nc, st)
                row = tsb(f"row_{tag}", [P, 2, G, P])
                turned = tps(f"turned_{tag}", [P, 2, 4 * BANK])
                turn_done = sem(f"turn_done_{tag}")
                row_ready = sem(f"row_ready_{tag}")
                row_out = [sem(f"row_out_{tag}{n}") for n in range(2)]
                scan_in = sem(f"scan_in_{tag}")
                with nc.Block() as block:
                    @block.tensor
                    def _(pe):
                        for h in range(heads):
                            if h >= 2:
                                pe.wait_ge(row_ready, h - 1)
                            for g in range(G):
                                k = min(P, T - g * P)
                                last = nc.tensor.transpose(turned[0:k, h % 2, g * P:(g + 1) * P], tl[:, h, g * P:g * P + k], ident[:])
                            last.then_inc(turn_done, 1)

                    @block.vector
                    def _(dve):
                        k = T - (G - 1) * P
                        for h in range(heads):
                            dve.wait_ge(turn_done, h + 1)
                            if h >= 2:
                                dve.wait_ge(row_out[h % 2], 32 * (h // 2))
                            nc.vector.tensor_copy(row[:, h % 2, 0:G - 1], turned[:, h % 2, 0:(G - 1) * P].rearrange("p (g c) -> p g c", c=P))
                            nc.vector.tensor_copy(row[0:k, h % 2, G - 1], turned[0:k, h % 2, (G - 1) * P:TP]).then_inc(row_ready, 1)

                    @block.sync
                    def _(sp):
                        k = T - (G - 1) * P
                        for h in range(heads):
                            sp.wait_ge(row_ready, h + 1)
                            flat = score_d[h]
                            sp.dma_start(flat[0:(G - 1) * P * P].rearrange("(g q c) -> q g c", q=P, c=P), row[:, h % 2, 0:G - 1]).then_inc(row_out[h % 2], 16)
                            sp.dma_start(flat[(G - 1) * P * P:EP].rearrange("(q c) -> q c", c=P), row[0:k, h % 2, G - 1]).then_inc(row_out[h % 2], 16)
                            sp.wait_ge(row_out[h % 2], 32 * (h // 2 + 1))
                            sp.dma_start(scan[:, h], flat[0:EP].rearrange("(p j) -> p j", p=P)).then_inc(scan_in, 16)
                        sp.wait_ge(scan_in, 16 * heads)

        def scan_to_tiles(tag, heads, scan, tl):
            with ExitStack() as st:
                tsb, tps = fresh(nc, st)
                row = tsb(f"row_{tag}", [P, 2, G, P])
                turned = tps(f"turned_{tag}", [P, 2, 4 * BANK])
                scan_out = sem(f"scan_out_{tag}")
                row_in = [sem(f"row_in_{tag}{n}") for n in range(2)]
                turn_done = sem(f"turn_done_{tag}")
                tile_ready = sem(f"tile_ready_{tag}")
                with nc.Block() as block:
                    @block.sync
                    def _(sp):
                        k = T - (G - 1) * P
                        for h in range(heads):
                            flat = prob_d[h]
                            sp.dma_start(flat[0:EP].rearrange("(p j) -> p j", p=P), scan[:, h]).then_inc(scan_out, 16)
                            sp.wait_ge(scan_out, 16 * (h + 1))
                            if h >= 2:
                                sp.wait_ge(turn_done, h - 1)
                            sp.dma_start(row[:, h % 2, 0:G - 1], flat[0:(G - 1) * P * P].rearrange("(g q c) -> q g c", q=P, c=P)).then_inc(row_in[h % 2], 16)
                            sp.dma_start(row[0:k, h % 2, G - 1], flat[(G - 1) * P * P:EP].rearrange("(q c) -> q c", c=P)).then_inc(row_in[h % 2], 16)

                    @block.tensor
                    def _(pe):
                        for h in range(heads):
                            pe.wait_ge(row_in[h % 2], 32 * (h // 2 + 1))
                            if h >= 2:
                                pe.wait_ge(tile_ready, h - 1)
                            for g in range(G):
                                k = min(P, T - g * P)
                                last = nc.tensor.transpose(turned[:, h % 2, g * P:g * P + k], row[0:k, h % 2, g], ident[0:k, 0:k])
                            last.then_inc(turn_done, 1)

                    @block.vector
                    def _(dve):
                        for h in range(heads):
                            dve.wait_ge(turn_done, h + 1)
                            nc.vector.tensor_copy(tl[:, h, 0:T], turned[:, h % 2, 0:T]).then_inc(tile_ready, 1)
                        dve.wait_ge(tile_ready, heads)

        def run_softmax(tag, heads, score, best):
            with ExitStack() as st:
                tsb, tps = fresh(nc, st)
                tail = tsb(f"tail_{tag}", [P, heads])
                row = tsb(f"tails_{tag}", [heads, P])
                state = tsb(f"states_{tag}", [heads, P])
                before = tsb(f"before_{tag}", [heads, P])
                carry = tsb(f"carry_{tag}", [P, heads])
                row_ps = tps(f"row_ps_{tag}", [heads, BANK])
                col_ps = tps(f"col_ps_{tag}", [P, BANK])
                chain = Count(sem(f"softmax_chain_{tag}"))
                tail_ready = sem(f"tail_ready_{tag}")
                row_done = sem(f"row_done_{tag}")
                before_ready = sem(f"before_ready_{tag}")
                col_done = sem(f"col_done_{tag}")
                diff_ready = sem(f"diff_ready_{tag}")
                with nc.Block() as block:
                    @block.vector
                    def _(dve):
                        link = linked(dve, chain)

                        def way(n, mneg, goes_on, src, flip, end):
                            v = (lambda a: a[:, ::-1]) if flip else (lambda a: a)
                            for h in range(heads):
                                link(nc.vector.tensor_tensor_scan(v(best[:, h]), v(mneg[:]), v(src[:, h]), LOW, ALU.add, ALU.max)) \
                                    if src is not best else link(nc.vector.tensor_tensor_scan(v(tmp[:]), v(mneg[:]), v(src[:, h]), LOW, ALU.add, ALU.max))
                                got = best[:, h] if src is not best else tmp[:]
                                link(nc.vector.tensor_copy(tail[:, h:h + 1], got[:, end:end + 1]))
                            nc.vector.tensor_copy(carry[:], tail[:]).then_inc(tail_ready, 1)
                            dve.wait_ge(row_done, n + 1)
                            link(nc.vector.tensor_copy(row[:], row_ps[:, 0:P]))
                            link(nc.vector.tensor_tensor_scan(v(state[:]), v(goes_on[0:heads, :]), v(row[:]), LOW, ALU.add, ALU.max))
                            link(nc.vector.memset(before[:], LOW))
                            if flip:
                                ins = nc.vector.tensor_copy(before[:, 0:P - 1], state[:, 1:P])
                            else:
                                ins = nc.vector.tensor_copy(before[:, 1:P], state[:, 0:P - 1])
                            ins.then_inc(before_ready, 1)
                            dve.wait_ge(col_done, n + 1)
                            link(nc.vector.tensor_copy(carry[:], col_ps[:, 0:heads]))
                            for h in range(heads):
                                link(nc.vector.tensor_tensor_scan(v(best[:, h]), v(mneg[:]), v(src[:, h]), carry[:, h:h + 1], ALU.add, ALU.max))

                        tmp = tsb(f"scan_tmp_{tag}", [P, T])
                        way(0, mneg_f, whole_f, score, False, T - 1)
                        way(1, mneg_b, whole_b, best, True, 0)
                        nc.vector.tensor_tensor(score[:], score[:], best[:], ALU.subtract).then_inc(diff_ready, 1)

                    @block.tensor
                    def _(pe):
                        for n in range(2):
                            pe.wait_ge(tail_ready, n + 1)
                            nc.tensor.transpose(row_ps[:, 0:P], carry[:], ident[:]).then_inc(row_done, 1)
                            pe.wait_ge(before_ready, n + 1)
                            nc.tensor.transpose(col_ps[:, 0:heads], before[:], ident[0:heads, 0:heads]).then_inc(col_done, 1)

                    @block.scalar
                    def _(act):
                        act.wait_ge(diff_ready, 1)
                        nc.scalar.activation(score[:], score[:], ACT.Exp).then_inc(diff_ready, 1)
                        act.wait_ge(diff_ready, 2)

        gather_sum("l0", table0)

        with ExitStack() as st:
            tsb, tps = fresh(nc, st)
            y = tsb("y0", [P, NB, D])
            tmp = tsb("tmp0", [P, NB, D])
            small = tsb("small0", [P, 4, NB])
            deg = tsb("in_deg", [P, NB])
            root = tsb("in_root", [P, NB])
            scale = tsb("in_scale", [P, NB])
            count_ps = tps("count_ps", [P, 2, BANK])
            total = tsb("total", [P, NB])
            upto = tsb("upto", [P, NB])
            deg_done = sem("in_deg_done")
            deg_ready = sem("in_deg_ready")
            root_ready = sem("in_root_ready")
            counts_ready = sem("counts_ready")
            counts_done = sem("counts_done")
            chain = Count(sem("rowstart_chain"))
            with nc.Block() as block:
                @block.vector
                def _(dve):
                    link = linked(dve, chain)
                    nc.vector.tensor_copy(total[:], agg[:, :, D]).then_inc(counts_ready, 1)
                    nc.vector.tensor_scalar(deg[:], agg[:, :, D], 1.0, None, ALU.max).then_inc(deg_ready, 1)
                    dve.wait_ge(counts_done, 1)
                    link(nc.vector.tensor_copy(total[:], count_ps[:, 1, 0:NB]))
                    link(nc.vector.tensor_tensor_scan(upto[:], ones[:, 0:NB], total[:], 0.0, ALU.mult, ALU.add))
                    link(nc.vector.tensor_tensor(upto[:], upto[:], total[:], ALU.subtract))
                    link(nc.vector.tensor_tensor(upto[:], upto[:], count_ps[:, 0, 0:NB], ALU.add))
                    link(nc.vector.tensor_copy(rowstart[:], upto[:]))
                    dve.wait_ge(root_ready, 1)
                    link(nc.vector.reciprocal(scale[:], root[:]))

                @block.scalar
                def _(act):
                    act.wait_ge(deg_ready, 1)
                    nc.scalar.sqrt(root[:], deg[:]).then_inc(root_ready, 1)

                @block.tensor
                def _(pe):
                    pe.wait_ge(counts_ready, 1)
                    nc.tensor.matmul(count_ps[:, 0, 0:NB], below[:], total[:], start=True, stop=True)
                    nc.tensor.matmul(count_ps[:, 1, 0:NB], ones[:], total[:], start=True, stop=True).then_inc(counts_done, 1)

            def mean_sum(dve, link, h):
                return lambda g: nc.vector.tensor_tensor(
                    h[:], agg[:, bass.ds(g * BPB, BPB), 0:D],
                    scale[:, bass.ds(g * BPB, BPB)].unsqueeze(2).broadcast_to([P, BPB, D]), ALU.mult)

            mlp("l0", w0a, b0a, w0b, b0b, D, ACT.Gelu, y, mean_sum)
            normalise("l0", y, tmp, small)
        recycle()

        with ExitStack() as layer:
            lsb, _ = fresh(nc, layer)
            node1 = lsb("node1", [P, NB, R])
            HALF = R // 2 * W1ROW

            def w1_load(sp, loaded):
                sp.dma_start(fc_s[:], fc.rearrange("r i o -> i r o")).then_inc(loaded, 16)
                sp.dma_start(attn_s[:], attn.rearrange("r k o -> (r k o)").partition_broadcast(D)).then_inc(loaded, 16)

            def w1_compute(dve, link, loaded, tsb, wsum):
                dve.wait_ge(loaded, 32)
                at = attn_s[:].rearrange("p (r k) -> p r k", r=R)
                link(nc.vector.tensor_tensor(prod[:], fc_s[:], at[:, :, 0:D], ALU.mult))
                link(nc.vector.reduce_sum(score_w[:, 0, :], prod[:], AX))
                link(nc.vector.tensor_tensor(prod[:], fc_s[:], at[:, :, D:2 * D], ALU.mult))
                link(nc.vector.reduce_sum(score_w[:, 1, :], prod[:], AX))
                for half in range(2):
                    to = wsum[:, half * (HALF + R):half * (HALF + R) + HALF].rearrange("p (r f) -> p r f", f=W1ROW)
                    rs = slice(half * R // 2, (half + 1) * R // 2)
                    link(nc.vector.tensor_copy(to[:, :, 0:D], fc_s[:, rs, :]))
                    link(nc.vector.tensor_copy(to[:, :, D], score_w[:, 0, rs]))
                return nc.vector.tensor_copy(wsum[:, HALF:HALF + R], score_w[:, 1, :])

            def keep1(z, stage, node, block, b):
                nc.vector.tensor_copy(stage[:, b, 0:HALF], z[:, 0, 0:HALF])
                nc.vector.tensor_copy(node[:, bass.ds(block, 1), :], z[:, 0, HALF:HALF + R].unsqueeze(1))
                return nc.vector.tensor_copy(stage[:, b, HALF:2 * HALF], z[:, 1, 0:HALF])

            with ExitStack() as st:
                tsb, _ = fresh(nc, st)
                fc_s = tsb("fc_s", [D, R, D])
                attn_s = tsb("attn_s", [D, R * 2 * D])
                prod = tsb("prod1", [D, R, D])
                score_w = tsb("score_w", [D, 2, R])
                table1_v = table1.rearrange("(b p r) f -> b p (r f)", p=P, r=R)
                project("l1", None, 2 * HALF + R, ((0, HALF + R), (HALF + R, 2 * HALF + R)), table1, nodes1,
                        dict(buffers=lambda tsb: (tsb("stage1", [P, BPB, 2 * HALF]), node1),
                             ones=lambda link, stage: None,
                             keep=keep1,
                             store=lambda sp, table, stage, block, b: sp.dma_start(
                                 table1_v[bass.ds(block, 1)].rearrange("o p f -> (o p) f"), stage[:, b])),
                        dict(load=w1_load, compute=w1_compute))

            target = lsb("target", [P, 1, T])
            with ExitStack() as st:
                tsb, _ = fresh(nc, st)
                values = tsb("values1", [P, T, R])
                et_i = tsb("et_i", [P, T], I32)
                et_s = tsb("et_s", [P, T])
                pick = tsb("pick", [P, 2, T])
                blank = sem("et_blank")
                loaded = sem("et_loaded")
                chain = Count(sem("pick_chain"))
                spread("l1", R, node1, nodes1, spread1, values)
                with nc.Block() as block:
                    @block.sync
                    def _(sp):
                        full = (P - 1) * T
                        sp.wait_ge(blank, 1)
                        sp.dma_start(et_i[0:P - 1, :], etype[0:full].rearrange("(p j) -> p j", j=T)).then_inc(loaded, 16)
                        sp.dma_start(et_i[P - 1:P, 0:E - full], etype[full:E].unsqueeze(0)).then_inc(loaded, 16)

                    @block.vector
                    def _(dve):
                        link = linked(dve, chain)
                        nc.vector.memset(et_i[:], 0).then_inc(blank, 1)
                        dve.wait_ge(loaded, 32)
                        link(nc.vector.tensor_copy(et_s[:], et_i[:]))
                        link(nc.vector.scalar_tensor_tensor(target[:, 0], et_s[:], 0.0, values[:, :, 0], ALU.is_equal, ALU.mult))
                        for r in range(1, R):
                            link(nc.vector.scalar_tensor_tensor(pick[:, r % 2], et_s[:], float(r), values[:, :, r], ALU.is_equal, ALU.mult))
                            link(nc.vector.tensor_tensor(target[:, 0], target[:, 0], pick[:, r % 2], ALU.add))

            score_tl = lsb("score_tl1", [P, 1, TP])
            gather_spill("g1", table1, idx1_tl, W1ROW, W1ROW + 1, spill1, score_tl, D, 1)
            score = lsb("score1", [P, 1, T])
            best = lsb("best1", [P, 1, T])
            tiles_to_scan("l1", 1, score_tl, score)
            chain = Count(sem("logit_chain_l1"))
            with nc.Block() as block:
                @block.vector
                def _(dve):
                    link = linked(dve, chain)
                    link(nc.vector.tensor_tensor(score[:], score[:], target[:], ALU.add))
                    link(nc.vector.tensor_scalar(score[:], score[:], 0.0, None, ALU.max))
            run_softmax("l1", 1, score, best)
            scan_to_tiles("l1b", 1, score, score_tl)
            spill_sum("s1", spill1, W1ROW + 1, 1, score_tl)

        def attention_mean(tag, y, count, at, heads, width):
            chain = Count(sem(f"mean_chain_{tag}"))
            with nc.Block() as block:
                @block.vector
                def _(dve):
                    link = linked(dve, chain)
                    link(nc.vector.tensor_scalar(count, at(agg), 1.0e-30, None, ALU.max))
                    link(nc.vector.reciprocal(count, count))
                    a4 = agg[:, :, 0:heads * width].rearrange("p b (h d) -> p b h d", h=heads)[:, :, :, 0:D // heads]
                    for h in range(heads):
                        link(nc.vector.tensor_tensor(y[:, :, h * (D // heads):(h + 1) * (D // heads)], a4[:, :, h],
                                                     along(count[:, h], D // heads), ALU.mult))
                    link(nc.vector.tensor_tensor(y[:], y[:], xcur[:], ALU.add))

        with ExitStack() as st:
            tsb, _ = fresh(nc, st)
            y = tsb("y1", [P, NB, D])
            tmp = tsb("tmp1", [P, NB, D])
            small = tsb("small1", [P, 4, NB])
            count = tsb("count1", [P, 1, NB])
            attention_mean("l1", y, count[:], lambda a: a[:, :, D + 1].unsqueeze(1), 1, W1ROW + 1)
            normalise("l1", y, tmp, small,
                      lambda sp, done: (sp.dma_start(node_rows(table2), xcur[:]).then_inc(done, 16), 16)[1])
        recycle()

        gather_sum("l2", table2)
        with ExitStack() as st:
            tsb, tps = fresh(nc, st)
            y = tsb("y2", [P, NB, D])
            tmp = tsb("tmp2", [P, NB, D])
            small = tsb("small2", [P, 4, NB])
            eps_s = tsb("eps_s", [P, 1])
            eps_in = sem("eps_in")
            eps_done = Count(sem("eps_done"))
            with nc.Block() as block:
                @block.sync
                def _(sp):
                    sp.dma_start(eps_s[:], eps2.partition_broadcast(P)).then_inc(eps_in, 16)

                @block.vector
                def _(dve):
                    dve.wait_ge(eps_in, 16)
                    linked(dve, eps_done)(nc.vector.tensor_scalar(eps_s[:], eps_s[:], 1.0, None, ALU.add))

            def own_and_sum(dve, link, h):
                return lambda g: nc.vector.scalar_tensor_tensor(
                    h[:], xcur[:, bass.ds(g * BPB, BPB), :], eps_s[:, 0:1], agg[:, bass.ds(g * BPB, BPB), 0:D], ALU.mult, ALU.add)

            mlp("l2", w2a, b2a, w2b, b2b, w2a.shape[1], ACT.Relu, y, own_and_sum)
            normalise("l2", y, tmp, small)
        recycle()

        with ExitStack() as layer:
            lsb, _ = fresh(nc, layer)
            node3 = lsb("node3", [P, NB, H])
            ve = lsb("ve", [P, 2 * H])
            KEY = H * (HD + 1)

            def w3_load(sp, loaded):
                sp.dma_start(wn_s[:], wn).then_inc(loaded, 16)
                for n, a in enumerate((ak, aq, ae)):
                    sp.dma_start(att_s[:, n], a.rearrange("h d -> (h d)").partition_broadcast(P)).then_inc(loaded, 16)
                for half in range(2):
                    sp.dma_start(we_s[half * D:(half + 1) * D, :], we).then_inc(loaded, 16)

            def w3_compute(dve, link, loaded, tsb, wsum):
                dve.wait_ge(loaded, 16 * 6)
                link(nc.vector.memset(wsum[:], 0.0))
                link(nc.vector.tensor_copy(wsum[:, 0:KEY].rearrange("p (h d) -> p h d", h=H)[:, :, 0:HD], wn_s[:].rearrange("p (h d) -> p h d", h=H)))
                link(nc.vector.memset(ve[:], 0.0))
                link(nc.vector.tensor_tensor(prod3[:], we_s[:], att_s[:, 2], ALU.mult))
                for half in range(2):
                    rs = slice(half * D, (half + 1) * D)
                    link(nc.vector.reduce_sum(ve[rs, half * H:(half + 1) * H], prod3[rs].rearrange("p (h d) -> p h d", h=H), AX))
                for n in range(2):
                    link(nc.vector.tensor_tensor(prod3[0:D], wn_s[:], att_s[0:D, n], ALU.mult))
                    last = nc.vector.reduce_sum(wsum[:, KEY + n * H:KEY + (n + 1) * H], prod3[0:D].rearrange("p (h d) -> p h d", h=H), AX)
                    if n == 0:
                        link(last)
                return last

            def keep3(z, stage, node, block, b):
                nc.vector.tensor_copy(stage[:, b, 0:KEY].rearrange("p (h d) -> p h d", h=H)[:, :, 0:HD],
                                      z[:, 0, 0:KEY].rearrange("p (h d) -> p h d", h=H)[:, :, 0:HD])
                nc.vector.tensor_copy(node[:, bass.ds(block, 1), :], z[:, 0, KEY + H:KEY + 2 * H].unsqueeze(1))
                return nc.vector.tensor_copy(stage[:, b, KEY:KEY + H], z[:, 0, KEY:KEY + H])

            with ExitStack() as st:
                tsb, _ = fresh(nc, st)
                wn_s = tsb("wn_s", [D, D])
                we_s = tsb("we_s", [P, D])
                att_s = tsb("att_s", [P, 3, D])
                prod3 = tsb("prod3", [P, D])
                table3_v = table3.rearrange("(b p) f -> b p f", p=P)
                project("l3", None, KEY + 2 * H, ((0, KEY + 2 * H),), table3, nodes3,
                        dict(buffers=lambda tsb: (tsb("stage3", [P, BPB, W3ROW]), node3),
                             ones=lambda link, stage: link(nc.vector.memset(stage[:], 1.0)),
                             keep=keep3,
                             store=lambda sp, table, stage, block, b: sp.dma_start(
                                 table3_v[bass.ds(block, 1)].rearrange("o p f -> (o p) f"), stage[:, b])),
                        dict(load=w3_load, compute=w3_compute))

            EC = 26
            NE = T // EC
            with ExitStack() as st:
                tsb, tps = fresh(nc, st)
                feat = tsb("feat", [P, 2, EC * D])
                feat_t = tsb("feat_t", [P, 2, 4 * P])
                part = tsb("part", [P, 2, EC * H])
                ft_ps = tps("ft_ps", [P, 2, BANK])
                we_ps = tps("we_ps", [P, 2, BANK])
                blank = sem("feat_blank")
                feat_in = [sem(f"feat_in{n}") for n in range(2)]
                ft_done = sem("ft_done")
                ft_kept = sem("ft_kept")
                we_done = sem("we_done")
                we_kept = sem("we_kept")
                part_out = [sem(f"part_out{n}") for n in range(2)]
                PAIRS = EC // 2
                QUADS = -(-PAIRS // 4)
                full = (E - (P - 1) * T) // EC
                attr = edge_attr[0:(P - 1) * T, :].rearrange("(p c j) f -> c p (j f)", p=P - 1, j=EC)
                last_attr = edge_attr[(P - 1) * T:(P - 1) * T + full * EC, :].rearrange("(c o j) f -> c o (j f)", o=1, j=EC)
                rest = E - (P - 1) * T - full * EC

                with nc.Block() as block:
                    @block.sync
                    def _(sp):
                        for c in range(NE):
                            s = c % 2
                            if c >= 2:
                                sp.wait_ge(ft_done, QUADS * (c - 1))
                            sp.dma_start(feat[0:P - 1, s], attr[c]).then_inc(feat_in[s], 16)
                            if c < full:
                                sp.dma_start(feat[P - 1:P, s], last_attr[c]).then_inc(feat_in[s], 16)
                            elif c == full:
                                sp.dma_start(feat[P - 1:P, s, 0:rest * D], edge_attr[E - rest:E, :].rearrange("(o j) f -> o (j f)", o=1)).then_inc(feat_in[s], 16)
                            else:
                                sp.dma_start(feat[P - 1:P, s, 0:D], edge_attr[E - 1:E, :]).then_inc(feat_in[s], 16)

                    @block.tensor
                    def _(pe):
                        quad = 0
                        for c in range(NE):
                            s = c % 2
                            pe.wait_ge(feat_in[s], 32 * (c // 2 + 1))
                            for qd in range(QUADS):
                                ps_ = range(4 * qd, min(4 * qd + 4, PAIRS))
                                if quad >= 2:
                                    pe.wait_ge(ft_kept, quad - 1)
                                for n, pr in enumerate(ps_):
                                    last = nc.tensor.transpose(ft_ps[:, quad % 2, n * P:(n + 1) * P], feat[:, s, 2 * pr * D:2 * (pr + 1) * D], ident[:])
                                last.then_inc(ft_done, 1)
                                if qd == 0 and c >= 2:
                                    pe.wait_ge(we_kept, c - 1)
                                pe.wait_ge(ft_kept, quad + 1)
                                for n, pr in enumerate(ps_):
                                    last = nc.tensor.matmul(we_ps[:, s, 2 * pr * H:2 * (pr + 1) * H], feat_t[:, quad % 2, n * P:(n + 1) * P], ve[:], start=True, stop=True)
                                quad += 1
                            last.then_inc(we_done, 1)

                    @block.scalar
                    def _(act):
                        quad = 0
                        for c in range(NE):
                            for qd in range(QUADS):
                                k = (min(4 * qd + 4, PAIRS) - 4 * qd) * P
                                act.wait_ge(ft_done, quad + 1)
                                nc.scalar.copy(feat_t[:, quad % 2, 0:k], ft_ps[:, quad % 2, 0:k]).then_inc(ft_kept, 1)
                                quad += 1

                    @block.vector
                    def _(dve):
                        for c in range(NE):
                            s = c % 2
                            dve.wait_ge(we_done, c + 1)
                            if c >= 2:
                                dve.wait_ge(part_out[s], 16 * (c // 2))
                            nc.vector.tensor_copy(part[:, s], we_ps[:, s, 0:EC * H]).then_inc(we_kept, 1)

                    @block.gpsimd
                    def _(pool):
                        for c in range(NE):
                            s = c % 2
                            pool.wait_ge(we_kept, c + 1)
                            pool.dma_start(we_d[:, c * EC * H:(c + 1) * EC * H], part[:, s]).then_inc(part_out[s], 16)
                        for s in range(2):
                            pool.wait_ge(part_out[s], 16 * (NE // 2))

            target = lsb("target3", [P, H, T])
            with ExitStack() as st:
                tsb, _ = fresh(nc, st)
                values = tsb("values3", [P, T, H])
                edge_s = tsb("edge_s", [P, T, H])
                loaded = sem("we_loaded")
                done = sem("target_done")
                spread("l3", H, node3, nodes3, spread3, values)
                with nc.Block() as block:
                    @block.sync
                    def _(sp):
                        sp.dma_start(edge_s[:].rearrange("p j h -> p (j h)"), we_d).then_inc(loaded, 16)

                    @block.vector
                    def _(dve):
                        dve.wait_ge(loaded, 16)
                        nc.vector.tensor_tensor(target[:].rearrange("p h j -> p j h"), values[:], edge_s[:], ALU.add).then_inc(done, 1)
                        dve.wait_ge(done, 1)

            score_tl = lsb("score_tl3", [P, H, TP])
            gather_spill("g3", table3, src_tl, W3ROW, W3ROW, spill3, score_tl, KEY, H)
            score = lsb("score3", [P, H, T])
            tiles_to_scan("l3", H, score_tl, score)
            chain = Count(sem("logit_chain_l3"))
            with nc.Block() as block:
                @block.vector
                def _(dve):
                    link = linked(dve, chain)
                    link(nc.vector.tensor_tensor(score[:], score[:], target[:], ALU.add))
                    link(nc.vector.scalar_tensor_tensor(score[:], score[:], 0.01, score[:], ALU.mult, ALU.max))
            run_softmax("l3", H, score, target)
            scan_to_tiles("l3b", H, score, score_tl)
            spill_sum("s3", spill3, W3ROW, H, score_tl)

        with ExitStack() as st:
            tsb, _ = fresh(nc, st)
            y = tsb("y3", [P, NB, D])
            tmp = tsb("tmp3", [P, NB, D])
            small = tsb("small3", [P, 4, NB])
            count = tsb("count3", [P, H, NB])
            bias_s = tsb("bias_s", [P, D])
            bias_in = sem("bias_in")
            chain = Count(sem("bias_chain"))
            attention_mean("l3", y, count[:], lambda a: a[:, :, 0:KEY].rearrange("p b (h d) -> p h b d", h=H)[:, :, :, HD], H, HD + 1)
            with nc.Block() as block:
                @block.sync
                def _(sp):
                    sp.dma_start(bias_s[:], bias3.partition_broadcast(P)).then_inc(bias_in, 16)

                @block.vector
                def _(dve):
                    link = linked(dve, chain)
                    link(nc.vector.tensor_tensor(y[:], y[:], xcur[:], ALU.add))
                    dve.wait_ge(bias_in, 16)
                    link(nc.vector.tensor_tensor(y[:], y[:], bias_s[:].unsqueeze(1).broadcast_to([P, NB, D]), ALU.add))

            def store(sp, done):
                sp.dma_start(out[0:(NB - 1) * P, :].rearrange("(b p) f -> p b f", p=P), xcur[:, 0:NB - 1, :]).then_inc(done, 16)
                sp.dma_start(out[(NB - 1) * P:N, :], xcur[0:NLAST, NB - 1, :]).then_inc(done, 16)
                return 32

            normalise("l3", y, tmp, small, store)


_INS = ["x", "src", "dst", "edge_attr_64", "edge_type_8", "L0_gnn_w1", "L0_gnn_b1", "L0_gnn_w2", "L0_gnn_b2",
        "L1_gnn_fc_weight", "L1_gnn_attn_weight", "L2_gnn_eps", "L2_gnn_W1", "L2_gnn_b1", "L2_gnn_W2", "L2_gnn_b2",
        "L3_gnn_W_node", "L3_gnn_W_edge", "L3_gnn_attn_query", "L3_gnn_attn_key", "L3_gnn_attn_edge", "L3_gnn_bias"]


def kernel(**inputs):
    import numpy as np
    import concourse.bacc as bacc
    from concourse.bass_utils import run_bass_kernel_spmd

    nc = bacc.Bacc("TRN2", target_bir_lowering=False, num_devices=1)
    arrays, args = {}, []
    for name in _INS:
        a = np.ascontiguousarray(inputs[name])
        arrays[name] = a
        args.append(nc.dram_tensor(name, a.shape, mybir.dt.from_np(a.dtype), kind="ExternalInput").ap())
    args.append(nc.dram_tensor("out", (N, D), F32, kind="ExternalOutput").ap())
    build(nc, *args)
    return run_bass_kernel_spmd(nc, [arrays], core_ids=[0]).results[0]["out"]
```

```python
from contextlib import ExitStack
import itertools

import concourse.bass as bass
from concourse import mybir

F32 = mybir.dt.float32
BF16 = mybir.dt.bfloat16
I32 = mybir.dt.int32
ALU = mybir.AluOpType
ACT = mybir.ActivationFunctionType
AX = mybir.AxisListType.X
PE_ONLY = (mybir.EngineType.PE,)

P = 128
N = 6250
NB = -(-N // P)
NLAST = N - (NB - 1) * P
E = 206250
T = -(-E // P)
EP = T * P
G = -(-(T + NB - 1) // P)
V = G * P
VP = V * P
CH = 16
SLOTS = 4
BODY = CH * SLOTS
ITERS = V // BODY
RING = 4
D = 64
R = 8
H = 4
HD = D // H
AW = 68
BANK = 512
BPB = BANK // AW
NG = NB // BPB
W1ROW = D + 1
W3ROW = H * (HD + 1) + H
EPS = 1e-5
LOW = -3.0e38
assert V == BODY * ITERS and NB == BPB * NG


class Count:

    def __init__(self, sem):
        self.sem, self.n = sem, 0

    def on(self, ins, k=1):
        ins.then_inc(self.sem, k)
        self.n += k
        return self.n


def fresh(nc, ctx):
    def sb(name, shape, dt=F32):
        return ctx.enter_context(nc.sbuf_tensor(name, shape, dt))

    def ps(name, shape, dt=F32):
        return ctx.enter_context(nc.psum_tensor(name, shape, dt))

    return sb, ps


def linked(engine, count):

    def link(ins):
        engine.wait_ge(count.sem, count.on(ins))

    return link


def along(ap, n):
    return ap.unsqueeze(2).broadcast_to([ap.shape[0], ap.shape[1], n])


def node_rows(table):
    return table.rearrange("(b p) f -> p b f", p=P)


def build(nc, x, src, dst, edge_attr, etype, w0a, b0a, w0b, b0b, fc, attn, eps2, w2a, b2a, w2b, b2b,
          wn, we, aq, ak, ae, bias3, out):
    with ExitStack() as whole:
        sb, _ = fresh(nc, whole)

        live = []

        def sem(name):
            live.append(nc.alloc_semaphore(name=name))
            return live[-1]

        def recycle():
            nc.all_engine_barrier()
            nc.clear_and_free_semaphores(live)
            nc.all_engine_barrier()
            live.clear()

        def dram(name, shape, dt=F32):
            return nc.dram_tensor(name, shape, dt, kind="Internal").ap()

        ident = sb("ident", [P, P])
        ones = sb("ones", [P, P])
        below = sb("below", [P, P])
        iota = sb("iota", [P, P])
        own = sb("own", [P, 1])
        zeros16 = sb("zeros16", [P, BANK], BF16)
        tile_of = sb("tile_of", [P, G], I32)
        src_tl = sb("src_tl", [P, V], I32)
        idx1_tl = sb("idx1_tl", [P, V], I32)
        rel_tl = sb("rel_tl", [P, V])
        offs = sb("offs", [1, V], I32)
        mneg_f = sb("mneg_f", [P, G, P], BF16)
        mneg_b = sb("mneg_b", [P, G, P], BF16)
        goes_f = sb("goes_f", [H, G, P], BF16)
        goes_b = sb("goes_b", [H, G, P], BF16)
        cont = sb("cont", [P, G])
        rel_first = sb("rel_first", [P, G])
        inside = sb("inside", [P, V], BF16)
        first_dst = sb("first_dst", [P, 1], I32)
        runstart = sb("runstart", [P, NB], I32)
        xcur = sb("xcur", [P, NB, D])
        agg = sb("agg", [P, NB, AW])

        table0 = dram("table0", (NB * P, D))
        table1 = dram("table1", (NB * P * R, W1ROW))
        table2 = dram("table2", (NB * P, D))
        table3 = dram("table3", (NB * P, W3ROW))
        edges_d = dram("edges_d", (T, 3 * P), I32)
        visit_d = dram("visit_d", (V,))
        offs_d = dram("offs_d", (V,), I32)
        key_d = dram("key_d", (VP + 2,))
        et_d = dram("et_d", (VP,))
        spread1 = dram("spread1", (VP + 1, R))
        spread3 = dram("spread3", (VP + 1, H))
        nodes1 = dram("nodes1", (NB * P, R))
        nodes3 = dram("nodes3", (NB * P, H))
        target_d = dram("target_d", (H, VP))
        we_d = dram("we_d", (P, T * H))

        def rows_of(flat):
            full = (G - 1) * P
            rest = E // P - full
            a = flat[0:full * P].rearrange("(g q c) -> q g c", q=P, c=P)
            b = flat[full * P:(full + rest) * P].rearrange("(q c) -> q c", c=P)
            return a, b, rest

        with ExitStack() as st:
            tsb, tps = fresh(nc, st)
            dst_r = tsb("dst_r", [P, G, P], I32)
            dst_t = tsb("dst_t", [P, G, P])
            pad = tsb("pad", [1, 3 * P], I32)
            edges_r = tsb("edges_r", [P, G, 3 * P], I32)
            src_f = tsb("src_f", [P, G, P])
            dst_f = tsb("dst_f", [P, G, P])
            et_f = tsb("et_f", [P, G, P])
            rel_f = tsb("rel_f", [P, G, P])
            valid = tsb("valid", [P, G, P])
            key = tsb("key", [P, G, P])
            prev = tsb("prev", [P, G, P])
            after = tsb("after", [P, G, P])
            key_s = tsb("key_s", [P, V])
            prev_s = tsb("prev_s", [P, V])
            base_f = tsb("base_f", [P, G])
            base_i = tsb("base_i", [P, G], I32)
            number_i = tsb("number_i", [P, G], I32)
            number = tsb("number", [P, G])
            at_b = tsb("at_b", [P, V])
            begun = tsb("begun", [P, 2, V], BF16)
            tile_f = tsb("tile_f", [P, G])
            block_f = tsb("block_f", [P, G])
            first_node = tsb("first_node", [P, G])
            blk = tsb("blk", [P, G])
            q = tsb("q", [P, G])
            off_f = tsb("off_f", [P, G])
            off_i = tsb("off_i", [P, G], I32)
            ends = tsb("ends", [1, 2])
            flag = tsb("flag", [P, 3, G])
            flag4 = tsb("flag4", [P, 2, G, H])
            zero = tsb("zero", [P, V])
            iota_i = tsb("iota_i", [P, P], I32)
            own_i = tsb("own_i", [P, 1], I32)
            turned = tps("turned", [P, 2, 4 * BANK])

            blank = sem("blank")
            loaded = sem("loaded")
            tiles_in = sem("tiles_in")
            edges_out = sem("edges_out")
            x_in = sem("x_in")
            consts = sem("consts")
            iota_ready = sem("iota_ready")
            zero_ready = sem("zero_ready")
            zeroed = sem("zeroed")
            chain = Count(sem("setup_chain"))
            at_ready = sem("at_ready")
            at_out = sem("at_out")
            at_in = sem("at_in")
            tile_ready = sem("tile_ready")
            edges_in = sem("edges_in")
            key_ready = sem("key_ready")
            key_out = sem("key_out")
            keys_in = sem("keys_in")
            rows_ready = sem("rows_ready")
            turn_done = sem("turn_done")
            turn_used = sem("turn_used")
            off_ready = sem("off_ready")
            off_out = sem("off_out")
            off_in = sem("off_in")
            et_out = sem("et_out")
            flags_ready = sem("flags_ready")
            flags_turned = sem("flags_turned")
            FULL = E // P
            REST = E % P

            with nc.Block() as block:
                @block.gpsimd
                def _(pool):
                    nc.gpsimd.memset(pad[:, 0:2 * P], N).then_inc(blank, 1)
                    nc.gpsimd.memset(pad[:, 2 * P:3 * P], 0).then_inc(blank, 1)
                    nc.gpsimd.memset(dst_r[:], N).then_inc(blank, 1)
                    nc.gpsimd.memset(xcur[:], 0.0).then_inc(blank, 1)
                    nc.gpsimd.iota(iota_i[:], [[1, P]], base=0, channel_multiplier=0).then_inc(iota_ready, 1)
                    nc.gpsimd.iota(own_i[:], [[0, 1]], base=0, channel_multiplier=1).then_inc(iota_ready, 1)
                    nc.gpsimd.iota(number_i[:], [[P, G]], base=0, channel_multiplier=1).then_inc(iota_ready, 1)
                    nc.gpsimd.memset(ident[:], 0.0).then_inc(consts, 1)
                    nc.gpsimd.memset(ones[:], 1.0).then_inc(consts, 1)
                    nc.gpsimd.memset(below[:], 1.0).then_inc(consts, 1)
                    pool.wait_ge(consts, 3)
                    nc.gpsimd.affine_select(out=ident[:], in_=ident[:], compare_op=ALU.not_equal, fill=1.0,
                                            base=0, pattern=[[-1, P]], channel_multiplier=1).then_inc(consts, 1)
                    nc.gpsimd.affine_select(out=below[:], in_=below[:], compare_op=ALU.is_gt, fill=0.0,
                                            base=0, pattern=[[1, P]], channel_multiplier=-1).then_inc(consts, 1)
                    pool.wait_ge(edges_out, 16 * 9)
                    pool.wait_ge(tile_ready, 1)
                    for g in range(G):
                        pool.indirect_dma_start(edges_r[:, g], None, edges_d, bass.IndirectOffsetOnAxis(tile_of[:, g:g + 1], 0)).then_inc(edges_in, 16)

                @block.sync
                def _(sp):
                    sp.wait_ge(blank, 4)
                    a, b, rest = rows_of(dst)
                    sp.dma_start(dst_r[:, 0:a.shape[1], :], a).then_inc(loaded, 16)
                    sp.dma_start(dst_r[0:rest, a.shape[1], :], b).then_inc(loaded, 16)
                    sp.dma_start(dst_r[rest:rest + 1, a.shape[1], 0:REST], dst[E - REST:E].unsqueeze(0)).then_inc(loaded, 16)
                    for n, flat in enumerate((src, dst, etype)):
                        sp.dma_start(edges_d[0:FULL, n * P:(n + 1) * P], flat[0:FULL * P].rearrange("(t c) -> t c", c=P)).then_inc(edges_out, 16)
                        sp.dma_start(edges_d[FULL:T, n * P:n * P + REST], flat[FULL * P:E].unsqueeze(0)).then_inc(edges_out, 16)
                        sp.dma_start(edges_d[FULL:T, n * P + REST:(n + 1) * P], pad[:, n * P + REST:(n + 1) * P]).then_inc(edges_out, 16)
                    sp.dma_start(xcur[:, 0:NB - 1, :], x[0:(NB - 1) * P, :].rearrange("(b p) f -> p b f", p=P)).then_inc(x_in, 16)
                    sp.dma_start(xcur[0:NLAST, NB - 1, :], x[(NB - 1) * P:N, :]).then_inc(x_in, 16)
                    sp.wait_ge(at_ready, 1)
                    sp.dma_start(visit_d.rearrange("(q g) -> q g", q=P), base_f[:]).then_inc(at_out, 16)
                    sp.wait_ge(at_out, 16)
                    sp.dma_start(at_b[:], visit_d.partition_broadcast(P)).then_inc(at_in, 16)
                    sp.wait_ge(zero_ready, 2)
                    spread1_v = spread1[0:VP, :].rearrange("(p j) r -> p (j r)", p=P)
                    for lo in range(0, V * R, V):
                        hi = lo + V
                        sp.dma_start(spread1_v[:, lo:hi], zero[:, 0:hi - lo]).then_inc(zeroed, 16)
                    spread3_v = spread3[0:VP, :].rearrange("(p j) r -> p (j r)", p=P)
                    for lo in range(0, V * H, V):
                        hi = lo + V
                        sp.dma_start(spread3_v[:, lo:hi], zero[:, 0:hi - lo]).then_inc(zeroed, 16)
                    sp.wait_ge(key_ready, 1)
                    sp.dma_start(key_d[1:VP + 1].rearrange("(g q c) -> q g c", q=P, c=P), key[:]).then_inc(key_out, 16)
                    sp.dma_start(key_d[0:1].unsqueeze(0), ends[:, 0:1]).then_inc(key_out, 16)
                    sp.dma_start(key_d[VP + 1:VP + 2].unsqueeze(0), ends[:, 1:2]).then_inc(key_out, 16)
                    sp.wait_ge(key_out, 48)
                    sp.dma_start(prev[:], key_d[0:VP].rearrange("(g q c) -> q g c", q=P, c=P)).then_inc(keys_in, 16)
                    sp.dma_start(after[:], key_d[2:VP + 2].rearrange("(g q c) -> q g c", q=P, c=P)).then_inc(keys_in, 16)
                    sp.dma_start(key_s[:], key_d[1:VP + 1].rearrange("(p j) -> p j", p=P)).then_inc(keys_in, 16)
                    sp.dma_start(prev_s[:], key_d[0:VP].rearrange("(p j) -> p j", p=P)).then_inc(keys_in, 16)
                    sp.dma_start(et_d.rearrange("(g q c) -> q g c", q=P, c=P), et_f[:]).then_inc(et_out, 16)
                    sp.wait_ge(off_ready, 1)
                    sp.dma_start(offs_d.rearrange("(g q) -> q g", q=P), off_i[:], allow_slow_non_contiguous=True).then_inc(off_out, 16)
                    sp.wait_ge(off_out, 16)
                    sp.dma_start(offs[:], offs_d.unsqueeze(0)).then_inc(off_in, 16)
                    sp.wait_ge(off_in, 16)
                    sp.wait_ge(et_out, 16)
                    sp.wait_ge(zeroed, 16 * (R + H))
                    sp.wait_ge(x_in, 32)

                @block.vector
                def _(dve):
                    link = linked(dve, chain)
                    nc.vector.memset(zero[:], 0.0).then_inc(zero_ready, 1)
                    nc.vector.memset(zeros16[:], 0.0).then_inc(zero_ready, 1)
                    link(nc.vector.memset(ends[:], -2.0))
                    dve.wait_ge(iota_ready, 3)
                    link(nc.vector.tensor_copy(iota[:], iota_i[:]))
                    link(nc.vector.tensor_copy(own[:], own_i[:]))
                    link(nc.vector.tensor_copy(number[:], number_i[:]))
                    dve.wait_ge(loaded, 48)
                    link(nc.vector.tensor_copy(dst_t[:], dst_r[:]))
                    link(nc.vector.tensor_reduce(base_f[:], dst_t[:], AX, ALU.min))
                    link(nc.vector.tensor_copy(base_i[:], base_f[:]))
                    link(nc.vector.tensor_scalar(base_i[:], base_i[:], 7, None, ALU.arith_shift_right))
                    link(nc.vector.tensor_copy(base_f[:], base_i[:]))
                    nc.vector.tensor_tensor(base_f[:], base_f[:], number[:], ALU.add).then_inc(at_ready, 1)
                    dve.wait_ge(at_in, 16)
                    for g in range(G):
                        link(nc.vector.tensor_scalar(begun[:, g % 2], at_b[:], number[:, g:g + 1], None, ALU.is_le))
                        link(nc.vector.reduce_sum(tile_f[:, g:g + 1], begun[:, g % 2], AX))
                    link(nc.vector.tensor_scalar(tile_f[:], tile_f[:], -1.0, 0.0, ALU.add, ALU.max))
                    link(nc.vector.tensor_scalar(tile_f[:], tile_f[:], float(T - 1), None, ALU.min))
                    nc.vector.tensor_copy(tile_of[:], tile_f[:]).then_inc(tile_ready, 1)
                    link(nc.vector.tensor_tensor(block_f[:], number[:], tile_f[:], ALU.subtract))
                    link(nc.vector.tensor_scalar(first_node[:], block_f[:], float(P), None, ALU.mult))
                    link(nc.vector.tensor_scalar(blk[:], block_f[:], float(NB - 1), None, ALU.min))
                    link(nc.vector.tensor_scalar(off_f[:], blk[:], float(AW), None, ALU.mult))
                    for k in range(1, NG):
                        link(nc.vector.tensor_scalar(q[:], blk[:], float(BPB * k), float(BANK - BPB * AW), ALU.is_ge, ALU.mult))
                        link(nc.vector.tensor_tensor(off_f[:], off_f[:], q[:], ALU.add))
                    nc.vector.tensor_copy(off_i[:], off_f[:]).then_inc(off_ready, 1)
                    dve.wait_ge(edges_in, 16 * G)
                    link(nc.vector.tensor_copy(dst_f[:], edges_r[:, :, P:2 * P]))
                    link(nc.vector.tensor_copy(src_f[:], edges_r[:, :, 0:P]))
                    link(nc.vector.tensor_copy(et_f[:], edges_r[:, :, 2 * P:3 * P]))
                    link(nc.vector.tensor_tensor(rel_f[:], dst_f[:], along(first_node[:], P), ALU.subtract))
                    link(nc.vector.tensor_copy(rel_first[:], rel_f[:, :, 0]))
                    link(nc.vector.tensor_scalar(valid[:], rel_f[:], 0.0, None, ALU.is_ge))
                    link(nc.vector.scalar_tensor_tensor(valid[:], rel_f[:], float(P), valid[:], ALU.is_lt, ALU.mult))
                    link(nc.vector.scalar_tensor_tensor(key[:], dst_f[:], 1.0, valid[:], ALU.add, ALU.mult))
                    nc.vector.tensor_scalar(key[:], key[:], -1.0, None, ALU.add).then_inc(key_ready, 1)
                    link(nc.vector.scalar_tensor_tensor(src_f[:], src_f[:], float(-N), valid[:], ALU.add, ALU.mult))
                    link(nc.vector.tensor_scalar(src_f[:], src_f[:], float(N), None, ALU.add))
                    nc.vector.scalar_tensor_tensor(dst_t[:], src_f[:], float(R), et_f[:], ALU.mult, ALU.add).then_inc(rows_ready, 1)
                    for n, tl in enumerate((src_tl, idx1_tl, rel_tl)):
                        dve.wait_ge(turn_done, n + 1)
                        nc.vector.tensor_copy(tl[:], turned[:, n % 2, 0:V]).then_inc(turn_used, 1)
                    dve.wait_ge(keys_in, 64)
                    link(nc.vector.tensor_tensor(inside[:], key_s[:], prev_s[:], ALU.is_equal))
                    link(nc.vector.tensor_scalar(first_dst[:], key_s[:, 0:1], 0.0, None, ALU.max))
                    for n, (other, mneg, edge) in enumerate(((prev, mneg_f[:], 0), (after, mneg_b[:, :, ::-1], P - 1))):
                        link(nc.vector.tensor_tensor(other[:], key[:], other[:], ALU.is_equal))
                        link(nc.vector.tensor_copy(flag[:, n], other[:, :, edge]))
                        link(nc.vector.tensor_scalar(mneg, other[:], 1.0, -LOW, ALU.subtract, ALU.mult))
                    link(nc.vector.tensor_copy(cont[:], flag[:, 0]))
                    link(nc.vector.tensor_tensor(flag[:, 2], key[:, :, 0], key[:, :, P - 1], ALU.is_equal))
                    for n in range(2):
                        link(nc.vector.tensor_tensor(flag[:, n], flag[:, n], flag[:, 2], ALU.mult))
                        link(nc.vector.tensor_scalar(flag[:, n], flag[:, n], 1.0, -LOW, ALU.subtract, ALU.mult))
                        nc.vector.tensor_copy(flag4[:, n], along(flag[:, n], H)).then_inc(flags_ready, 1)
                    for n, goes in enumerate((goes_f[:], goes_b[:, :, ::-1])):
                        dve.wait_ge(flags_turned, n + 1)
                        link(nc.vector.tensor_copy(goes, turned[0:H, n, 0:V].rearrange("h (g c) -> h g c", c=P)))

                @block.tensor
                def _(pe):
                    pe.wait_ge(consts, 5)
                    pe.wait_ge(rows_ready, 1)
                    for n, rows in enumerate((src_f, dst_t, rel_f)):
                        if n >= 2:
                            pe.wait_ge(turn_used, n - 1)
                        for g in range(G):
                            last = nc.tensor.transpose(turned[:, n % 2, g * P:(g + 1) * P], rows[:, g, :], ident[:])
                        last.then_inc(turn_done, 1)
                    pe.wait_ge(flags_ready, 2)
                    pe.wait_ge(turn_used, 3)
                    for n in range(2):
                        for g in range(G):
                            last = nc.tensor.transpose(turned[0:H, n, g * P:(g + 1) * P], flag4[:, n, g], ident[:])
                        last.then_inc(flags_turned, 1)



        serial = itertools.count()

        def held(engine, value):
            if isinstance(value, int):
                return value
            register = engine.alloc_register(f"held_{next(serial)}")
            engine.reg_mov(register, value)
            return engine.snap(register)

        def steps(engine, body):
            body(0, True)
            with engine.Fori(1, ITERS) as i:
                body(i, False)

        with ExitStack() as st:
            tsb, tps = fresh(nc, st)
            part_i = tsb("part_i", [P, V], I32)
            lo_f = tsb("lo_f", [P, V])
            hi_f = tsb("hi_f", [P, V])
            lo_hot = tsb("lo_hot", [P, SLOTS, CH, P], BF16)
            hi_hot = tsb("hi_hot", [P, SLOTS, CH, NB], BF16)
            deg = tsb("deg", [P, NB])
            root = tsb("root", [P, NB])
            xs = tsb("xs", [P, NB, D])
            deg_ps = tps("deg_ps", [P, NB])
            chain = Count(sem("deg_chain"))
            hot_ready = sem("hot_ready")
            counted = sem("counted")
            deg_ready = sem("deg_ready")
            root_ready = sem("root_ready")
            xs_ready = sem("xs_ready")
            xs_out = sem("xs_out")
            with nc.Block() as block:
                @block.vector
                def _(dve):
                    link = linked(dve, chain)
                    link(nc.vector.tensor_scalar(part_i[:], src_tl[:], P - 1, None, ALU.bitwise_and))
                    link(nc.vector.tensor_copy(lo_f[:], part_i[:]))
                    link(nc.vector.tensor_scalar(part_i[:], src_tl[:], 7, None, ALU.arith_shift_right))
                    link(nc.vector.tensor_copy(hi_f[:], part_i[:]))

                    def body(i, first):
                        for s in range(SLOTS):
                            c = i * SLOTS + s
                            if not first:
                                dve.wait_ge(counted, c - SLOTS + 1)
                            nc.vector.tensor_tensor(
                                lo_hot[:, s], iota[:, 0:P].unsqueeze(1).broadcast_to([P, CH, P]),
                                along(lo_f[:, bass.ds(c * CH, CH)], P), ALU.is_equal).then_inc(hot_ready, 1)
                            nc.vector.tensor_tensor(
                                hi_hot[:, s], iota[:, 0:NB].unsqueeze(1).broadcast_to([P, CH, NB]),
                                along(hi_f[:, bass.ds(c * CH, CH)], NB), ALU.is_equal).then_inc(hot_ready, 1)

                    steps(dve, body)
                    dve.wait_ge(counted, V // CH)
                    nc.vector.tensor_scalar(deg[:], deg_ps[:], 1.0, None, ALU.max).then_inc(deg_ready, 1)
                    dve.wait_ge(root_ready, 1)
                    link(nc.vector.reciprocal(deg[:], root[:]))
                    nc.vector.tensor_tensor(xs[:], xcur[:], along(deg[:], D), ALU.mult).then_inc(xs_ready, 1)

                @block.tensor
                def _(pe):
                    nc.tensor.matmul(deg_ps[:], zeros16[:, 0:P], zeros16[:, 0:NB], start=True, stop=True, skip_group_check=True)

                    def body(i, first):
                        for s in range(SLOTS):
                            c = i * SLOTS + s
                            pe.wait_ge(hot_ready, 2 * (c + 1))
                            for k in range(CH):
                                last = nc.tensor.matmul(deg_ps[:], lo_hot[:, s, k], hi_hot[:, s, k], start=False, stop=True,
                                                        skip_group_check=True)
                            last.then_inc(counted, 1)

                    steps(pe, body)

                @block.scalar
                def _(act):
                    act.wait_ge(deg_ready, 1)
                    nc.scalar.sqrt(root[:], deg[:]).then_inc(root_ready, 1)

                @block.sync
                def _(sp):
                    sp.wait_ge(xs_ready, 1)
                    sp.dma_start(node_rows(table0), xs[:]).then_inc(xs_out, 16)
                    sp.wait_ge(xs_out, 16)

        TOP = (NG - 1) * BANK + (BPB - 1) * AW

        def zero_sums(acc, summed):
            for b in range(NG):
                last = nc.tensor.matmul(acc[:, b * BANK:(b + 1) * BANK], zeros16[:, 0:P], zeros16[:], start=True, stop=True,
                                        skip_group_check=True)
            last.then_inc(summed, 1)

        def add_visit(acc, at, hot, row):
            return nc.tensor.matmul(acc[:, bass.ds(at, row.shape[-1])], hot, row, start=False, stop=True, skip_group_check=True)

        def keep_sums(dve, acc, summed, kept, width):
            dve.wait_ge(summed, V + 1)
            for b in range(NG):
                nc.vector.tensor_copy(agg[:, b * BPB:(b + 1) * BPB, 0:width],
                                      acc[:, b * BANK:b * BANK + BPB * AW].rearrange("p (b f) -> p b f", f=AW)[:, :, 0:width])\
                    .then_inc(kept, 1)
            dve.wait_ge(kept, NG)

        def gather_sum(tag, table):
            with ExitStack() as st:
                tsb, tps = fresh(nc, st)
                rows = tsb(f"rows_{tag}", [P, SLOTS, CH, D + 1])
                idx_c = tsb(f"idx_c_{tag}", [P, SLOTS, CH], I32)
                rel_c = tsb(f"rel_c_{tag}", [P, SLOTS, CH])
                hot = tsb(f"hot_{tag}", [P, RING, P])
                acc = tps(f"acc_{tag}", [P, NG * BANK])
                chunk_ready = sem(f"chunk_ready_{tag}")
                gathered = [sem(f"gathered_{tag}_{s}") for s in range(SLOTS)]
                hot_ready = sem(f"hot_ready_{tag}")
                summed = sem(f"summed_{tag}")
                kept = sem(f"kept_{tag}")
                one = sem(f"one_{tag}")
                with nc.Block() as block:
                    @block.scalar
                    def _(act):
                        def body(i, first):
                            for s in range(SLOTS):
                                c = i * SLOTS + s
                                if not first:
                                    act.wait_ge(summed, 1 + i * BODY + (s + 1 - SLOTS) * CH)
                                nc.scalar.copy(idx_c[:, s], src_tl[:, bass.ds(c * CH, CH)]).then_inc(chunk_ready, 1)
                                nc.scalar.copy(rel_c[:, s], rel_tl[:, bass.ds(c * CH, CH)]).then_inc(chunk_ready, 1)

                        steps(act, body)

                    @block.gpsimd
                    def _(pool):
                        def body(i, first):
                            for s in range(SLOTS):
                                want = held(pool, 2 * (i * SLOTS + s + 1))
                                pool.wait_ge(one, 1)
                                pool.wait_ge(chunk_ready, want)
                                for k in range(CH):
                                    pool.indirect_dma_start(rows[:, s, k, 0:D], None, table,
                                                            bass.IndirectOffsetOnAxis(idx_c[:, s, k:k + 1], 0)).then_inc(gathered[s], 16)

                        steps(pool, body)

                    @block.vector
                    def _(dve):
                        nc.vector.memset(rows[:, :, :, D:D + 1], 1.0).then_inc(one, 1)

                        def body(i, first):
                            for s in range(SLOTS):
                                dve.wait_ge(chunk_ready, 2 * (i * SLOTS + s + 1))
                                for k in range(CH):
                                    n = s * CH + k
                                    if not (first and n < RING):
                                        dve.wait_ge(summed, 1 + i * BODY + n - RING + 1)
                                    nc.vector.tensor_scalar(hot[:, n % RING], iota[:], rel_c[:, s, k:k + 1], None, ALU.is_equal)\
                                        .then_inc(hot_ready, 1)

                        steps(dve, body)
                        keep_sums(dve, acc, summed, kept, D + 1)

                    @block.tensor
                    def _(pe):
                        zero_sums(acc, summed)
                        pe.wait_ge(one, 1)

                        def body(i, first):
                            for s in range(SLOTS):
                                _, at = nc.values_load_multi_w_load_instructions(
                                    offs[0:1, bass.ds((i * SLOTS + s) * CH, CH)], engines=PE_ONLY, min_val=0, max_val=TOP)
                                pe.wait_ge(gathered[s], 16 * CH * (i + 1))
                                for k in range(CH):
                                    n = s * CH + k
                                    pe.wait_ge(hot_ready, i * BODY + n + 1)
                                    add_visit(acc, at[k], hot[:, n % RING], rows[:, s, k, :]).then_inc(summed, 1)

                        steps(pe, body)

        def attend(tag, table, idx_tl, row, width, score_at, heads, target, curve):
            sums = width if heads == 1 else heads * (HD + 1)
            part = sums // heads
            PIECE = 16
            with ExitStack() as st:
                tsb, tps = fresh(nc, st)
                rows = tsb(f"rows_{tag}", [P, 2, P, width])
                idx_c = tsb(f"idx_c_{tag}", [P, 2, P], I32)
                rel_c = tsb(f"rel_c_{tag}", [P, 2, P])
                hot = tsb(f"hot_{tag}", [P, RING, P])
                msg = tsb(f"msg_{tag}", [P, 2, PIECE, sums]) if heads > 1 else None
                prob = tsb(f"prob_{tag}", [P, heads, P])
                score = tsb(f"score_{tag}", [P, heads, P])
                local = tsb(f"local_{tag}", [P, heads, P])
                best = tsb(f"best_{tag}", [P, heads, P])
                best_b = tsb(f"best_b_{tag}", [P, heads, P])
                tail = tsb(f"tail_{tag}", [P, heads])
                carry = tsb(f"carry_{tag}", [P, 2, heads])
                tails = tsb(f"tails_{tag}", [heads, P])
                state = tsb(f"state_{tag}", [heads, P])
                before = tsb(f"before_{tag}", [heads, P])
                so_far = tsb(f"so_far_{tag}", [heads, 1])
                rise = tsb(f"rise_{tag}", [1, heads + 1])
                scale = tsb(f"scale_{tag}", [P, heads + 1])
                acc = tps(f"acc_{tag}", [P, NG * BANK])
                work = tps(f"work_{tag}", [P, BANK])
                chain_sem = sem(f"chain_{tag}")
                chunk_ready = sem(f"chunk_ready_{tag}")
                gathered = [sem(f"gathered_{tag}_{s}") for s in range(2)]
                scores_done = sem(f"scores_done_{tag}")
                tails_ready = sem(f"tails_ready_{tag}")
                tails_done = sem(f"tails_done_{tag}")
                before_ready = sem(f"before_ready_{tag}")
                before_done = sem(f"before_done_{tag}")
                rise_ready = sem(f"rise_ready_{tag}")
                rise_spread = sem(f"rise_spread_{tag}")
                rise_done = sem(f"rise_done_{tag}")
                diff_ready = sem(f"diff_ready_{tag}")
                exp_ready = sem(f"exp_ready_{tag}")
                factor_ready = sem(f"factor_ready_{tag}")
                prob_done = sem(f"prob_done_{tag}")
                scaled = sem(f"scaled_{tag}")
                msg_ready = sem(f"msg_ready_{tag}")
                hot_ready = sem(f"hot_ready_{tag}")
                summed = sem(f"summed_{tag}")
                kept = sem(f"kept_{tag}")
                one = sem(f"one_{tag}")

                def groups(engine, body):
                    body(0, 0, 0, True)
                    with engine.Fori(0, G // 2) as j:
                        body(1 + 2 * j, 1, j, False)
                        body(2 + 2 * j, 0, j + 1, False)

                with nc.Block() as block:
                    @block.scalar
                    def _(act):
                        def columns(g, u):
                            nc.scalar.copy(idx_c[:, u], idx_tl[:, bass.ds(g * P, P)]).then_inc(chunk_ready, 1)
                            nc.scalar.copy(rel_c[:, u], rel_tl[:, bass.ds(g * P, P)]).then_inc(chunk_ready, 1)

                        def exps(g, first):
                            act.wait_ge(diff_ready, g + 1)
                            nc.scalar.activation(score[:], score[:], ACT.Exp).then_inc(exp_ready, 1)
                            if not first:
                                act.wait_ge(rise_done, g)
                                nc.scalar.activation(scale[:, 0:heads], scale[:, 0:heads], ACT.Exp).then_inc(factor_ready, 1)

                        def body(g, u, uses, first):
                            if first:
                                columns(0, 0)
                                columns(1, 1)
                            else:
                                act.wait_ge(summed, 1 + P * g)
                                columns(g + 1, 1 - u)
                            exps(g, first)

                        body(0, 0, 0, True)
                        with act.Fori(0, G // 2 - 1) as j:
                            body(1 + 2 * j, 1, j, False)
                            body(2 + 2 * j, 0, j + 1, False)
                        body(G - 2, 1, G // 2 - 1, False)
                        exps(G - 1, False)

                    @block.gpsimd
                    def _(pool):
                        def body(g, u, uses, first):
                            want = held(pool, 2 * (g + 1))
                            pool.wait_ge(one, 1)
                            pool.wait_ge(chunk_ready, want)
                            for k in range(P):
                                pool.indirect_dma_start(rows[:, u, k, 0:row], None, table,
                                                        bass.IndirectOffsetOnAxis(idx_c[:, u, k:k + 1], 0)).then_inc(gathered[u], 16)

                        groups(pool, body)

                    @block.vector
                    def _(dve):
                        if width > row:
                            nc.vector.memset(rows[:, :, :, row:width], 1.0).then_inc(one, 1)
                        else:
                            nc.vector.memset(tail[:], 0.0).then_inc(one, 1)
                        LINKS = 16 + 4 * heads

                        def body(g, u, uses, first):
                            done = [0]

                            def link(ins):
                                done[0] += 1
                                ins.then_inc(chain_sem, 1)
                                dve.wait_ge(chain_sem, g * LINKS + done[0])

                            def way(n, mneg, goes, what, into, flip, end):
                                v = (lambda a: a[:, ::-1]) if flip else (lambda a: a)
                                m = mneg[:, bass.ds(g, 1), :].rearrange("p o c -> p (o c)")
                                go = goes[0:heads, bass.ds(g, 1), :].rearrange("p o c -> p (o c)")
                                for h in range(heads):
                                    link(nc.vector.tensor_tensor_scan(v(local[:, h]), m, v(what[:, h]), LOW, ALU.add, ALU.max))
                                nc.vector.tensor_copy(tail[:], local[:, :, end]).then_inc(tails_ready, 1)
                                dve.wait_ge(tails_done, 2 * g + n + 1)
                                link(nc.vector.tensor_copy(tails[:], work[0:heads, 0:P]))
                                start = LOW if flip or first else so_far[:, 0:1]
                                link(nc.vector.tensor_tensor_scan(v(state[:]), go, v(tails[:]), start, ALU.add, ALU.max))
                                if flip:
                                    link(nc.vector.memset(before[:, P - 1:P], LOW))
                                    nc.vector.tensor_copy(before[:, 0:P - 1], state[:, 1:P]).then_inc(before_ready, 1)
                                else:
                                    if first:
                                        link(nc.vector.memset(before[:, 0:1], LOW))
                                    else:
                                        link(nc.vector.tensor_copy(before[:, 0:1], so_far[:]))
                                    link(nc.vector.tensor_copy(so_far[:], state[:, P - 1:P]))
                                    nc.vector.tensor_copy(before[:, 1:P], state[:, 0:P - 1]).then_inc(before_ready, 1)
                                dve.wait_ge(before_done, 2 * g + n + 1)
                                link(nc.vector.tensor_copy(carry[:, n], work[:, 0:heads]))
                                for h in range(heads):
                                    link(nc.vector.tensor_tensor_scan(v(into[:, h]), m, v(what[:, h]), carry[:, n, h:h + 1], ALU.add, ALU.max))

                            dve.wait_ge(scores_done, g + 1)
                            link(nc.vector.tensor_tensor(score[:], work[:, 0:heads * P].rearrange("p (h c) -> p h c", h=heads),
                                                         target[:, :, bass.ds(g * P, P)], ALU.add))
                            link(curve(score[:]))
                            way(0, mneg_f, goes_f, score, best, False, P - 1)
                            way(1, mneg_b, goes_b, best, best_b, True, 0)
                            nc.vector.tensor_tensor(score[:], score[:], best_b[:], ALU.subtract).then_inc(diff_ready, 1)
                            dve.wait_ge(prob_done, g + 1)
                            link(nc.vector.tensor_copy(prob[:], work[:, 0:heads * P].rearrange("p (h c) -> p h c", h=heads)))
                            if not first:
                                link(nc.vector.tensor_tensor(rise[:, 0:heads], carry[0:1, 0], best_b[0:1, :, 0], ALU.subtract))
                                link(nc.vector.tensor_scalar(rise[:, 0:heads], rise[:, 0:heads], cont[0:1, bass.ds(g, 1)], None, ALU.mult))
                                nc.vector.tensor_copy(rise[:, heads:heads + 1], rel_first[0:1, bass.ds(g, 1)]).then_inc(rise_ready, 1)
                                dve.wait_ge(rise_spread, g)
                                link(nc.vector.tensor_copy(scale[:], work[:, 0:heads + 1]))
                                link(nc.vector.tensor_tensor(scale[:, heads:heads + 1], scale[:, heads:heads + 1], own[:], ALU.is_equal))
                                nc.vector.tensor_scalar(scale[:, 0:heads], scale[:, 0:heads], scale[:, heads:heads + 1], None, ALU.mult)\
                                    .then_inc(rise_done, 1)
                                dve.wait_ge(factor_ready, g)
                                dve.wait_ge(summed, 1 + P * g)
                                at = dve.value_load(offs[0:1, bass.ds(g * P, 1)], min_val=0, max_val=TOP)
                                for h in range(heads):
                                    here = acc[:, bass.ds(at + h * part, part)]
                                    nc.vector.tensor_scalar(here, here, scale[:, h:h + 1], None, ALU.mult).then_inc(scaled, 1)
                            if first:
                                for _ in range(LINKS - done[0]):
                                    link(nc.vector.memset(tail[:], 0.0))
                            assert done[0] == LINKS

                            for k in range(P):
                                n = g * P + k
                                if heads > 1 and k % PIECE == 0:
                                    m = k // PIECE
                                    if not (first and m < 2):
                                        dve.wait_ge(summed, 1 + g * P + k - PIECE)
                                    nc.vector.tensor_tensor(
                                        msg[:, m % 2].rearrange("p k (h d) -> p k h d", h=heads),
                                        rows[:, u, k:k + PIECE, 0:sums].rearrange("p k (h d) -> p k h d", h=heads),
                                        prob[:, :, k:k + PIECE].rearrange("p h k -> p k h").unsqueeze(3).broadcast_to([P, PIECE, heads, part]),
                                        ALU.mult).then_inc(msg_ready, 1)
                                if not (first and k < RING):
                                    dve.wait_ge(summed, 1 + n - RING + 1)
                                if heads > 1:
                                    ins = nc.vector.tensor_scalar(hot[:, k % RING], iota[:], rel_c[:, u, k:k + 1], None, ALU.is_equal)
                                else:
                                    ins = nc.vector.tensor_scalar(hot[:, k % RING], iota[:], rel_c[:, u, k:k + 1], prob[:, 0, k:k + 1],
                                                                  ALU.is_equal, ALU.mult)
                                ins.then_inc(hot_ready, 1)

                        groups(dve, body)
                        keep_sums(dve, acc, summed, kept, sums)

                    @block.tensor
                    def _(pe):
                        zero_sums(acc, summed)
                        pe.wait_ge(one, 1)

                        def body(g, u, uses, first):
                            pe.wait_ge(gathered[u], 16 * P * (uses + 1))
                            for h in range(heads):
                                last = nc.tensor.transpose(work[:, h * P:(h + 1) * P], rows[:, u, :, score_at + h], ident[:])
                            last.then_inc(scores_done, 1)
                            for n in range(2):
                                want = held(pe, 2 * g + n + 1)
                                pe.wait_ge(one, 1)
                                pe.wait_ge(tails_ready, want)
                                nc.tensor.transpose(work[0:heads, 0:P], tail[:], ident[:]).then_inc(tails_done, 1)
                                pe.wait_ge(one, 1)
                                pe.wait_ge(before_ready, want)
                                nc.tensor.transpose(work[:, 0:heads], before[:], ident[0:heads, 0:heads]).then_inc(before_done, 1)
                            pe.wait_ge(exp_ready, g + 1)
                            for h in range(heads):
                                last = nc.tensor.transpose(work[:, h * P:(h + 1) * P], score[:, h], ident[:])
                            last.then_inc(prob_done, 1)
                            if not first:
                                want = held(pe, g)
                                pe.wait_ge(one, 1)
                                pe.wait_ge(rise_ready, want)
                                nc.tensor.matmul(work[:, 0:heads + 1], ones[0:1, :], rise[:], start=True, stop=True).then_inc(rise_spread, 1)
                                pe.wait_ge(scaled, heads * g)
                            for lo in range(0, P, CH):
                                _, at = nc.values_load_multi_w_load_instructions(
                                    offs[0:1, bass.ds(g * P + lo, CH)], engines=PE_ONLY, min_val=0, max_val=TOP)
                                if heads > 1:
                                    pe.wait_ge(msg_ready, g * (P // PIECE) + lo // PIECE + 1)
                                for k in range(lo, lo + CH):
                                    pe.wait_ge(hot_ready, g * P + k + 1)
                                    what = rows[:, u, k, :] if heads == 1 else msg[:, (k // PIECE) % 2, k % PIECE, :]
                                    add_visit(acc, at[k - lo], hot[:, k % RING], what).then_inc(summed, 1)

                        groups(pe, body)

        def normalise(tag, y, tmp, small, result_out=None):
            chain = Count(sem(f"norm_chain_{tag}"))
            var_ready = sem(f"var_ready_{tag}")
            std_ready = sem(f"std_ready_{tag}")
            x_ready = sem(f"x_ready_{tag}")
            x_out = sem(f"x_out_{tag}")
            mean, var, std, rstd = (small[:, n] for n in range(4))
            with nc.Block() as block:
                @block.vector
                def _(dve):
                    link = linked(dve, chain)
                    link(nc.vector.reduce_sum(mean, y[:], AX))
                    link(nc.vector.tensor_scalar(mean, mean, 1.0 / D, None, ALU.mult))
                    link(nc.vector.tensor_tensor(y[:], y[:], along(mean, D), ALU.subtract))
                    link(nc.vector.tensor_tensor(tmp[:], y[:], y[:], ALU.mult))
                    link(nc.vector.reduce_sum(var, tmp[:], AX))
                    nc.vector.tensor_scalar(var, var, 1.0 / D, EPS, ALU.mult, ALU.add).then_inc(var_ready, 1)
                    dve.wait_ge(std_ready, 1)
                    link(nc.vector.reciprocal(rstd, std))
                    nc.vector.tensor_tensor(xcur[:], y[:], along(rstd, D), ALU.mult).then_inc(x_ready, 1)

                @block.scalar
                def _(act):
                    act.wait_ge(var_ready, 1)
                    nc.scalar.sqrt(std, var).then_inc(std_ready, 1)

                @block.sync
                def _(sp):
                    if result_out is not None:
                        sp.wait_ge(x_ready, 1)
                        n = result_out(sp, x_out)
                        sp.wait_ge(x_out, n)

        def mlp(tag, w_in, b_in, w_out, b_out, hidden, func, y, prepare):
            with ExitStack() as st:
                tsb, tps = fresh(nc, st)
                wa = tsb(f"wa_{tag}", [D, hidden])
                ba = tsb(f"ba_{tag}", [hidden, 1])
                wb = tsb(f"wb_{tag}", [hidden, D])
                bb = tsb(f"bb_{tag}", [P, D])
                h = tsb(f"h_{tag}", [P, BPB, D])
                h_t = tsb(f"h_t_{tag}", [D, BPB * P])
                g_t = tsb(f"g_t_{tag}", [hidden, BPB * P])
                t_ps = tps(f"t_ps_{tag}", [D, 2 * BANK])
                g_ps = tps(f"g_ps_{tag}", [hidden, 2 * BANK])
                o_ps = tps(f"o_ps_{tag}", [P, BPB * D])
                loaded = sem(f"weights_{tag}")
                chain = Count(sem(f"mlp_chain_{tag}"))
                h_ready = sem(f"h_ready_{tag}")
                t_done = sem(f"t_done_{tag}")
                ht_ready = sem(f"ht_ready_{tag}")
                g_done = sem(f"g_done_{tag}")
                gt_ready = sem(f"gt_ready_{tag}")
                o_done = sem(f"o_done_{tag}")
                y_done = sem(f"y_done_{tag}")
                with nc.Block() as block:
                    @block.sync
                    def _(sp):
                        sp.dma_start(wa[:], w_in).then_inc(loaded, 16)
                        sp.dma_start(ba[:], b_in.unsqueeze(1)).then_inc(loaded, 16)
                        sp.dma_start(wb[:], w_out).then_inc(loaded, 16)
                        sp.dma_start(bb[:], b_out.partition_broadcast(P)).then_inc(loaded, 16)

                    @block.vector
                    def _(dve):
                        link = linked(dve, chain)
                        group = prepare(dve, link, h)
                        dve.wait_ge(loaded, 64)
                        link(nc.vector.tensor_tensor(y[:], xcur[:], bb[:].unsqueeze(1).broadcast_to([P, NB, D]), ALU.add))
                        with dve.Fori(0, NG) as g:
                            group(g).then_inc(h_ready, 1)
                            dve.wait_ge(t_done, g + 1)
                            nc.vector.tensor_copy(h_t[:], t_ps[:, 0:BPB * P]).then_inc(ht_ready, 1)
                            dve.wait_ge(o_done, g + 1)
                            yg = y[:, bass.ds(g * BPB, BPB), :]
                            nc.vector.tensor_tensor(yg, yg, o_ps[:].rearrange("p (b f) -> p b f", f=D), ALU.add).then_inc(y_done, 1)
                        dve.wait_ge(y_done, NG)

                    @block.tensor
                    def _(pe):
                        pe.wait_ge(loaded, 64)
                        with pe.Fori(0, NG) as g:
                            want = held(pe, g + 1)
                            pe.wait_ge(loaded, 64)
                            pe.wait_ge(h_ready, want)
                            for b in range(BPB):
                                last = nc.tensor.transpose(t_ps[:, b * P:(b + 1) * P], h[:, b], ident[:])
                            last.then_inc(t_done, 1)
                            want = held(pe, g + 1)
                            pe.wait_ge(loaded, 64)
                            pe.wait_ge(ht_ready, want)
                            for a, b in ((0, BANK), (BANK, BPB * P)):
                                last = nc.tensor.matmul(g_ps[:, a:b], wa[:], h_t[:, a:b], start=True, stop=True)
                            last.then_inc(g_done, 1)
                            want = held(pe, g + 1)
                            pe.wait_ge(loaded, 64)
                            pe.wait_ge(gt_ready, want)
                            for b in range(BPB):
                                last = nc.tensor.matmul(o_ps[:, b * D:(b + 1) * D], g_t[:, b * P:(b + 1) * P], wb[:], start=True, stop=True)
                            last.then_inc(o_done, 1)

                    @block.scalar
                    def _(act):
                        act.wait_ge(loaded, 64)
                        with act.Fori(0, NG) as g:
                            act.wait_ge(g_done, g + 1)
                            nc.scalar.activation(g_t[:], g_ps[:, 0:BPB * P], func, bias=ba[:, 0:1]).then_inc(gt_ready, 1)

        def project(tag, weights, cols, split, table, nodes, emit, make_weights):
            with ExitStack() as st:
                tsb, tps = fresh(nc, st)
                wsum = tsb(f"wsum_{tag}", [D, cols])
                h = tsb(f"ph_{tag}", [P, BPB, D])
                h_t = tsb(f"ph_t_{tag}", [D, BPB * P])
                stage, node = emit["buffers"](tsb)
                t_ps = tps(f"pt_ps_{tag}", [D, 2 * BANK])
                z_ps = tps(f"z_ps_{tag}", [P, 3, 2, BANK])
                chain = Count(sem(f"proj_chain_{tag}"))
                w_ready = sem(f"w_ready_{tag}")
                h_ready = sem(f"ph_ready_{tag}")
                t_done = sem(f"pt_done_{tag}")
                ht_ready = sem(f"pht_ready_{tag}")
                z_done = sem(f"z_done_{tag}")
                z_kept = sem(f"z_kept_{tag}")
                staged = sem(f"staged_{tag}")
                nodes_out = sem(f"nodes_out_{tag}")
                loaded = sem(f"pw_{tag}")

                with nc.Block() as block:
                    @block.sync
                    def _(sp):
                        make_weights["load"](sp, loaded)

                        def body(g, first):
                            for b in range(BPB):
                                sp.wait_ge(z_kept, g * BPB + b + 1)
                                emit["store"](sp, table, stage, g * BPB + b, b).then_inc(staged, 16)

                        body(0, True)
                        with sp.Fori(1, NG) as g:
                            body(g, False)
                        sp.dma_start(node_rows(nodes), node[:]).then_inc(nodes_out, 16)
                        sp.wait_ge(staged, 16 * NB)
                        sp.wait_ge(nodes_out, 16)

                    @block.vector
                    def _(dve):
                        link = linked(dve, chain)
                        make_weights["compute"](dve, link, loaded, tsb, wsum).then_inc(w_ready, 1)
                        emit["ones"](link, stage)

                        def body(g, first):
                            nc.vector.tensor_copy(h[:], xcur[:, bass.ds(g * BPB, BPB), :] if not first else xcur[:, 0:BPB, :])\
                                .then_inc(h_ready, 1)
                            dve.wait_ge(t_done, g + 1)
                            nc.vector.tensor_copy(h_t[:], t_ps[:, 0:BPB * P]).then_inc(ht_ready, 1)
                            if not first:
                                dve.wait_ge(staged, g * (16 * BPB))
                            for b in range(BPB):
                                dve.wait_ge(z_done, g * BPB + b + 1)
                                emit["keep"](z_ps[:, b % 3], stage, node, g * BPB + b, b).then_inc(z_kept, 1)

                        body(0, True)
                        with dve.Fori(1, NG) as g:
                            body(g, False)

                    @block.tensor
                    def _(pe):
                        pe.wait_ge(w_ready, 1)

                        def body(g, first):
                            want = held(pe, g + 1)
                            pe.wait_ge(w_ready, 1)
                            pe.wait_ge(h_ready, want)
                            for b in range(BPB):
                                last = nc.tensor.transpose(t_ps[:, b * P:(b + 1) * P], h[:, b], ident[:])
                            last.then_inc(t_done, 1)
                            want = held(pe, g + 1)
                            pe.wait_ge(w_ready, 1)
                            pe.wait_ge(ht_ready, want)
                            for b in range(BPB):
                                if b >= 3:
                                    pe.wait_ge(z_kept, g * BPB + b - 2)
                                elif not first:
                                    pe.wait_ge(z_kept, g * BPB)
                                for n, (lo, hi) in enumerate(split):
                                    last = nc.tensor.matmul(z_ps[:, b % 3, n, 0:hi - lo], h_t[:, b * P:(b + 1) * P], wsum[:, lo:hi],
                                                            start=True, stop=True)
                                last.then_inc(z_done, 1)

                        body(0, True)
                        with pe.Fori(1, NG) as g:
                            body(g, False)

        def spread(tag, cols, node, nodes, edges, starts, out_of):
            scattered = sem(f"scattered_{tag}")
            first_in = sem(f"first_in_{tag}")
            loaded = sem(f"spread_in_{tag}")
            done = sem(f"spread_done_{tag}")
            with ExitStack() as st:
                tsb, _ = fresh(nc, st)
                first = tsb(f"first_{tag}", [P, cols])
                with nc.Block() as block:
                    @block.gpsimd
                    def _(pool):
                        pool.indirect_dma_start(first[:], None, nodes, bass.IndirectOffsetOnAxis(first_dst[:, 0:1], 0)).then_inc(first_in, 16)
                        for b in range(NB):
                            k = P if b < NB - 1 else NLAST
                            pool.indirect_dma_start(edges, bass.IndirectOffsetOnAxis(runstart[0:k, b:b + 1], 0), node[0:k, b, :], None)\
                                .then_inc(scattered, 16)

                    @block.sync
                    def _(sp):
                        sp.wait_ge(scattered, 16 * NB)
                        sp.dma_start(starts[:], edges[0:VP, :].rearrange("(p j) r -> p j r", p=P)).then_inc(loaded, 16)

                    @block.vector
                    def _(dve):
                        dve.wait_ge(first_in, 16)
                        dve.wait_ge(loaded, 16)
                        for r in range(cols):
                            nc.vector.tensor_tensor_scan(out_of(r), inside[:], starts[:, :, r], first[:, r:r + 1], ALU.mult, ALU.add)\
                                .then_inc(done, 1)
                        dve.wait_ge(done, cols)

        gather_sum("l0", table0)

        with ExitStack() as st:
            tsb, tps = fresh(nc, st)
            y = tsb("y0", [P, NB, D])
            tmp = tsb("tmp0", [P, NB, D])
            small = tsb("small0", [P, 4, NB])
            deg = tsb("in_deg", [P, NB])
            root = tsb("in_root", [P, NB])
            scale = tsb("in_scale", [P, NB])
            count_ps = tps("count_ps", [P, 2, BANK])
            total = tsb("total", [P, NB])
            upto = tsb("upto", [P, NB])
            deg_done = sem("in_deg_done")
            deg_ready = sem("in_deg_ready")
            root_ready = sem("in_root_ready")
            counts_ready = sem("counts_ready")
            counts_done = sem("counts_done")
            chain = Count(sem("runstart_chain"))
            with nc.Block() as block:
                @block.vector
                def _(dve):
                    link = linked(dve, chain)
                    nc.vector.tensor_copy(total[:], agg[:, :, D]).then_inc(counts_ready, 1)
                    nc.vector.tensor_scalar(deg[:], agg[:, :, D], 1.0, None, ALU.max).then_inc(deg_ready, 1)
                    dve.wait_ge(counts_done, 1)
                    link(nc.vector.tensor_copy(total[:], count_ps[:, 1, 0:NB]))
                    link(nc.vector.tensor_tensor_scan(upto[:], ones[:, 0:NB], total[:], 0.0, ALU.mult, ALU.add))
                    link(nc.vector.tensor_tensor(upto[:], upto[:], total[:], ALU.subtract))
                    link(nc.vector.tensor_tensor(upto[:], upto[:], count_ps[:, 0, 0:NB], ALU.add))
                    link(nc.vector.scalar_tensor_tensor(upto[:], iota[:, 0:NB], float(P), upto[:], ALU.mult, ALU.add))
                    link(nc.vector.tensor_scalar(total[:], agg[:, :, D], 0.0, float(VP), ALU.is_equal, ALU.mult))
                    link(nc.vector.tensor_tensor(upto[:], upto[:], total[:], ALU.max))
                    link(nc.vector.tensor_copy(runstart[:], upto[:]))
                    dve.wait_ge(root_ready, 1)
                    link(nc.vector.reciprocal(scale[:], root[:]))

                @block.scalar
                def _(act):
                    act.wait_ge(deg_ready, 1)
                    nc.scalar.sqrt(root[:], deg[:]).then_inc(root_ready, 1)

                @block.tensor
                def _(pe):
                    pe.wait_ge(counts_ready, 1)
                    nc.tensor.matmul(count_ps[:, 0, 0:NB], below[:], total[:], start=True, stop=True)
                    nc.tensor.matmul(count_ps[:, 1, 0:NB], ones[:], total[:], start=True, stop=True).then_inc(counts_done, 1)

            def mean_sum(dve, link, h):
                return lambda g: nc.vector.tensor_tensor(
                    h[:], agg[:, bass.ds(g * BPB, BPB), 0:D],
                    scale[:, bass.ds(g * BPB, BPB)].unsqueeze(2).broadcast_to([P, BPB, D]), ALU.mult)

            mlp("l0", w0a, b0a, w0b, b0b, D, ACT.Gelu, y, mean_sum)
            normalise("l0", y, tmp, small)
        recycle()

        with ExitStack() as layer:
            lsb, _ = fresh(nc, layer)
            node1 = lsb("node1", [P, NB, R])
            HALF = R // 2 * W1ROW

            def w1_load(sp, loaded):
                sp.dma_start(fc_s[:], fc.rearrange("r i o -> i r o")).then_inc(loaded, 16)
                sp.dma_start(attn_s[:], attn.rearrange("r k o -> (r k o)").partition_broadcast(D)).then_inc(loaded, 16)

            def w1_compute(dve, link, loaded, tsb, wsum):
                dve.wait_ge(loaded, 32)
                at = attn_s[:].rearrange("p (r k) -> p r k", r=R)
                link(nc.vector.tensor_tensor(prod[:], fc_s[:], at[:, :, 0:D], ALU.mult))
                link(nc.vector.reduce_sum(score_w[:, 0, :], prod[:], AX))
                link(nc.vector.tensor_tensor(prod[:], fc_s[:], at[:, :, D:2 * D], ALU.mult))
                link(nc.vector.reduce_sum(score_w[:, 1, :], prod[:], AX))
                for half in range(2):
                    to = wsum[:, half * (HALF + R):half * (HALF + R) + HALF].rearrange("p (r f) -> p r f", f=W1ROW)
                    rs = slice(half * R // 2, (half + 1) * R // 2)
                    link(nc.vector.tensor_copy(to[:, :, 0:D], fc_s[:, rs, :]))
                    link(nc.vector.tensor_copy(to[:, :, D], score_w[:, 0, rs]))
                return nc.vector.tensor_copy(wsum[:, HALF:HALF + R], score_w[:, 1, :])

            def keep1(z, stage, node, block, b):
                nc.vector.tensor_copy(stage[:, b, 0:HALF], z[:, 0, 0:HALF])
                nc.vector.tensor_copy(node[:, bass.ds(block, 1), :], z[:, 0, HALF:HALF + R].unsqueeze(1))
                return nc.vector.tensor_copy(stage[:, b, HALF:2 * HALF], z[:, 1, 0:HALF])

            with ExitStack() as st:
                tsb, _ = fresh(nc, st)
                fc_s = tsb("fc_s", [D, R, D])
                attn_s = tsb("attn_s", [D, R * 2 * D])
                prod = tsb("prod1", [D, R, D])
                score_w = tsb("score_w", [D, 2, R])
                table1_v = table1.rearrange("(b p r) f -> b p (r f)", p=P, r=R)
                project("l1", None, 2 * HALF + R, ((0, HALF + R), (HALF + R, 2 * HALF + R)), table1, nodes1,
                        dict(buffers=lambda tsb: (tsb("stage1", [P, BPB, 2 * HALF]), node1),
                             ones=lambda link, stage: None,
                             keep=keep1,
                             store=lambda sp, table, stage, block, b: sp.dma_start(
                                 table1_v[bass.ds(block, 1)].rearrange("o p f -> (o p) f"), stage[:, b])),
                        dict(load=w1_load, compute=w1_compute))

            target = lsb("target1", [P, 1, V])
            with ExitStack() as st:
                tsb, _ = fresh(nc, st)
                values = tsb("values1", [P, V, R])
                et_s = tsb("et_s", [P, V])
                pick = tsb("pick", [P, 2, V])
                score_s = tsb("target_s", [P, V])
                loaded = sem("et_loaded")
                picked = sem("picked")
                target_out = sem("target_out1")
                target_in = sem("target_in1")
                chain = Count(sem("pick_chain"))
                spread("l1", R, node1, nodes1, spread1, values, lambda r: values[:, :, r])
                with nc.Block() as block:
                    @block.sync
                    def _(sp):
                        sp.dma_start(et_s[:], et_d.rearrange("(p j) -> p j", p=P)).then_inc(loaded, 16)
                        sp.wait_ge(picked, 1)
                        sp.dma_start(target_d[0].rearrange("(p j) -> p j", p=P), score_s[:]).then_inc(target_out, 16)
                        sp.wait_ge(target_out, 16)
                        sp.dma_start(target[:, 0].rearrange("q (g c) -> q g c", c=P), target_d[0].rearrange("(g q c) -> q g c", q=P, c=P)).then_inc(target_in, 16)
                        sp.wait_ge(target_in, 16)

                    @block.vector
                    def _(dve):
                        link = linked(dve, chain)
                        dve.wait_ge(loaded, 16)
                        link(nc.vector.scalar_tensor_tensor(score_s[:], et_s[:], 0.0, values[:, :, 0], ALU.is_equal, ALU.mult))
                        for r in range(1, R):
                            link(nc.vector.scalar_tensor_tensor(pick[:, r % 2], et_s[:], float(r), values[:, :, r], ALU.is_equal, ALU.mult))
                            last = nc.vector.tensor_tensor(score_s[:], score_s[:], pick[:, r % 2], ALU.add)
                            if r < R - 1:
                                link(last)
                        last.then_inc(picked, 1)

            attend("a1", table1, idx1_tl, W1ROW, W1ROW + 1, D, 1, target,
                   lambda s: nc.vector.tensor_scalar(s, s, 0.0, None, ALU.max))


        def attention_mean(tag, y, count, at, heads, width):
            chain = Count(sem(f"mean_chain_{tag}"))
            with nc.Block() as block:
                @block.vector
                def _(dve):
                    link = linked(dve, chain)
                    link(nc.vector.tensor_scalar(count, at(agg), 1.0e-30, None, ALU.max))
                    link(nc.vector.reciprocal(count, count))
                    a4 = agg[:, :, 0:heads * width].rearrange("p b (h d) -> p b h d", h=heads)[:, :, :, 0:D // heads]
                    for h in range(heads):
                        link(nc.vector.tensor_tensor(y[:, :, h * (D // heads):(h + 1) * (D // heads)], a4[:, :, h],
                                                     along(count[:, h], D // heads), ALU.mult))
                    link(nc.vector.tensor_tensor(y[:], y[:], xcur[:], ALU.add))

        with ExitStack() as st:
            tsb, _ = fresh(nc, st)
            y = tsb("y1", [P, NB, D])
            tmp = tsb("tmp1", [P, NB, D])
            small = tsb("small1", [P, 4, NB])
            count = tsb("count1", [P, 1, NB])
            attention_mean("l1", y, count[:], lambda a: a[:, :, D + 1].unsqueeze(1), 1, W1ROW + 1)
            normalise("l1", y, tmp, small,
                      lambda sp, done: (sp.dma_start(node_rows(table2), xcur[:]).then_inc(done, 16), 16)[1])
        recycle()

        gather_sum("l2", table2)
        with ExitStack() as st:
            tsb, tps = fresh(nc, st)
            y = tsb("y2", [P, NB, D])
            tmp = tsb("tmp2", [P, NB, D])
            small = tsb("small2", [P, 4, NB])
            eps_s = tsb("eps_s", [P, 1])
            eps_in = sem("eps_in")
            eps_done = Count(sem("eps_done"))
            with nc.Block() as block:
                @block.sync
                def _(sp):
                    sp.dma_start(eps_s[:], eps2.partition_broadcast(P)).then_inc(eps_in, 16)

                @block.vector
                def _(dve):
                    dve.wait_ge(eps_in, 16)
                    linked(dve, eps_done)(nc.vector.tensor_scalar(eps_s[:], eps_s[:], 1.0, None, ALU.add))

            def own_and_sum(dve, link, h):
                return lambda g: nc.vector.scalar_tensor_tensor(
                    h[:], xcur[:, bass.ds(g * BPB, BPB), :], eps_s[:, 0:1], agg[:, bass.ds(g * BPB, BPB), 0:D], ALU.mult, ALU.add)

            mlp("l2", w2a, b2a, w2b, b2b, w2a.shape[1], ACT.Relu, y, own_and_sum)
            normalise("l2", y, tmp, small)
        recycle()

        with ExitStack() as layer:
            lsb, _ = fresh(nc, layer)
            node3 = lsb("node3", [P, NB, H])
            ve = lsb("ve", [P, 2 * H])
            KEY = H * (HD + 1)

            def w3_load(sp, loaded):
                sp.dma_start(wn_s[:], wn).then_inc(loaded, 16)
                for n, a in enumerate((ak, aq, ae)):
                    sp.dma_start(att_s[:, n], a.rearrange("h d -> (h d)").partition_broadcast(P)).then_inc(loaded, 16)
                for half in range(2):
                    sp.dma_start(we_s[half * D:(half + 1) * D, :], we).then_inc(loaded, 16)

            def w3_compute(dve, link, loaded, tsb, wsum):
                dve.wait_ge(loaded, 16 * 6)
                link(nc.vector.memset(wsum[:], 0.0))
                link(nc.vector.tensor_copy(wsum[:, 0:KEY].rearrange("p (h d) -> p h d", h=H)[:, :, 0:HD], wn_s[:].rearrange("p (h d) -> p h d", h=H)))
                link(nc.vector.memset(ve[:], 0.0))
                link(nc.vector.tensor_tensor(prod3[:], we_s[:], att_s[:, 2], ALU.mult))
                for half in range(2):
                    rs = slice(half * D, (half + 1) * D)
                    link(nc.vector.reduce_sum(ve[rs, half * H:(half + 1) * H], prod3[rs].rearrange("p (h d) -> p h d", h=H), AX))
                for n in range(2):
                    link(nc.vector.tensor_tensor(prod3[0:D], wn_s[:], att_s[0:D, n], ALU.mult))
                    last = nc.vector.reduce_sum(wsum[:, KEY + n * H:KEY + (n + 1) * H], prod3[0:D].rearrange("p (h d) -> p h d", h=H), AX)
                    if n == 0:
                        link(last)
                return last

            def keep3(z, stage, node, block, b):
                nc.vector.tensor_copy(stage[:, b, 0:KEY].rearrange("p (h d) -> p h d", h=H)[:, :, 0:HD],
                                      z[:, 0, 0:KEY].rearrange("p (h d) -> p h d", h=H)[:, :, 0:HD])
                nc.vector.tensor_copy(node[:, bass.ds(block, 1), :], z[:, 0, KEY + H:KEY + 2 * H].unsqueeze(1))
                return nc.vector.tensor_copy(stage[:, b, KEY:KEY + H], z[:, 0, KEY:KEY + H])

            with ExitStack() as st:
                tsb, _ = fresh(nc, st)
                wn_s = tsb("wn_s", [D, D])
                we_s = tsb("we_s", [P, D])
                att_s = tsb("att_s", [P, 3, D])
                prod3 = tsb("prod3", [P, D])
                table3_v = table3.rearrange("(b p) f -> b p f", p=P)
                project("l3", None, KEY + 2 * H, ((0, KEY + 2 * H),), table3, nodes3,
                        dict(buffers=lambda tsb: (tsb("stage3", [P, BPB, W3ROW]), node3),
                             ones=lambda link, stage: link(nc.vector.memset(stage[:], 1.0)),
                             keep=keep3,
                             store=lambda sp, table, stage, block, b: sp.dma_start(
                                 table3_v[bass.ds(block, 1)].rearrange("o p f -> (o p) f"), stage[:, b])),
                        dict(load=w3_load, compute=w3_compute))

            EC = 26
            NE = T // EC
            with ExitStack() as st:
                tsb, tps = fresh(nc, st)
                feat = tsb("feat", [P, 2, EC * D])
                feat_t = tsb("feat_t", [P, 2, 4 * P])
                part = tsb("part", [P, 2, EC * H])
                ft_ps = tps("ft_ps", [P, 2, BANK])
                we_ps = tps("we_ps", [P, 2, BANK])
                blank = sem("feat_blank")
                feat_in = [sem(f"feat_in{n}") for n in range(2)]
                ft_done = sem("ft_done")
                ft_kept = sem("ft_kept")
                we_done = sem("we_done")
                we_kept = sem("we_kept")
                part_out = [sem(f"part_out{n}") for n in range(2)]
                PAIRS = EC // 2
                QUADS = -(-PAIRS // 4)
                full = (E - (P - 1) * T) // EC
                attr = edge_attr[0:(P - 1) * T, :].rearrange("(p c j) f -> c p (j f)", p=P - 1, j=EC)
                last_attr = edge_attr[(P - 1) * T:(P - 1) * T + full * EC, :].rearrange("(c o j) f -> c o (j f)", o=1, j=EC)
                rest = E - (P - 1) * T - full * EC

                with nc.Block() as block:
                    @block.sync
                    def _(sp):
                        for c in range(NE):
                            s = c % 2
                            if c >= 2:
                                sp.wait_ge(ft_done, QUADS * (c - 1))
                            sp.dma_start(feat[0:P - 1, s], attr[c]).then_inc(feat_in[s], 16)
                            if c < full:
                                sp.dma_start(feat[P - 1:P, s], last_attr[c]).then_inc(feat_in[s], 16)
                            elif c == full:
                                sp.dma_start(feat[P - 1:P, s, 0:rest * D], edge_attr[E - rest:E, :].rearrange("(o j) f -> o (j f)", o=1)).then_inc(feat_in[s], 16)
                            else:
                                sp.dma_start(feat[P - 1:P, s, 0:D], edge_attr[E - 1:E, :]).then_inc(feat_in[s], 16)

                    @block.tensor
                    def _(pe):
                        quad = 0
                        for c in range(NE):
                            s = c % 2
                            pe.wait_ge(feat_in[s], 32 * (c // 2 + 1))
                            for qd in range(QUADS):
                                ps_ = range(4 * qd, min(4 * qd + 4, PAIRS))
                                if quad >= 2:
                                    pe.wait_ge(ft_kept, quad - 1)
                                for n, pr in enumerate(ps_):
                                    last = nc.tensor.transpose(ft_ps[:, quad % 2, n * P:(n + 1) * P], feat[:, s, 2 * pr * D:2 * (pr + 1) * D], ident[:])
                                last.then_inc(ft_done, 1)
                                if qd == 0 and c >= 2:
                                    pe.wait_ge(we_kept, c - 1)
                                pe.wait_ge(ft_kept, quad + 1)
                                for n, pr in enumerate(ps_):
                                    last = nc.tensor.matmul(we_ps[:, s, 2 * pr * H:2 * (pr + 1) * H], feat_t[:, quad % 2, n * P:(n + 1) * P], ve[:], start=True, stop=True)
                                quad += 1
                            last.then_inc(we_done, 1)

                    @block.scalar
                    def _(act):
                        quad = 0
                        for c in range(NE):
                            for qd in range(QUADS):
                                k = (min(4 * qd + 4, PAIRS) - 4 * qd) * P
                                act.wait_ge(ft_done, quad + 1)
                                nc.scalar.copy(feat_t[:, quad % 2, 0:k], ft_ps[:, quad % 2, 0:k]).then_inc(ft_kept, 1)
                                quad += 1

                    @block.vector
                    def _(dve):
                        for c in range(NE):
                            s = c % 2
                            dve.wait_ge(we_done, c + 1)
                            if c >= 2:
                                dve.wait_ge(part_out[s], 16 * (c // 2))
                            nc.vector.tensor_copy(part[:, s], we_ps[:, s, 0:EC * H]).then_inc(we_kept, 1)

                    @block.gpsimd
                    def _(pool):
                        for c in range(NE):
                            s = c % 2
                            pool.wait_ge(we_kept, c + 1)
                            pool.dma_start(we_d[:, c * EC * H:(c + 1) * EC * H], part[:, s]).then_inc(part_out[s], 16)
                        for s in range(2):
                            pool.wait_ge(part_out[s], 16 * (NE // 2))

            target = lsb("target3", [P, H, V])
            with ExitStack() as st:
                tsb, _ = fresh(nc, st)
                starts = tsb("starts3", [P, V, H])
                values = tsb("values3", [P, H, V])
                edge_r = tsb("edge_r", [P, G, P * H])
                target_out = sem("target_out3")
                target_in = sem("target_in3")
                edge_in = sem("edge_in")
                done = sem("target_done")
                spread("l3", H, node3, nodes3, spread3, starts, lambda r: values[:, r])
                with nc.Block() as block:
                    @block.gpsimd
                    def _(pool):
                        by_tile = we_d.rearrange("p x -> (p x)").rearrange("(t x) -> t x", x=P * H)
                        for g in range(G):
                            pool.indirect_dma_start(edge_r[:, g], None, by_tile, bass.IndirectOffsetOnAxis(tile_of[:, g:g + 1], 0)).then_inc(edge_in, 16)

                    @block.sync
                    def _(sp):
                        for h in range(H):
                            sp.dma_start(target_d[h].rearrange("(p j) -> p j", p=P), values[:, h]).then_inc(target_out, 16)
                        sp.wait_ge(target_out, 16 * H)
                        for h in range(H):
                            sp.dma_start(target[:, h].rearrange("q (g c) -> q g c", c=P), target_d[h].rearrange("(g q c) -> q g c", q=P, c=P)).then_inc(target_in, 16)

                    @block.vector
                    def _(dve):
                        dve.wait_ge(target_in, 16 * H)
                        dve.wait_ge(edge_in, 16 * G)
                        for h in range(H):
                            t = target[:, h].rearrange("q (g c) -> q g c", c=P)
                            nc.vector.tensor_tensor(t, t, edge_r[:].rearrange("q g (c h) -> q h g c", h=H)[:, h], ALU.add).then_inc(done, 1)
                        dve.wait_ge(done, H)

            attend("a3", table3, src_tl, W3ROW, W3ROW, KEY, H, target,
                   lambda s: nc.vector.scalar_tensor_tensor(s, s, 0.01, s, ALU.mult, ALU.max))


        with ExitStack() as st:
            tsb, _ = fresh(nc, st)
            y = tsb("y3", [P, NB, D])
            tmp = tsb("tmp3", [P, NB, D])
            small = tsb("small3", [P, 4, NB])
            count = tsb("count3", [P, H, NB])
            bias_s = tsb("bias_s", [P, D])
            bias_in = sem("bias_in")
            chain = Count(sem("bias_chain"))
            attention_mean("l3", y, count[:], lambda a: a[:, :, 0:KEY].rearrange("p b (h d) -> p h b d", h=H)[:, :, :, HD], H, HD + 1)
            with nc.Block() as block:
                @block.sync
                def _(sp):
                    sp.dma_start(bias_s[:], bias3.partition_broadcast(P)).then_inc(bias_in, 16)

                @block.vector
                def _(dve):
                    link = linked(dve, chain)
                    link(nc.vector.tensor_tensor(y[:], y[:], xcur[:], ALU.add))
                    dve.wait_ge(bias_in, 16)
                    link(nc.vector.tensor_tensor(y[:], y[:], bias_s[:].unsqueeze(1).broadcast_to([P, NB, D]), ALU.add))

            def store(sp, done):
                sp.dma_start(out[0:(NB - 1) * P, :].rearrange("(b p) f -> p b f", p=P), xcur[:, 0:NB - 1, :]).then_inc(done, 16)
                sp.dma_start(out[(NB - 1) * P:N, :], xcur[0:NLAST, NB - 1, :]).then_inc(done, 16)
                return 32

            normalise("l3", y, tmp, small, store)


_INS = ["x", "src", "dst", "edge_attr_64", "edge_type_8", "L0_gnn_w1", "L0_gnn_b1", "L0_gnn_w2", "L0_gnn_b2",
        "L1_gnn_fc_weight", "L1_gnn_attn_weight", "L2_gnn_eps", "L2_gnn_W1", "L2_gnn_b1", "L2_gnn_W2", "L2_gnn_b2",
        "L3_gnn_W_node", "L3_gnn_W_edge", "L3_gnn_attn_query", "L3_gnn_attn_key", "L3_gnn_attn_edge", "L3_gnn_bias"]


def kernel(**inputs):
    import numpy as np
    import concourse.bacc as bacc
    from concourse.bass_utils import run_bass_kernel_spmd

    nc = bacc.Bacc("TRN2", target_bir_lowering=False, num_devices=1)
    arrays, args = {}, []
    for name in _INS:
        a = np.ascontiguousarray(inputs[name])
        arrays[name] = a
        args.append(nc.dram_tensor(name, a.shape, mybir.dt.from_np(a.dtype), kind="ExternalInput").ap())
    args.append(nc.dram_tensor("out", (N, D), F32, kind="ExternalOutput").ap())
    build(nc, *args)
    return run_bass_kernel_spmd(nc, [arrays], core_ids=[0]).results[0]["out"]
```

```python
from contextlib import ExitStack
import itertools

import concourse.bass as bass
from concourse import mybir

F32 = mybir.dt.float32
BF16 = mybir.dt.bfloat16
I32 = mybir.dt.int32
ALU = mybir.AluOpType
ACT = mybir.ActivationFunctionType
AX = mybir.AxisListType.X
PE_ONLY = (mybir.EngineType.PE,)

P = 128
N = 6250
NB = -(-N // P)
NLAST = N - (NB - 1) * P
E = 206250
T = -(-E // P)
EP = T * P
G = -(-(T + NB - 1) // P)
V = G * P
VP = V * P
CH = 16
SLOTS = 4
BODY = CH * SLOTS
ITERS = V // BODY
RING = 8
QUAD = 4
EARLY = 2
HCH = 26
HSLOTS = 2
HITERS = T // (HCH * HSLOTS)
EQ = 125
PIECES = ITERS - 1
EC = E // (EQ * PIECES)
UNIT = 3
UNITS = EC // (2 * UNIT)
D = 64
R = 8
H = 4
HD = D // H
AW = 68
BANK = 512
BPB = BANK // AW
NG = NB // BPB
W1ROW = D + 1
W3ROW = H * (HD + 1) + H
HALVES = (0, NB // 2), (NB // 2, NB)
EPS = 1e-5
LOW = -3.0e38
assert E == EQ * PIECES * UNITS * UNIT * 2 and V == BODY * ITERS and T == HCH * HSLOTS * HITERS and NB == BPB * NG


class Count:

    def __init__(self, sem):
        self.sem, self.n = sem, 0

    def on(self, ins, k=1):
        ins.then_inc(self.sem, k)
        self.n += k
        return self.n


class Before:

    def __init__(self, sync, pool, vector):
        self.sync, self.pool, self.vector = sync, pool, vector


class Beside:

    def __init__(self, sync, vector_first, vector, vector_last, tensor, tensor_last):
        self.sync, self.vector_first, self.vector, self.vector_last = sync, vector_first, vector, vector_last
        self.tensor, self.tensor_last = tensor, tensor_last


def fresh(nc, ctx):
    def sb(name, shape, dt=F32):
        return ctx.enter_context(nc.sbuf_tensor(name, shape, dt))

    def ps(name, shape, dt=F32):
        return ctx.enter_context(nc.psum_tensor(name, shape, dt))

    return sb, ps


def linked(engine, count):

    def link(ins):
        engine.wait_ge(count.sem, count.on(ins))

    return link


def along(ap, n):
    return ap.unsqueeze(2).broadcast_to([ap.shape[0], ap.shape[1], n])


def node_rows(table):
    return table.rearrange("(b p) f -> p b f", p=P)


def build(nc, x, src, dst, edge_attr, etype, w0a, b0a, w0b, b0b, fc, attn, eps2, w2a, b2a, w2b, b2b,
          wn, we, aq, ak, ae, bias3, out):
    with ExitStack() as whole:
        sb, _ = fresh(nc, whole)

        live = []

        def sem(name):
            live.append(nc.alloc_semaphore(name=name))
            return live[-1]

        def recycle():
            nc.all_engine_barrier()
            nc.clear_and_free_semaphores(live)
            nc.all_engine_barrier()
            live.clear()

        def dram(name, shape, dt=F32):
            return nc.dram_tensor(name, shape, dt, kind="Internal").ap()

        ident = sb("ident", [P, P])
        ones = sb("ones", [P, P])
        below = sb("below", [P, P])
        iota = sb("iota", [P, P])
        own = sb("own", [P, 1])
        zeros16 = sb("zeros16", [P, BANK], BF16)
        tile_of = sb("tile_of", [P, G], I32)
        src_tl = sb("src_tl", [P, V], I32)
        idx1_tl = sb("idx1_tl", [P, V], I32)
        neg_tl = sb("neg_tl", [P, V])
        offs = sb("offs", [1, V], I32)
        mneg_f = sb("mneg_f", [P, G, P], BF16)
        mneg_b = sb("mneg_b", [P, G, P], BF16)
        goes_f = sb("goes_f", [H, G, P], BF16)
        goes_b = sb("goes_b", [H, G, P], BF16)
        cont = sb("cont", [P, G])
        rel_first = sb("rel_first", [P, G])
        inside = sb("inside", [P, V], BF16)
        first_dst = sb("first_dst", [P, 1], I32)
        runstart = sb("runstart", [P, NB], I32)
        in_scale = sb("in_scale", [P, NB])
        eps_s = sb("eps_s", [P, 1])
        xcur = sb("xcur", [P, NB, D])
        agg = sb("agg", [P, NB, AW])

        table0 = dram("table0", (NB * P, D))
        table1 = dram("table1", (NB * P * R, W1ROW))
        table2 = dram("table2", (NB * P, D))
        table3 = dram("table3", (NB * P, W3ROW))
        edges_d = dram("edges_d", (T, 3 * P), I32)
        offs_d = dram("offs_d", (V,), I32)
        key_d = dram("key_d", (VP + 2,))
        et_d = dram("et_d", (VP,))
        spread1 = dram("spread1", (VP + 1, R))
        spread3 = dram("spread3", (VP + 1, H))
        nodes1 = dram("nodes1", (NB * P, R))
        nodes3 = dram("nodes3", (NB * P, H))
        target_d = dram("target_d", (H, VP))
        we_d = dram("we_d", (EP * H,))

        def rows_of(flat):
            full = (G - 1) * P
            rest = E // P - full
            a = flat[0:full * P].rearrange("(g q c) -> q g c", q=P, c=P)
            b = flat[full * P:(full + rest) * P].rearrange("(q c) -> q c", c=P)
            return a, b, rest

        with ExitStack() as st:
            tsb, tps = fresh(nc, st)
            dst_r = tsb("dst_r", [P, G, P], I32)
            dst_t = tsb("dst_t", [P, G, P])
            pad = tsb("pad", [1, 3 * P], I32)
            edges_r = tsb("edges_r", [P, G, 3 * P], I32)
            src_f = tsb("src_f", [P, G, P])
            dst_f = dst_t
            et_f = tsb("et_f", [P, G, P])
            rel_f = tsb("rel_f", [P, G, P])
            valid = tsb("valid", [P, G, P])
            key = tsb("key", [P, G, P])
            prev = valid
            after = tsb("after", [P, G, P])
            prev_s = tsb("prev_s", [P, V])
            base_f = tsb("base_f", [P, G])
            base_i = tsb("base_i", [P, G], I32)
            number_i = tsb("number_i", [P, G], I32)
            number = tsb("number", [P, G])
            iota_v = tsb("iota_v", [P, V])
            iota_vi = edges_r[:].rearrange("p g x -> p (g x)")[:, 0:V]
            key_s = iota_v
            begun = tsb("begun", [P, 2, V], BF16)
            src_h = tsb("src_h", [P, T], I32)
            part_i = edges_r[:].rearrange("p g x -> p (g x)")[:, V:V + T]
            lo16 = tsb("lo16", [P, T], BF16)
            hi16 = tsb("hi16", [P, T], BF16)
            iota_h = tsb("iota_h", [P, P, HCH], BF16)
            lo_hot = tsb("lo_hot", [P, HSLOTS, P, HCH], BF16)
            hi_hot = tsb("hi_hot", [P, HSLOTS, NB, HCH], BF16)
            deg = tsb("deg", [P, NB])
            root = tsb("root", [P, NB])
            tile_f = tsb("tile_f", [P, G])
            block_f = tsb("block_f", [P, G])
            first_node = tsb("first_node", [P, G])
            blk = tsb("blk", [P, G])
            q = tsb("q", [P, G])
            off_f = tsb("off_f", [P, G])
            off_i = tsb("off_i", [P, G], I32)
            ends = tsb("ends", [1, 2])
            flag = tsb("flag", [P, 3, G])
            flag4 = tsb("flag4", [P, 2, G, H])
            iota_i = tsb("iota_i", [P, P], I32)
            own_i = tsb("own_i", [P, 1], I32)
            turned = tps("turned", [P, 4 * BANK])
            deg_ps = tps("deg_ps", [P, NB])
            begun_ps = tps("begun_ps", [P, G])
            ones16 = tsb("ones16", [P, 1], BF16)

            blank = sem("blank")
            loaded = sem("loaded")
            tiles_in = sem("tiles_in")
            edges_out = sem("edges_out")
            x_in = sem("x_in")
            consts = sem("consts")
            iota_ready = sem("iota_ready")
            zero_ready = sem("zero_ready")
            src_in = sem("src_in")
            hot_ready = sem("hot_ready")
            counted = sem("counted")
            deg_ready = sem("deg_ready")
            root_ready = sem("root_ready")
            xs_ready = sem("xs_ready")
            xs_out = sem("xs_out")
            chain = Count(sem("setup_chain"))
            parts_ready = sem("parts_ready")
            halves_ready = sem("halves_ready")
            visits_ready = sem("visits_ready")
            dst_ready = sem("dst_ready")
            begun_ready = sem("begun_ready")
            begun_used = sem("begun_used")
            edges_ready = sem("edges_ready")
            tile_ready = sem("tile_ready")
            edges_in = sem("edges_in")
            key_ready = sem("key_ready")
            key_out = sem("key_out")
            keys_in = sem("keys_in")
            rows_ready = sem("rows_ready")
            turn_done = sem("turn_done")
            turn_used = sem("turn_used")
            off_ready = sem("off_ready")
            off_out = sem("off_out")
            off_in = sem("off_in")
            et_out = sem("et_out")
            flags_ready = sem("flags_ready")
            flags_turned = sem("flags_turned")
            FULL = E // P
            REST = E % P
            SHARES = (0, 1, 4, 8, HITERS)

            with nc.Block() as block:
                @block.gpsimd
                def _(pool):
                    nc.gpsimd.memset(src_h[:, T - 1:T], N).then_inc(blank, 1)
                    nc.gpsimd.memset(pad[:, 0:2 * P], N).then_inc(blank, 1)
                    nc.gpsimd.memset(pad[:, 2 * P:3 * P], 0).then_inc(blank, 1)
                    nc.gpsimd.memset(dst_r[:], N).then_inc(blank, 1)
                    nc.gpsimd.memset(xcur[:], 0.0).then_inc(blank, 1)
                    nc.gpsimd.iota(iota_i[:], [[1, P]], base=0, channel_multiplier=0).then_inc(iota_ready, 1)
                    nc.gpsimd.iota(own_i[:], [[0, 1]], base=0, channel_multiplier=1).then_inc(iota_ready, 1)
                    nc.gpsimd.iota(number_i[:], [[P, G]], base=0, channel_multiplier=1).then_inc(iota_ready, 1)
                    nc.gpsimd.iota(iota_vi, [[1, V]], base=0, channel_multiplier=0).then_inc(iota_ready, 1)
                    nc.gpsimd.memset(ident[:], 0.0).then_inc(consts, 1)
                    nc.gpsimd.memset(ones[:], 1.0).then_inc(consts, 1)
                    nc.gpsimd.memset(below[:], 1.0).then_inc(consts, 1)
                    pool.wait_ge(consts, 3)
                    nc.gpsimd.affine_select(out=ident[:], in_=ident[:], compare_op=ALU.not_equal, fill=1.0,
                                            base=0, pattern=[[-1, P]], channel_multiplier=1).then_inc(consts, 1)
                    nc.gpsimd.affine_select(out=below[:], in_=below[:], compare_op=ALU.is_gt, fill=0.0,
                                            base=0, pattern=[[1, P]], channel_multiplier=-1).then_inc(consts, 1)
                    pool.wait_ge(edges_out, 16 * 9)
                    pool.wait_ge(tile_ready, 1)
                    for g in range(G):
                        pool.indirect_dma_start(edges_r[:, g], None, edges_d, bass.IndirectOffsetOnAxis(tile_of[:, g:g + 1], 0)).then_inc(edges_in, 16)

                @block.sync
                def _(sp):
                    sp.wait_ge(blank, 5)
                    a, b, rest = rows_of(dst)
                    sp.dma_start(dst_r[:, 0:a.shape[1], :], a).then_inc(loaded, 16)
                    sp.dma_start(dst_r[0:rest, a.shape[1], :], b).then_inc(loaded, 16)
                    sp.dma_start(dst_r[rest:rest + 1, a.shape[1], 0:REST], dst[E - REST:E].unsqueeze(0)).then_inc(loaded, 16)
                    sp.dma_start(src_h[:, 0:T - 1], src[0:P * (T - 1)].rearrange("(p j) -> p j", p=P)).then_inc(src_in, 16)
                    sp.dma_start(src_h[0:E - P * (T - 1), T - 1:T], src[P * (T - 1):E].unsqueeze(1)).then_inc(src_in, 16)
                    for n, flat in enumerate((src, dst, etype)):
                        sp.dma_start(edges_d[0:FULL, n * P:(n + 1) * P], flat[0:FULL * P].rearrange("(t c) -> t c", c=P)).then_inc(edges_out, 16)
                        sp.dma_start(edges_d[FULL:T, n * P:n * P + REST], flat[FULL * P:E].unsqueeze(0)).then_inc(edges_out, 16)
                        sp.dma_start(edges_d[FULL:T, n * P + REST:(n + 1) * P], pad[:, n * P + REST:(n + 1) * P]).then_inc(edges_out, 16)
                    sp.dma_start(xcur[:, 0:NB - 1, :], x[0:(NB - 1) * P, :].rearrange("(b p) f -> p b f", p=P)).then_inc(x_in, 16)
                    sp.dma_start(xcur[0:NLAST, NB - 1, :], x[(NB - 1) * P:N, :]).then_inc(x_in, 16)
                    sp.wait_ge(key_ready, 1)
                    sp.dma_start(key_d[1:VP + 1].rearrange("(g q c) -> q g c", q=P, c=P), key[:]).then_inc(key_out, 16)
                    sp.dma_start(key_d[0:1].unsqueeze(0), ends[:, 0:1]).then_inc(key_out, 16)
                    sp.dma_start(key_d[VP + 1:VP + 2].unsqueeze(0), ends[:, 1:2]).then_inc(key_out, 16)
                    sp.wait_ge(key_out, 48)
                    sp.wait_ge(rows_ready, 1)
                    sp.dma_start(prev[:], key_d[0:VP].rearrange("(g q c) -> q g c", q=P, c=P)).then_inc(keys_in, 16)
                    sp.dma_start(after[:], key_d[2:VP + 2].rearrange("(g q c) -> q g c", q=P, c=P)).then_inc(keys_in, 16)
                    sp.dma_start(key_s[:], key_d[1:VP + 1].rearrange("(p j) -> p j", p=P)).then_inc(keys_in, 16)
                    sp.dma_start(prev_s[:], key_d[0:VP].rearrange("(p j) -> p j", p=P)).then_inc(keys_in, 16)
                    sp.dma_start(et_d.rearrange("(g q c) -> q g c", q=P, c=P), et_f[:]).then_inc(et_out, 16)
                    sp.wait_ge(off_ready, 1)
                    sp.dma_start(offs_d.rearrange("(g q) -> q g", q=P), off_i[:], allow_slow_non_contiguous=True).then_inc(off_out, 16)
                    sp.wait_ge(off_out, 16)
                    sp.dma_start(offs[:], offs_d.unsqueeze(0)).then_inc(off_in, 16)
                    sp.wait_ge(off_in, 16)
                    sp.wait_ge(et_out, 16)
                    for n, (lo, hi) in enumerate(HALVES):
                        sp.wait_ge(xs_ready, n + 1)
                        sp.dma_start(node_rows(table0)[:, lo:hi], agg[:, lo:hi, 0:D]).then_inc(xs_out, 16)
                    sp.wait_ge(xs_out, 32)

                @block.vector
                def _(dve):
                    link = linked(dve, chain)
                    nc.vector.memset(zeros16[:], 0.0).then_inc(zero_ready, 1)
                    nc.vector.memset(ones16[:], 1.0).then_inc(zero_ready, 1)
                    link(nc.vector.memset(ends[:], -2.0))

                    def count(share):
                        def body(i, first):
                            for s in range(HSLOTS):
                                c = i * HSLOTS + s
                                if not first:
                                    dve.wait_ge(counted, c - HSLOTS + 1)
                                for hot, part, n in ((lo_hot, lo16, P), (hi_hot, hi16, NB)):
                                    nc.vector.tensor_tensor(
                                        hot[:, s], iota_h[:, 0:n],
                                        part[:, bass.ds(c * HCH, HCH)].unsqueeze(1).broadcast_to([P, n, HCH]),
                                        ALU.is_equal).then_inc(hot_ready, 1)

                        if share == 0:
                            for i in range(SHARES[1]):
                                body(i, i == 0)
                        else:
                            with dve.Fori(SHARES[share], SHARES[share + 1]) as i:
                                body(i, False)

                    dve.wait_ge(iota_ready, 3)
                    link(nc.vector.tensor_copy(iota[:], iota_i[:]))
                    link(nc.vector.tensor_copy(own[:], own_i[:]))
                    link(nc.vector.tensor_copy(number[:], number_i[:]))
                    dve.wait_ge(src_in, 32)
                    link(nc.vector.tensor_scalar(part_i, src_h[:], P - 1, None, ALU.bitwise_and))
                    nc.vector.tensor_scalar(src_h[:], src_h[:], 7, None, ALU.arith_shift_right).then_inc(parts_ready, 1)
                    dve.wait_ge(halves_ready, 3)
                    count(0)
                    dve.wait_ge(dst_ready, 1)
                    link(nc.vector.tensor_reduce(base_f[:], dst_t[:], AX, ALU.min))
                    link(nc.vector.tensor_copy(base_i[:], base_f[:]))
                    link(nc.vector.tensor_scalar(base_i[:], base_i[:], 7, None, ALU.arith_shift_right))
                    link(nc.vector.tensor_copy(base_f[:], base_i[:]))
                    link(nc.vector.tensor_tensor(base_f[:], base_f[:], number[:], ALU.add))
                    dve.wait_ge(visits_ready, 1)
                    for g in range(G):
                        if g >= 2:
                            dve.wait_ge(begun_used, g - 1)
                        nc.vector.tensor_scalar(begun[:, g % 2], iota_v[:], base_f[:, g:g + 1], None, ALU.is_ge).then_inc(begun_ready, 1)
                    dve.wait_ge(begun_used, G)
                    link(nc.vector.tensor_scalar(tile_f[:], begun_ps[:], -1.0, 0.0, ALU.add, ALU.max))
                    link(nc.vector.tensor_scalar(tile_f[:], tile_f[:], float(T - 1), None, ALU.min))
                    nc.vector.tensor_copy(tile_of[:], tile_f[:]).then_inc(tile_ready, 1)
                    link(nc.vector.tensor_tensor(block_f[:], number[:], tile_f[:], ALU.subtract))
                    link(nc.vector.tensor_scalar(first_node[:], block_f[:], float(P), None, ALU.mult))
                    link(nc.vector.tensor_scalar(blk[:], block_f[:], float(NB - 1), None, ALU.min))
                    link(nc.vector.tensor_scalar(off_f[:], blk[:], float(AW), None, ALU.mult))
                    for k in range(1, NG):
                        link(nc.vector.tensor_scalar(q[:], blk[:], float(BPB * k), float(BANK - BPB * AW), ALU.is_ge, ALU.mult))
                        link(nc.vector.tensor_tensor(off_f[:], off_f[:], q[:], ALU.add))
                    nc.vector.tensor_copy(off_i[:], off_f[:]).then_inc(off_ready, 1)
                    count(1)
                    dve.wait_ge(edges_ready, 3)
                    link(nc.vector.tensor_tensor(rel_f[:], dst_f[:], along(first_node[:], P), ALU.subtract))
                    link(nc.vector.tensor_copy(rel_first[:], rel_f[:, :, 0]))
                    link(nc.vector.tensor_scalar(valid[:], rel_f[:], 0.0, None, ALU.is_ge))
                    link(nc.vector.scalar_tensor_tensor(valid[:], rel_f[:], float(P), valid[:], ALU.is_lt, ALU.mult))
                    link(nc.vector.scalar_tensor_tensor(key[:], dst_f[:], 1.0, valid[:], ALU.add, ALU.mult))
                    nc.vector.tensor_scalar(key[:], key[:], -1.0, None, ALU.add).then_inc(key_ready, 1)
                    link(nc.vector.scalar_tensor_tensor(src_f[:], src_f[:], float(-N), valid[:], ALU.add, ALU.mult))
                    link(nc.vector.tensor_scalar(src_f[:], src_f[:], float(N), None, ALU.add))
                    nc.vector.scalar_tensor_tensor(dst_t[:], src_f[:], float(R), et_f[:], ALU.mult, ALU.add).then_inc(rows_ready, 1)
                    count(2)
                    dve.wait_ge(keys_in, 64)
                    link(nc.vector.tensor_tensor(inside[:], key_s[:], prev_s[:], ALU.is_equal))
                    link(nc.vector.tensor_scalar(first_dst[:], key_s[:, 0:1], 0.0, None, ALU.max))
                    for n, (other, mneg, edge) in enumerate(((prev, mneg_f[:], 0), (after, mneg_b[:, :, ::-1], P - 1))):
                        link(nc.vector.tensor_tensor(other[:], key[:], other[:], ALU.is_equal))
                        link(nc.vector.tensor_copy(flag[:, n], other[:, :, edge]))
                        link(nc.vector.tensor_scalar(mneg, other[:], 1.0, -LOW, ALU.subtract, ALU.mult))
                    link(nc.vector.tensor_copy(cont[:], flag[:, 0]))
                    link(nc.vector.tensor_tensor(flag[:, 2], key[:, :, 0], key[:, :, P - 1], ALU.is_equal))
                    for n in range(2):
                        link(nc.vector.tensor_tensor(flag[:, n], flag[:, n], flag[:, 2], ALU.mult))
                        link(nc.vector.tensor_scalar(flag[:, n], flag[:, n], 1.0, -LOW, ALU.subtract, ALU.mult))
                        nc.vector.tensor_copy(flag4[:, n], along(flag[:, n], H)).then_inc(flags_ready, 1)
                    count(3)
                    dve.wait_ge(counted, HSLOTS * HITERS)
                    nc.vector.tensor_scalar(deg[:], deg_ps[:], 1.0, None, ALU.max).then_inc(deg_ready, 1)
                    dve.wait_ge(root_ready, 1)
                    link(nc.vector.reciprocal(deg[:], root[:]))
                    dve.wait_ge(x_in, 32)
                    for lo, hi in HALVES:
                        nc.vector.tensor_tensor(agg[:, lo:hi, 0:D], xcur[:, lo:hi], along(deg[:, lo:hi], D), ALU.mult).then_inc(xs_ready, 1)

                @block.scalar
                def _(act):
                    act.wait_ge(iota_ready, 4)
                    nc.scalar.copy(iota_h[:], along(iota_i[:], HCH)).then_inc(halves_ready, 1)
                    act.wait_ge(parts_ready, 1)
                    nc.scalar.copy(lo16[:], part_i).then_inc(halves_ready, 1)
                    nc.scalar.copy(hi16[:], src_h[:]).then_inc(halves_ready, 1)
                    act.wait_ge(loaded, 48)
                    nc.scalar.copy(dst_t[:], dst_r[:]).then_inc(dst_ready, 1)
                    nc.scalar.copy(iota_v[:], iota_vi).then_inc(visits_ready, 1)
                    act.wait_ge(edges_in, 16 * G)
                    for n, part in ((1, dst_f), (0, src_f), (2, et_f)):
                        nc.scalar.copy(part[:], edges_r[:, :, n * P:(n + 1) * P]).then_inc(edges_ready, 1)
                    for n, (tl, sign) in enumerate(((src_tl, 1.0), (idx1_tl, 1.0), (neg_tl, -1.0))):
                        act.wait_ge(turn_done, n + 1)
                        nc.scalar.mul(tl[:], turned[:, 0:V], sign).then_inc(turn_used, 1)
                    for n, goes in enumerate((goes_f[:], goes_b[:, :, ::-1])):
                        act.wait_ge(flags_turned, n + 1)
                        nc.scalar.copy(goes, turned[0:H, 0:V].rearrange("h (g c) -> h g c", c=P)).then_inc(turn_used, 1)
                    act.wait_ge(deg_ready, 1)
                    nc.scalar.sqrt(root[:], deg[:]).then_inc(root_ready, 1)

                @block.tensor
                def _(pe):
                    pe.wait_ge(zero_ready, 2)
                    nc.tensor.matmul(deg_ps[:], zeros16[:, 0:P], zeros16[:, 0:NB], start=True, stop=True, skip_group_check=True)
                    nc.tensor.matmul(begun_ps[:], zeros16[:, 0:P], zeros16[:, 0:G], start=True, stop=True, skip_group_check=True)

                    def count(share):
                        def body(i):
                            for s in range(HSLOTS):
                                pe.wait_ge(hot_ready, 2 * (i * HSLOTS + s + 1))
                                for k in range(HCH):
                                    last = nc.tensor.matmul(deg_ps[:], lo_hot[:, s, :, k], hi_hot[:, s, :, k], start=False, stop=True,
                                                            skip_group_check=True)
                                last.then_inc(counted, 1)

                        if share == 0:
                            for i in range(SHARES[1]):
                                body(i)
                        else:
                            with pe.Fori(SHARES[share], SHARES[share + 1]) as i:
                                body(i)

                    count(0)
                    for g in range(G):
                        pe.wait_ge(begun_ready, g + 1)
                        for v in range(G):
                            last = nc.tensor.matmul(begun_ps[:, v:v + 1], begun[:, g % 2, v * P:(v + 1) * P], ones16[:], start=False, stop=True,
                                                    skip_group_check=True)
                        last.then_inc(begun_used, 1)
                    count(1)
                    pe.wait_ge(consts, 5)
                    pe.wait_ge(rows_ready, 1)
                    for n, rows in enumerate((src_f, dst_t, rel_f)):
                        if n >= 1:
                            pe.wait_ge(turn_used, n)
                        for g in range(G):
                            last = nc.tensor.transpose(turned[:, g * P:(g + 1) * P], rows[:, g, :], ident[:])
                        last.then_inc(turn_done, 1)
                    count(2)
                    pe.wait_ge(flags_ready, 2)
                    for n in range(2):
                        pe.wait_ge(turn_used, 3 + n)
                        for g in range(G):
                            last = nc.tensor.transpose(turned[0:H, g * P:(g + 1) * P], flag4[:, n, g], ident[:])
                        last.then_inc(flags_turned, 1)
                    count(3)


        serial = itertools.count()

        def held(engine, value):
            if isinstance(value, int):
                return value
            register = engine.alloc_register(f"held_{next(serial)}")
            engine.reg_mov(register, value)
            return engine.snap(register)

        def steps(engine, body):
            body(0, True)
            with engine.Fori(1, ITERS) as i:
                body(i, False)

        TOP = (NG - 1) * BANK + (BPB - 1) * AW

        def zero_sums(acc, summed):
            for b in range(NG):
                last = nc.tensor.matmul(acc[:, b * BANK:(b + 1) * BANK], zeros16[:, 0:P], zeros16[:], start=True, stop=True,
                                        skip_group_check=True)
            last.then_inc(summed, 1)

        def add_visit(acc, at, hot, row):
            return nc.tensor.matmul(acc[:, bass.ds(at, row.shape[-1])], hot, row, start=False, stop=True, skip_group_check=True)

        def keep_sums(dve, acc, summed, kept, width):
            dve.wait_ge(summed, V + 1)
            for b in range(NG):
                nc.vector.tensor_copy(agg[:, b * BPB:(b + 1) * BPB, 0:width],
                                      acc[:, b * BANK:b * BANK + BPB * AW].rearrange("p (b f) -> p b f", f=AW)[:, :, 0:width])\
                    .then_inc(kept, 1)
            dve.wait_ge(kept, NG)

        def edge_scores(tsb, tps):
            HALF_A = -(-UNITS // 2)
            half = (slice(0, HALF_A * UNIT * 2 * D), slice(HALF_A * UNIT * 2 * D, EC * D))
            at = [u * BODY // UNITS for u in range(UNITS)]
            W = UNIT * P
            C = UNIT * 2 * H
            feat = tsb("feat", [P, EC * D])
            feat_t = tsb("feat_t", [P, W])
            part = tsb("part", [P, UNITS * C])
            zero = tsb("zero", [P, V])
            we_s = tsb("we_s", [P, D])
            ae_s = tsb("ae_s", [P, D])
            ve = tsb("ve", [P, 2 * H])
            turn = tps("turn", [P, BANK])
            blank = sem("feat_blank")
            zeroed = sem("zeroed")
            weights_in = sem("weights_in")
            chain = Count(sem("ve_chain"))
            ve_ready = sem("ve_ready")
            feat_in = [sem("feat_in_a"), sem("feat_in_b")]
            turned = sem("feat_turned")
            unit_kept = sem("unit_kept")
            part_out = sem("part_out")
            attr = edge_attr.rearrange("(p c j) f -> c p (j f)", p=EQ, c=PIECES)
            scores = we_d[0:E * H].rearrange("(p c x) -> c p x", p=EQ, c=PIECES)

            def sync(sp):
                for n in range(2):
                    sp.dma_start(we_s[n * D:(n + 1) * D, :], we).then_inc(weights_in, 16)
                sp.dma_start(ae_s[:], ae.rearrange("h d -> (h d)").partition_broadcast(P)).then_inc(weights_in, 16)
                sp.wait_ge(blank, 2)
                for n in range(2):
                    sp.dma_start(feat[0:EQ, half[n]], attr[0][:, half[n]]).then_inc(feat_in[n], 16)
                sp.dma_start(we_d[E * H:EP * H].unsqueeze(0), zero[0:1, 0:(EP - E) * H]).then_inc(part_out, 16)
                for table, cols in ((spread1, R), (spread3, H)):
                    rows = table[0:VP, :].rearrange("(p j) r -> p (j r)", p=P)
                    for n in range(cols):
                        sp.dma_start(rows[:, n * V:(n + 1) * V], zero[:]).then_inc(zeroed, 16)
                with sp.Fori(0, PIECES - 1) as c:
                    sp.wait_ge(turned, c * UNITS + HALF_A)
                    sp.dma_start(feat[0:EQ, half[0]], attr[bass.ds(c + 1, 1)].rearrange("o p x -> (o p) x")[:, half[0]]).then_inc(feat_in[0], 16)
                    sp.wait_ge(turned, c * UNITS + UNITS)
                    sp.dma_start(feat[0:EQ, half[1]], attr[bass.ds(c + 1, 1)].rearrange("o p x -> (o p) x")[:, half[1]]).then_inc(feat_in[1], 16)
                    sp.wait_ge(unit_kept, c * (2 * UNITS) + 2 * (UNITS + 1) + 1)
                    sp.dma_start(scores[bass.ds(c, 1)].rearrange("o p x -> (o p) x"), part[0:EQ, :]).then_inc(part_out, 16)
                sp.wait_ge(unit_kept, 2 * (PIECES * UNITS + 1) + 1)
                sp.dma_start(scores[PIECES - 1], part[0:EQ, :]).then_inc(part_out, 16)
                sp.wait_ge(part_out, 16 * (PIECES + 1))
                sp.wait_ge(zeroed, 16 * (R + H))

            def vector_first(dve):
                link = linked(dve, chain)
                nc.vector.memset(zero[:], 0.0).then_inc(blank, 1)
                nc.vector.memset(feat[:], 0.0).then_inc(blank, 1)
                nc.vector.memset(feat_t[:], 0.0).then_inc(unit_kept, 1)
                link(nc.vector.memset(ve[:], 0.0))
                dve.wait_ge(weights_in, 48)
                link(nc.vector.tensor_tensor(we_s[:], we_s[:], ae_s[:], ALU.mult))
                for n in range(2):
                    rs = slice(n * D, (n + 1) * D)
                    nc.vector.reduce_sum(ve[rs, n * H:(n + 1) * H], we_s[rs].rearrange("p (h d) -> p h d", h=H), AX).then_inc(ve_ready, 1)

            def keep(before):
                nc.vector.tensor_copy(part[:, before * C:(before + 1) * C], turn[:, W:W + C]).then_inc(unit_kept, 1)

            def vector(dve, i):
                for u in range(UNITS):
                    dve.wait_ge(turned, (i - 1) * UNITS + u + 1)
                    nc.vector.tensor_copy(feat_t[:], turn[:, 0:W]).then_inc(unit_kept, 1)
                    if u == 1:
                        dve.wait_ge(part_out, i * 16)
                    keep((u - 1) % UNITS)

            def vector_last(dve):
                dve.wait_ge(turned, PIECES * UNITS + 1)
                nc.vector.tensor_copy(feat_t[:], turn[:, 0:W]).then_inc(unit_kept, 1)
                keep(UNITS - 1)

            def multiply(pe, m):
                want = held(pe, m * 2 + 1)
                pe.wait_ge(ve_ready, 2)
                pe.wait_ge(unit_kept, want)
                for pair in range(UNIT):
                    last = nc.tensor.matmul(turn[:, W + pair * 2 * H:W + (pair + 1) * 2 * H], feat_t[:, pair * P:(pair + 1) * P], ve[:],
                                            start=True, stop=True)
                return last

            def tensor(pe, i, n):
                if n not in at:
                    return
                u = at.index(n)
                multiply(pe, (i - 1) * UNITS + u)
                if u in (0, HALF_A):
                    want = held(pe, i * 16)
                    pe.wait_ge(ve_ready, 2)
                    pe.wait_ge(feat_in[0 if u == 0 else 1], want)
                for pair in range(u * UNIT, (u + 1) * UNIT):
                    last = nc.tensor.transpose(turn[:, (pair - u * UNIT) * P:(pair - u * UNIT + 1) * P], feat[:, pair * 2 * D:(pair + 1) * 2 * D], ident[:])
                last.then_inc(turned, 1)

            def tensor_last(pe):
                multiply(pe, PIECES * UNITS).then_inc(turned, 1)

            return Beside(sync=sync, vector_first=vector_first, vector=vector, vector_last=vector_last,
                                   tensor=tensor, tensor_last=tensor_last)

        def one_hots(act, neg, dist, hot, u, dist_ready, before, hot_ready):
            if not (isinstance(before, int) and before < 2):
                act.wait_ge(hot_ready, before - 1)
            for k in range(QUAD):
                nc.scalar.activation(dist[:, u, k], iota[:], ACT.Abs, bias=neg[:, k:k + 1]).then_inc(dist_ready, 1)
            act.wait_ge(dist_ready, before * QUAD + QUAD)
            nc.scalar.activation(hot[:, u * QUAD:(u + 1) * QUAD], dist[:, u], ACT.Relu, bias=ones[:, 0:1], scale=-1.0).then_inc(hot_ready, 1)

        def gather_sum(tag, table, beside=None):
            with ExitStack() as st:
                tsb, tps = fresh(nc, st)
                more = beside(tsb, tps) if beside else None
                rows = tsb(f"rows_{tag}", [P, SLOTS, CH, D + 1])
                idx_c = tsb(f"idx_c_{tag}", [P, SLOTS, CH], I32)
                neg_c = tsb(f"neg_c_{tag}", [P, SLOTS, CH])
                hot = tsb(f"hot_{tag}", [P, RING, P])
                dist = tsb(f"dist_{tag}", [P, 2, QUAD, P], BF16)
                acc = tps(f"acc_{tag}", [P, NG * BANK])
                chunk_ready = sem(f"chunk_ready_{tag}")
                gathered = [sem(f"gathered_{tag}_{s}") for s in range(SLOTS)]
                dist_ready = sem(f"dist_ready_{tag}")
                hot_ready = sem(f"hot_ready_{tag}")
                summed = sem(f"summed_{tag}")
                kept = sem(f"kept_{tag}")
                one = sem(f"one_{tag}")
                with nc.Block() as block:
                    @block.scalar
                    def _(act):
                        def columns(i, s, first):
                            c = i * SLOTS + s
                            if not first:
                                act.wait_ge(summed, 1 + i * BODY + (s + 1 - SLOTS) * CH)
                            nc.scalar.copy(idx_c[:, s], src_tl[:, bass.ds(c * CH, CH)]).then_inc(chunk_ready, 1)
                            nc.scalar.copy(neg_c[:, s], neg_tl[:, bass.ds(c * CH, CH)]).then_inc(chunk_ready, 1)

                        def hots(i, s, first):
                            act.wait_ge(chunk_ready, 2 * (i * SLOTS + s + 1))
                            for k in range(0, CH, QUAD):
                                n = s * CH + k
                                if not (first and n < RING):
                                    act.wait_ge(summed, 1 + i * BODY + n - RING + QUAD)
                                one_hots(act, neg_c[:, s, k:k + QUAD], dist, hot, n // QUAD % 2, dist_ready, i * (BODY // QUAD) + n // QUAD, hot_ready)

                        AHEAD = SLOTS - 1

                        def body(i, first):
                            for s in range(SLOTS):
                                columns(i, s, first)
                                if s >= AHEAD:
                                    hots(i, s - AHEAD, first)
                                elif not first:
                                    hots(i - 1, s - AHEAD + SLOTS, False)

                        body(0, True)
                        with act.Fori(1, ITERS) as i:
                            body(i, False)
                        for s in range(1, SLOTS):
                            hots(ITERS - 1, s, False)

                    @block.gpsimd
                    def _(pool):
                        def body(i, first):
                            for s in range(SLOTS):
                                want = held(pool, 2 * (i * SLOTS + s + 1))
                                pool.wait_ge(one, 1)
                                pool.wait_ge(chunk_ready, want)
                                for k in range(CH):
                                    pool.indirect_dma_start(rows[:, s, k, 0:D], None, table,
                                                            bass.IndirectOffsetOnAxis(idx_c[:, s, k:k + 1], 0)).then_inc(gathered[s], 16)

                        steps(pool, body)

                    @block.vector
                    def _(dve):
                        nc.vector.memset(rows[:, :, :, D:D + 1], 1.0).then_inc(one, 1)
                        if more:
                            more.vector_first(dve)

                            with dve.Fori(1, ITERS) as i:
                                more.vector(dve, i)
                            more.vector_last(dve)
                        keep_sums(dve, acc, summed, kept, D + 1)

                    @block.tensor
                    def _(pe):
                        zero_sums(acc, summed)
                        pe.wait_ge(one, 1)

                        def body(i, first):
                            for s in range(SLOTS):
                                _, at = nc.values_load_multi_w_load_instructions(
                                    offs[0:1, bass.ds((i * SLOTS + s) * CH, CH)], engines=PE_ONLY, min_val=0, max_val=TOP)
                                pe.wait_ge(gathered[s], 16 * CH * (i + 1))
                                for k in range(CH):
                                    n = s * CH + k
                                    if more and not first:
                                        more.tensor(pe, i, n)
                                    if k % QUAD == 0:
                                        pe.wait_ge(hot_ready, i * (BODY // QUAD) + n // QUAD + 1)
                                    add_visit(acc, at[k], hot[:, n % RING], rows[:, s, k, :]).then_inc(summed, 1)

                        steps(pe, body)
                        if more:
                            more.tensor_last(pe)

                    if more:
                        block.sync(more.sync)

        def attend(tag, table, idx_tl, row, width, score_at, heads, target, curve, before_first, edge_scores=None):
            sums = width if heads == 1 else heads * (HD + 1)
            part = sums // heads
            PIECE = 16
            with ExitStack() as st:
                tsb, tps = fresh(nc, st)
                rows = tsb(f"rows_{tag}", [P, 2, P, width])
                idx_c = tsb(f"idx_c_{tag}", [P, 2, P], I32)
                neg_c = tsb(f"neg_c_{tag}", [P, 2, P])
                hot = tsb(f"hot_{tag}", [P, RING, P])
                dist = tsb(f"dist_{tag}", [P, 2, QUAD, P], BF16)
                msg = tsb(f"msg_{tag}", [P, 2, PIECE, sums])
                prob = tsb(f"prob_{tag}", [P, heads, P])
                score = tsb(f"score_{tag}", [P, heads, P])
                local = tsb(f"local_{tag}", [P, heads, P])
                best = tsb(f"best_{tag}", [P, heads, P])
                best_b = tsb(f"best_b_{tag}", [P, heads, P])
                tail = tsb(f"tail_{tag}", [P, heads])
                carry = tsb(f"carry_{tag}", [P, 2, heads])
                tails = tsb(f"tails_{tag}", [heads, P])
                state = tsb(f"state_{tag}", [heads, P])
                before = tsb(f"before_{tag}", [heads, P])
                so_far = tsb(f"so_far_{tag}", [heads, 1])
                rise = tsb(f"rise_{tag}", [P, heads + 1])
                scale = tsb(f"scale_{tag}", [P, heads + 1])
                acc = tps(f"acc_{tag}", [P, NG * BANK])
                work = tps(f"work_{tag}", [P, BANK])
                if edge_scores is not None:
                    tile_c = tsb(f"tile_c_{tag}", [P, 2, 1], I32)
                    edge_c = tsb(f"edge_c_{tag}", [P, 2, P * heads])
                    edge_in = [sem(f"edge_in_{tag}_{s}") for s in range(2)]
                COLUMNS = 2 if edge_scores is None else 3
                first_part = before_first(tsb, tps)
                chain_sem = sem(f"chain_{tag}")
                chunk_ready = sem(f"chunk_ready_{tag}")
                gathered = [sem(f"gathered_{tag}_{s}") for s in range(2)]
                gathered_last = sem(f"gathered_last_{tag}")
                scores_done = sem(f"scores_done_{tag}")
                tails_ready = sem(f"tails_ready_{tag}")
                tails_done = sem(f"tails_done_{tag}")
                before_ready = sem(f"before_ready_{tag}")
                before_done = sem(f"before_done_{tag}")
                rise_ready = sem(f"rise_ready_{tag}")
                rise_spread = sem(f"rise_spread_{tag}")
                rise_done = sem(f"rise_done_{tag}")
                diff_ready = sem(f"diff_ready_{tag}")
                exp_ready = sem(f"exp_ready_{tag}")
                factor_ready = sem(f"factor_ready_{tag}")
                prob_done = sem(f"prob_done_{tag}")
                scaled = sem(f"scaled_{tag}")
                msg_ready = sem(f"msg_ready_{tag}")
                dist_ready = sem(f"dist_ready_{tag}")
                hot_ready = sem(f"hot_ready_{tag}")
                summed = sem(f"summed_{tag}")
                kept = sem(f"kept_{tag}")
                one = sem(f"one_{tag}")

                HALF = P // 2

                def groups(engine, body):
                    body(0, 0, 0, True)
                    with engine.Fori(0, G // 2 - 1) as j:
                        body(1 + 2 * j, 1, j, False)
                        body(2 + 2 * j, 0, j + 1, False)
                    body(G - 2, 1, G // 2 - 1, False)
                    body(G - 1, 0, G // 2, False, G - 1, 0, HALF)
                    body(G - 1, 0, G // 2, False, G, HALF, P)

                with nc.Block() as block:
                    @block.scalar
                    def _(act):
                        def columns(g, u):
                            nc.scalar.copy(idx_c[:, u], idx_tl[:, bass.ds(g * P, P)]).then_inc(chunk_ready, 1)
                            nc.scalar.copy(neg_c[:, u], neg_tl[:, bass.ds(g * P, P)]).then_inc(chunk_ready, 1)
                            if edge_scores is not None:
                                nc.scalar.copy(tile_c[:, u], tile_of[:, bass.ds(g, 1)]).then_inc(chunk_ready, 1)

                        def exps(g, first):
                            act.wait_ge(diff_ready, g + 1)
                            nc.scalar.activation(score[:], score[:], ACT.Exp).then_inc(exp_ready, 1)
                            if not first:
                                act.wait_ge(rise_done, g)
                                nc.scalar.activation(scale[:, 0:heads], scale[:, 0:heads], ACT.Exp).then_inc(factor_ready, 1)

                        def body(g, u, uses, first, last_group=False):
                            if first:
                                columns(0, 0)
                                columns(1, 1)
                            else:
                                act.wait_ge(summed, 1 + P * g)
                                columns(g + 1, 1 - u)
                            exps(g, first)
                            if not (isinstance(g, int) and g >= G - 2):
                                hots(g, u, first)

                        def hots(g, u, first):
                            for k in range(0, P, QUAD):
                                if not (first and k < RING):
                                    act.wait_ge(summed, 1 + g * P + k - RING + QUAD)
                                one_hots(act, neg_c[:, u, k:k + QUAD], dist, hot, k // QUAD % 2, dist_ready, g * (P // QUAD) + k // QUAD, hot_ready)

                        body(0, 0, 0, True)
                        with act.Fori(0, G // 2 - 1) as j:
                            body(1 + 2 * j, 1, j, False)
                            body(2 + 2 * j, 0, j + 1, False)
                        body(G - 2, 1, G // 2 - 1, False)
                        exps(G - 1, False)
                        exps(G, False)

                    @block.gpsimd
                    def _(pool):
                        def body(g, u, uses, first, turn=None, q0=0, q1=P):
                            if q0 > 0:
                                for k in range(q0, q1):
                                    pool.indirect_dma_start(rows[:, u, k, 0:row], None, table,
                                                            bass.IndirectOffsetOnAxis(idx_c[:, u, k:k + 1], 0)).then_inc(gathered_last, 16)
                                return
                            want = held(pool, COLUMNS * (g + 1))
                            pool.wait_ge(one, 1)
                            pool.wait_ge(chunk_ready, want)
                            if edge_scores is not None:
                                pool.indirect_dma_start(edge_c[:, u], None, edge_scores.rearrange("(t x) -> t x", x=P * heads),
                                                        bass.IndirectOffsetOnAxis(tile_c[:, u], 0)).then_inc(edge_in[u], 16)
                            for k in range(q0, q1):
                                pool.indirect_dma_start(rows[:, u, k, 0:row], None, table,
                                                        bass.IndirectOffsetOnAxis(idx_c[:, u, k:k + 1], 0)).then_inc(gathered[u], 16)

                        first_part.pool(pool)
                        groups(pool, body)

                    block.sync(first_part.sync)

                    @block.vector
                    def _(dve):
                        if width > row:
                            nc.vector.memset(rows[:, :, :, row:width], 1.0).then_inc(one, 1)
                        else:
                            nc.vector.memset(tail[:], 0.0).then_inc(one, 1)
                        first_part.vector(dve)
                        LINKS = 14 + COLUMNS + 4 * heads

                        def body(g, u, uses, first, turn=None, q0=0, q1=P):
                            done = [0]
                            late = isinstance(g, int) and g >= G - 2
                            turn = g if turn is None else turn

                            def link(ins):
                                done[0] += 1
                                ins.then_inc(chain_sem, 1)
                                dve.wait_ge(chain_sem, turn * LINKS + done[0])

                            def way(n, mneg, goes, what, into, flip, end):
                                v = (lambda a: a[:, ::-1]) if flip else (lambda a: a)
                                m = mneg[:, bass.ds(g, 1), :].rearrange("p o c -> p (o c)")
                                go = goes[0:heads, bass.ds(g, 1), P - q1 if flip else q0:P - q0 if flip else q1].rearrange("p o c -> p (o c)")
                                for h in range(heads):
                                    link(nc.vector.tensor_tensor_scan(v(local[:, h]), m, v(what[:, h]), LOW, ALU.add, ALU.max))
                                nc.vector.tensor_copy(tail[:], local[:, :, end]).then_inc(tails_ready, 1)
                                dve.wait_ge(tails_done, 2 * turn + n + 1)
                                link(nc.vector.tensor_copy(tails[:], work[0:heads, 0:P]))
                                start = LOW if flip or first else so_far[:, 0:1]
                                link(nc.vector.tensor_tensor_scan(v(state[:, q0:q1]), go, v(tails[:, q0:q1]), start, ALU.add, ALU.max))
                                if flip:
                                    link(nc.vector.memset(before[:, q1 - 1:q1], LOW))
                                    nc.vector.tensor_copy(before[:, q0:q1 - 1], state[:, q0 + 1:q1]).then_inc(before_ready, 1)
                                else:
                                    if first:
                                        link(nc.vector.memset(before[:, 0:1], LOW))
                                    else:
                                        link(nc.vector.tensor_copy(before[:, q0:q0 + 1], so_far[:]))
                                    link(nc.vector.tensor_copy(so_far[:], state[:, q1 - 1:q1]))
                                    nc.vector.tensor_copy(before[:, q0 + 1:q1], state[:, q0:q1 - 1]).then_inc(before_ready, 1)
                                dve.wait_ge(before_done, 2 * turn + n + 1)
                                link(nc.vector.tensor_copy(carry[:, n], work[:, 0:heads]))
                                for h in range(heads):
                                    link(nc.vector.tensor_tensor_scan(v(into[:, h]), m, v(what[:, h]), carry[:, n, h:h + 1], ALU.add, ALU.max))

                            dve.wait_ge(scores_done, turn + 1)
                            link(nc.vector.tensor_tensor(score[:], work[:, 0:heads * P].rearrange("p (h c) -> p h c", h=heads),
                                                         target[:, :, bass.ds(g * P, P)], ALU.add))
                            if edge_scores is not None:
                                dve.wait_ge(edge_in[u], 16 * (uses + 1))
                                link(nc.vector.tensor_tensor(score[:], score[:], edge_c[:, u].rearrange("p (c h) -> p h c", h=heads), ALU.add))
                            link(curve(score[:]))
                            way(0, mneg_f, goes_f, score, best, False, P - 1)
                            way(1, mneg_b, goes_b, best, best_b, True, 0)
                            nc.vector.tensor_tensor(score[:], score[:], best_b[:], ALU.subtract).then_inc(diff_ready, 1)
                            dve.wait_ge(prob_done, turn + 1)
                            link(nc.vector.tensor_copy(prob[:], work[:, 0:heads * P].rearrange("p (h c) -> p h c", h=heads)))
                            if not first:
                                f = slice(q0, q0 + 1)
                                link(nc.vector.tensor_tensor(rise[f, 0:heads], carry[f, 0], best_b[f, :, 0], ALU.subtract))
                                link(nc.vector.tensor_scalar(rise[f, 0:heads], rise[f, 0:heads], cont[f, bass.ds(g, 1)], None, ALU.mult))
                                nc.vector.tensor_copy(rise[f, heads:heads + 1], rel_first[f, bass.ds(g, 1)]).then_inc(rise_ready, 1)
                                dve.wait_ge(rise_spread, turn)
                                link(nc.vector.tensor_copy(scale[:], work[:, 0:heads + 1]))
                                link(nc.vector.tensor_tensor(scale[:, heads:heads + 1], scale[:, heads:heads + 1], own[:], ALU.is_equal))
                                nc.vector.tensor_scalar(scale[:, 0:heads], scale[:, 0:heads], scale[:, heads:heads + 1], None, ALU.mult)\
                                    .then_inc(rise_done, 1)
                                dve.wait_ge(factor_ready, turn)
                                dve.wait_ge(summed, 1 + P * g + q0)
                                at = dve.value_load(offs[0:1, bass.ds(g * P + q0, 1)], min_val=0, max_val=TOP)
                                for h in range(heads):
                                    here = acc[:, bass.ds(at + h * part, part)]
                                    nc.vector.tensor_scalar(here, here, scale[:, h:h + 1], None, ALU.mult).then_inc(scaled, 1)
                            if first:
                                for _ in range(LINKS - done[0]):
                                    link(nc.vector.memset(tail[:], 0.0))
                            assert done[0] == LINKS

                            for k in range(q0, q1, PIECE):
                                m = k // PIECE % 2
                                if not (first and k < 2 * PIECE):
                                    dve.wait_ge(summed, 1 + g * P + k - PIECE)
                                nc.vector.tensor_tensor(
                                    msg[:, m].rearrange("p k (h d) -> p k h d", h=heads),
                                    rows[:, u, k:k + PIECE, 0:sums].rearrange("p k (h d) -> p k h d", h=heads),
                                    prob[:, :, k:k + PIECE].rearrange("p h k -> p k h").unsqueeze(3).broadcast_to([P, PIECE, heads, part]),
                                    ALU.mult).then_inc(msg_ready, 1)
                                if late:
                                    for n in range(k, k + PIECE):
                                        if n % QUAD == 0:
                                            dve.wait_ge(summed, 1 + g * P + n - RING + QUAD)
                                        ins = nc.vector.tensor_scalar(hot[:, n % RING], iota[:], neg_c[:, u, n:n + 1], 0.0, ALU.add, ALU.is_equal)
                                        if n % QUAD == QUAD - 1:
                                            ins.then_inc(hot_ready, 1)

                        groups(dve, body)
                        keep_sums(dve, acc, summed, kept, sums)

                    @block.tensor
                    def _(pe):
                        zero_sums(acc, summed)
                        pe.wait_ge(one, 1)

                        def offsets(g, lo):
                            return nc.values_load_multi_w_load_instructions(
                                offs[0:1, bass.ds(g * P + lo, CH)], engines=PE_ONLY, min_val=0, max_val=TOP)[1]

                        def body(g, u, uses, first, turn=None, q0=0, q1=P):
                            turn = g if turn is None else turn
                            places = {lo: offsets(g, lo) for lo in range(q0, q0 + EARLY * CH, CH)}
                            if q0 > 0:
                                pe.wait_ge(gathered_last, 16 * (q1 - q0))
                            else:
                                pe.wait_ge(gathered[u], 16 * P * uses + 16 * q1)
                            for h in range(heads):
                                last = nc.tensor.transpose(work[0:q1, h * P:(h + 1) * P], rows[:, u, 0:q1, score_at + h], ident[:])
                            last.then_inc(scores_done, 1)
                            for n in range(2):
                                want = held(pe, 2 * turn + n + 1)
                                pe.wait_ge(one, 1)
                                pe.wait_ge(tails_ready, want)
                                nc.tensor.transpose(work[0:heads, 0:P], tail[:], ident[:]).then_inc(tails_done, 1)
                                pe.wait_ge(one, 1)
                                pe.wait_ge(before_ready, want)
                                nc.tensor.transpose(work[:, 0:heads], before[:], ident[0:heads, 0:heads]).then_inc(before_done, 1)
                            pe.wait_ge(exp_ready, turn + 1)
                            for h in range(heads):
                                last = nc.tensor.transpose(work[:, h * P:(h + 1) * P], score[:, h], ident[:])
                            last.then_inc(prob_done, 1)
                            if not first:
                                want = held(pe, turn)
                                pe.wait_ge(one, 1)
                                pe.wait_ge(rise_ready, want)
                                nc.tensor.matmul(work[:, 0:heads + 1], ones[q0:q0 + 1, :], rise[q0:q0 + 1, :], start=True, stop=True).then_inc(rise_spread, 1)
                                pe.wait_ge(scaled, heads * turn)
                            for lo in range(q0, q1, CH):
                                at = places[lo] if lo in places else offsets(g, lo)
                                pe.wait_ge(msg_ready, g * (P // PIECE) + lo // PIECE + 1)
                                for k in range(lo, lo + CH):
                                    if k % QUAD == 0:
                                        pe.wait_ge(hot_ready, g * (P // QUAD) + k // QUAD + 1)
                                    add_visit(acc, at[k - lo], hot[:, k % RING], msg[:, (k // PIECE) % 2, k % PIECE, :]).then_inc(summed, 1)

                        groups(pe, body)

        def normalise(tag, y, tmp, small, result_out=None):
            chain = Count(sem(f"norm_chain_{tag}"))
            var_ready = sem(f"var_ready_{tag}")
            std_ready = sem(f"std_ready_{tag}")
            x_ready = sem(f"x_ready_{tag}")
            x_out = sem(f"x_out_{tag}")
            mean, var, std, rstd = (small[:, n] for n in range(4))
            with nc.Block() as block:
                @block.vector
                def _(dve):
                    link = linked(dve, chain)
                    link(nc.vector.reduce_sum(mean, y[:], AX))
                    link(nc.vector.tensor_scalar(mean, mean, 1.0 / D, None, ALU.mult))
                    link(nc.vector.tensor_tensor(y[:], y[:], along(mean, D), ALU.subtract))
                    link(nc.vector.tensor_tensor(tmp[:], y[:], y[:], ALU.mult))
                    link(nc.vector.reduce_sum(var, tmp[:], AX))
                    nc.vector.tensor_scalar(var, var, 1.0 / D, EPS, ALU.mult, ALU.add).then_inc(var_ready, 1)
                    dve.wait_ge(std_ready, 1)
                    link(nc.vector.reciprocal(rstd, std))
                    nc.vector.tensor_tensor(xcur[:], y[:], along(rstd, D), ALU.mult).then_inc(x_ready, 1)

                @block.scalar
                def _(act):
                    act.wait_ge(var_ready, 1)
                    nc.scalar.sqrt(std, var).then_inc(std_ready, 1)

                @block.sync
                def _(sp):
                    if result_out is not None:
                        sp.wait_ge(x_ready, 1)
                        n = result_out(sp, x_out)
                        sp.wait_ge(x_out, n)

        def node_layer(tag, w_in, b_in, w_out, b_out, hidden, func, inputs, cols, split, nodes, edges, emit, make_weights):
            with ExitStack() as st:
                tsb, tps = fresh(nc, st)
                wa = tsb(f"wa_{tag}", [D, hidden])
                ba = tsb(f"ba_{tag}", [hidden, 1])
                wb = tsb(f"wb_{tag}", [hidden, D])
                bb = tsb(f"bb_{tag}", [P, D])
                wsum = tsb(f"wsum_{tag}", [D, cols])
                h = tsb(f"h_{tag}", [P, BPB, D])
                h_t = tsb(f"h_t_{tag}", [D, BPB * P])
                g_t = tsb(f"g_t_{tag}", [hidden, BPB * P])
                y = tsb(f"y_{tag}", [P, BPB, D])
                square = tsb(f"square_{tag}", [P, BPB, D])
                xg = tsb(f"xg_{tag}", [P, BPB, D])
                x_t = tsb(f"x_t_{tag}", [D, BPB * P])
                small = tsb(f"small_{tag}", [P, 4, BPB])
                mean, var, std, rstd = (small[:, n] for n in range(4))
                stage, node = emit["buffers"](tsb)
                t_ps = tps(f"t_ps_{tag}", [D, 2 * BANK])
                g_ps = tps(f"g_ps_{tag}", [hidden, 2 * BANK])
                o_ps = tps(f"o_ps_{tag}", [P, BPB * D])
                z_ps = tps(f"z_ps_{tag}", [P, 3, BANK])
                loaded = sem(f"weights_{tag}")
                proj_in = sem(f"proj_in_{tag}")
                w_chain = Count(sem(f"w_chain_{tag}"))
                chain_sem = sem(f"chain_{tag}")
                w_ready = sem(f"w_ready_{tag}")
                h_ready = sem(f"h_ready_{tag}")
                t_done = sem(f"t_done_{tag}")
                ht_ready = sem(f"ht_ready_{tag}")
                g_done = sem(f"g_done_{tag}")
                gt_ready = sem(f"gt_ready_{tag}")
                o_done = sem(f"o_done_{tag}")
                var_ready = sem(f"var_ready_{tag}")
                std_ready = sem(f"std_ready_{tag}")
                x_ready = sem(f"x_ready_{tag}")
                tx_done = sem(f"tx_done_{tag}")
                xt_ready = sem(f"xt_ready_{tag}")
                z_done = sem(f"z_done_{tag}")
                z_kept = sem(f"z_kept_{tag}")
                staged = sem(f"staged_{tag}")
                nodes_out = sem(f"nodes_out_{tag}")
                scattered = sem(f"scattered_{tag}")
                S = len(split)
                PRODUCTS = BPB * S

                def groups(engine, body):
                    body(0, True, False)
                    with engine.Fori(1, NG - 1) as g:
                        body(g, False, False)
                    body(NG - 1, False, True)

                with nc.Block() as block:
                    @block.sync
                    def _(sp):
                        sp.dma_start(wa[:], w_in).then_inc(loaded, 16)
                        sp.dma_start(ba[:], b_in.unsqueeze(1)).then_inc(loaded, 16)
                        sp.dma_start(wb[:], w_out).then_inc(loaded, 16)
                        sp.dma_start(bb[:], b_out.partition_broadcast(P)).then_inc(loaded, 16)
                        make_weights["load"](sp, proj_in)

                        def body(g, first, last):
                            for b in range(BPB):
                                sp.wait_ge(z_kept, g * PRODUCTS + (b + 1) * S)
                                emit["store"](sp, stage, g * BPB + b, b).then_inc(staged, 16)

                        groups(sp, body)
                        sp.dma_start(node_rows(nodes), node[:]).then_inc(nodes_out, 16)
                        sp.wait_ge(staged, 16 * NB)
                        sp.wait_ge(nodes_out, 16)

                    @block.gpsimd
                    def _(pool):
                        for b in range(NB):
                            k = P if b < NB - 1 else NLAST
                            pool.wait_ge(z_kept, (b + 1) * S)
                            pool.indirect_dma_start(edges, bass.IndirectOffsetOnAxis(runstart[0:k, b:b + 1], 0), node[0:k, b, :], None)\
                                .then_inc(scattered, 16)
                        pool.wait_ge(scattered, 16 * NB)

                    @block.vector
                    def _(dve):
                        def turn(g):
                            dve.wait_ge(t_done, g + 1)
                            nc.vector.tensor_copy(h_t[:], t_ps[:, 0:BPB * P]).then_inc(ht_ready, 1)

                        LINKS = 9

                        def body(g, first, last):
                            done = [0]

                            def link(ins):
                                done[0] += 1
                                ins.then_inc(chain_sem, 1)
                                dve.wait_ge(chain_sem, g * LINKS + done[0])

                            here = bass.ds(g * BPB, BPB)
                            if not last:
                                inputs(h, g + 1).then_inc(h_ready, 1)
                                turn(g + 1)
                            dve.wait_ge(o_done, g + 1)
                            link(nc.vector.tensor_tensor(y[:], o_ps[:].rearrange("p (b f) -> p b f", f=D), xcur[:, here, :], ALU.add))
                            link(nc.vector.tensor_tensor(y[:], y[:], bb[:].unsqueeze(1).broadcast_to([P, BPB, D]), ALU.add))
                            link(nc.vector.reduce_sum(mean, y[:], AX))
                            link(nc.vector.tensor_scalar(mean, mean, 1.0 / D, None, ALU.mult))
                            link(nc.vector.tensor_tensor(y[:], y[:], along(mean, D), ALU.subtract))
                            link(nc.vector.tensor_tensor(square[:], y[:], y[:], ALU.mult))
                            link(nc.vector.reduce_sum(var, square[:], AX))
                            nc.vector.tensor_scalar(var, var, 1.0 / D, EPS, ALU.mult, ALU.add).then_inc(var_ready, 1)
                            dve.wait_ge(std_ready, g + 1)
                            link(nc.vector.reciprocal(rstd, std))
                            nc.vector.tensor_tensor(xg[:], y[:], along(rstd, D), ALU.mult).then_inc(x_ready, 1)
                            link(nc.vector.tensor_tensor(xcur[:, here, :], y[:], along(rstd, D), ALU.mult))
                            assert done[0] == LINKS
                            dve.wait_ge(tx_done, g + 1)
                            nc.vector.tensor_copy(x_t[:], t_ps[:, 0:BPB * P]).then_inc(xt_ready, 1)

                        inputs(h, 0).then_inc(h_ready, 1)
                        turn(0)
                        emit["ones"](linked(dve, w_chain), stage)
                        make_weights["compute"](dve, linked(dve, w_chain), proj_in, tsb, wsum).then_inc(w_ready, 1)
                        dve.wait_ge(loaded, 64)
                        groups(dve, body)

                    @block.scalar
                    def _(act):
                        def keep(g, ms, first):
                            for m in ms:
                                if m == 0 and not first:
                                    act.wait_ge(staged, g * (16 * BPB))
                                act.wait_ge(z_done, g * PRODUCTS + m + 1)
                                emit["keep"](z_ps[:, m % 3], m % S, stage, node, g * BPB + m // S, m // S).then_inc(z_kept, 1)

                        FIRST_HALF = range(0, PRODUCTS // 2)
                        SECOND_HALF = range(PRODUCTS // 2, PRODUCTS)

                        def body(g, first, last):
                            act.wait_ge(g_done, g + 1)
                            nc.scalar.activation(g_t[:], g_ps[:, 0:BPB * P], func, bias=ba[:, 0:1]).then_inc(gt_ready, 1)
                            if not first:
                                keep(g - 1, FIRST_HALF, second(g))
                            act.wait_ge(var_ready, g + 1)
                            nc.scalar.sqrt(std, var).then_inc(std_ready, 1)
                            if not first:
                                keep(g - 1, SECOND_HALF, second(g))

                        def second(g):
                            return isinstance(g, int) and g == 1

                        act.wait_ge(loaded, 64)
                        act.wait_ge(w_ready, 1)
                        body(0, True, False)
                        body(1, False, False)
                        with act.Fori(2, NG) as g:
                            body(g, False, False)
                        keep(NG - 1, FIRST_HALF, False)
                        keep(NG - 1, SECOND_HALF, False)

                    @block.tensor
                    def _(pe):
                        def turn(g):
                            want = held(pe, g + 1)
                            pe.wait_ge(loaded, 64)
                            pe.wait_ge(h_ready, want)
                            if not (isinstance(g, int) and g <= 1):
                                pe.wait_ge(xt_ready, g - 1)
                            for b in range(BPB):
                                last = nc.tensor.transpose(t_ps[:, b * P:(b + 1) * P], h[:, b], ident[:])
                            last.then_inc(t_done, 1)

                        def project(g, first):
                            want = held(pe, g + 1)
                            pe.wait_ge(w_ready, 1)
                            pe.wait_ge(xt_ready, want)
                            for m in range(PRODUCTS):
                                if m >= 3:
                                    pe.wait_ge(z_kept, g * PRODUCTS + m - 2)
                                elif not first:
                                    pe.wait_ge(z_kept, g * PRODUCTS)
                                lo, hi = split[m % S]
                                b = m // S
                                nc.tensor.matmul(z_ps[:, m % 3, 0:hi - lo], x_t[:, b * P:(b + 1) * P], wsum[:, lo:hi], start=True, stop=True)\
                                    .then_inc(z_done, 1)

                        def body(g, first, last):
                            want = held(pe, g + 1)
                            pe.wait_ge(loaded, 64)
                            pe.wait_ge(ht_ready, want)
                            for lo, hi in ((0, BANK), (BANK, BPB * P)):
                                ins = nc.tensor.matmul(g_ps[:, lo:hi], wa[:], h_t[:, lo:hi], start=True, stop=True)
                            ins.then_inc(g_done, 1)
                            if not last:
                                turn(g + 1)
                            want = held(pe, g + 1)
                            pe.wait_ge(loaded, 64)
                            pe.wait_ge(gt_ready, want)
                            for b in range(BPB):
                                ins = nc.tensor.matmul(o_ps[:, b * D:(b + 1) * D], g_t[:, b * P:(b + 1) * P], wb[:], start=True, stop=True)
                            ins.then_inc(o_done, 1)
                            if not first:
                                project(g - 1, isinstance(g, int) and g == 1)
                            want = held(pe, g + 1)
                            pe.wait_ge(loaded, 64)
                            pe.wait_ge(x_ready, want)
                            if not last:
                                pe.wait_ge(ht_ready, g + 2)
                            for b in range(BPB):
                                ins = nc.tensor.transpose(t_ps[:, b * P:(b + 1) * P], xg[:, b], ident[:])
                            ins.then_inc(tx_done, 1)

                        turn(0)
                        body(0, True, False)
                        body(1, False, False)
                        with pe.Fori(2, NG - 1) as g:
                            body(g, False, False)
                        body(NG - 1, False, True)
                        project(NG - 1, False)

        def target_rows(tag, cols, heads, nodes, edges, target, parts, by_relation):
            def make(tsb, tps):
                W = V // parts
                starts = tsb(f"starts_{tag}", [P, W, cols])
                first = tsb(f"first_{tag}", [P, cols])
                part = tsb(f"part_{tag}", [P, heads, W])
                et_s = tsb(f"et_s_{tag}", [P, W]) if by_relation else None
                pick = tsb(f"pick_{tag}", [P, W]) if by_relation else None
                first_in = sem(f"first_in_{tag}")
                starts_in = sem(f"starts_in_{tag}")
                part_ready = sem(f"part_ready_{tag}")
                part_out = sem(f"part_out_{tag}")
                target_in = sem(f"target_in_{tag}")
                chain = Count(sem(f"spread_chain_{tag}"))
                LOADS = 2 if by_relation else 1
                places = edges[0:VP, :].rearrange("(p j) r -> p j r", p=P)
                types = et_d.rearrange("(p j) -> p j", p=P)
                out_places = target_d[0:heads].rearrange("h (p j) -> p h j", p=P)

                def sync(sp):
                    for k in range(parts):
                        at = slice(k * W, (k + 1) * W)
                        if k >= 1:
                            sp.wait_ge(part_ready, k)
                        sp.dma_start(starts[:], places[:, at, :]).then_inc(starts_in, 16)
                        if by_relation:
                            sp.dma_start(et_s[:], types[:, at]).then_inc(starts_in, 16)
                        if k >= 1:
                            sp.dma_start(out_places[:, :, (k - 1) * W:k * W], part[:]).then_inc(part_out, 16)
                    sp.wait_ge(part_ready, parts)
                    sp.dma_start(out_places[:, :, (parts - 1) * W:V], part[:]).then_inc(part_out, 16)
                    sp.wait_ge(part_out, 16 * parts)
                    for h in range(heads):
                        sp.dma_start(target[:, h].rearrange("q (g c) -> q g c", c=P), target_d[h].rearrange("(g q c) -> q g c", q=P, c=P)).then_inc(target_in, 16)

                def pool(pool):
                    pool.indirect_dma_start(first[:], None, nodes, bass.IndirectOffsetOnAxis(first_dst[:, 0:1], 0)).then_inc(first_in, 16)

                def vector(dve):
                    link = linked(dve, chain)
                    dve.wait_ge(first_in, 16)
                    for k in range(parts):
                        dve.wait_ge(starts_in, 16 * LOADS * (k + 1))
                        if k >= 1:
                            dve.wait_ge(part_out, 16 * k)
                        for r in range(cols):
                            spread = starts[:, :, r] if by_relation else part[:, r]
                            link(nc.vector.tensor_tensor_scan(spread, inside[:, k * W:(k + 1) * W], starts[:, :, r], first[:, r:r + 1], ALU.mult, ALU.add))
                            last = nc.vector.tensor_copy(first[:, r:r + 1], spread[:, W - 1:W])
                            if by_relation or r < cols - 1:
                                link(last)
                        if by_relation:
                            link(nc.vector.scalar_tensor_tensor(part[:, 0], et_s[:], 0.0, starts[:, :, 0], ALU.is_equal, ALU.mult))
                            for r in range(1, R):
                                link(nc.vector.scalar_tensor_tensor(pick[:], et_s[:], float(r), starts[:, :, r], ALU.is_equal, ALU.mult))
                                last = nc.vector.tensor_tensor(part[:, 0], part[:, 0], pick[:], ALU.add)
                                if r < R - 1:
                                    link(last)
                        last.then_inc(part_ready, 1)
                    dve.wait_ge(target_in, 16 * heads)

                return Before(sync, pool, vector)

            return make

        gather_sum("l0", table0, edge_scores)

        with ExitStack() as st:
            tsb, tps = fresh(nc, st)
            deg = tsb("in_deg", [P, NB])
            root = tsb("in_root", [P, NB])
            count_ps = tps("count_ps", [P, 2, BANK])
            total = tsb("total", [P, NB])
            upto = tsb("upto", [P, NB])
            deg_done = sem("in_deg_done")
            deg_ready = sem("in_deg_ready")
            root_ready = sem("in_root_ready")
            counts_ready = sem("counts_ready")
            counts_done = sem("counts_done")
            chain = Count(sem("runstart_chain"))
            with nc.Block() as block:
                @block.vector
                def _(dve):
                    link = linked(dve, chain)
                    nc.vector.tensor_copy(total[:], agg[:, :, D]).then_inc(counts_ready, 1)
                    nc.vector.tensor_scalar(deg[:], agg[:, :, D], 1.0, None, ALU.max).then_inc(deg_ready, 1)
                    dve.wait_ge(counts_done, 1)
                    link(nc.vector.tensor_copy(total[:], count_ps[:, 1, 0:NB]))
                    link(nc.vector.tensor_tensor_scan(upto[:], ones[:, 0:NB], total[:], 0.0, ALU.mult, ALU.add))
                    link(nc.vector.tensor_tensor(upto[:], upto[:], total[:], ALU.subtract))
                    link(nc.vector.tensor_tensor(upto[:], upto[:], count_ps[:, 0, 0:NB], ALU.add))
                    link(nc.vector.scalar_tensor_tensor(upto[:], iota[:, 0:NB], float(P), upto[:], ALU.mult, ALU.add))
                    link(nc.vector.tensor_scalar(total[:], agg[:, :, D], 0.0, float(VP), ALU.is_equal, ALU.mult))
                    link(nc.vector.tensor_tensor(upto[:], upto[:], total[:], ALU.max))
                    link(nc.vector.tensor_copy(runstart[:], upto[:]))
                    dve.wait_ge(root_ready, 1)
                    link(nc.vector.reciprocal(in_scale[:], root[:]))

                @block.scalar
                def _(act):
                    act.wait_ge(deg_ready, 1)
                    nc.scalar.sqrt(root[:], deg[:]).then_inc(root_ready, 1)

                @block.tensor
                def _(pe):
                    pe.wait_ge(counts_ready, 1)
                    nc.tensor.matmul(count_ps[:, 0, 0:NB], below[:], total[:], start=True, stop=True)
                    nc.tensor.matmul(count_ps[:, 1, 0:NB], ones[:], total[:], start=True, stop=True).then_inc(counts_done, 1)
        recycle()

        with ExitStack() as layer:
            lsb, _ = fresh(nc, layer)
            node1 = lsb("node1", [P, NB, R])
            HALF = R // 2 * W1ROW

            def w1_load(sp, loaded):
                sp.dma_start(fc_s[:], fc.rearrange("r i o -> i r o")).then_inc(loaded, 16)
                sp.dma_start(attn_s[:], attn.rearrange("r k o -> (r k o)").partition_broadcast(D)).then_inc(loaded, 16)

            def w1_compute(dve, link, loaded, tsb, wsum):
                dve.wait_ge(loaded, 32)
                at = attn_s[:].rearrange("p (r k) -> p r k", r=R)
                link(nc.vector.tensor_tensor(prod[:], fc_s[:], at[:, :, 0:D], ALU.mult))
                link(nc.vector.reduce_sum(score_w[:, 0, :], prod[:], AX))
                link(nc.vector.tensor_tensor(prod[:], fc_s[:], at[:, :, D:2 * D], ALU.mult))
                link(nc.vector.reduce_sum(score_w[:, 1, :], prod[:], AX))
                for half in range(2):
                    to = wsum[:, half * (HALF + R):half * (HALF + R) + HALF].rearrange("p (r f) -> p r f", f=W1ROW)
                    rs = slice(half * R // 2, (half + 1) * R // 2)
                    link(nc.vector.tensor_copy(to[:, :, 0:D], fc_s[:, rs, :]))
                    link(nc.vector.tensor_copy(to[:, :, D], score_w[:, 0, rs]))
                return nc.vector.tensor_copy(wsum[:, HALF:HALF + R], score_w[:, 1, :])

            def keep1(z, half, stage, node, block, b):
                if half == 0:
                    nc.scalar.copy(node[:, bass.ds(block, 1), :], z[:, HALF:HALF + R].unsqueeze(1))
                return nc.scalar.copy(stage[:, b, half * HALF:(half + 1) * HALF], z[:, 0:HALF])

            def mean_sum(h, g):
                return nc.vector.tensor_tensor(h[:], agg[:, bass.ds(g * BPB, BPB), 0:D],
                                               in_scale[:, bass.ds(g * BPB, BPB)].unsqueeze(2).broadcast_to([P, BPB, D]), ALU.mult)

            with ExitStack() as st:
                tsb, _ = fresh(nc, st)
                fc_s = tsb("fc_s", [D, R, D])
                attn_s = tsb("attn_s", [D, R * 2 * D])
                prod = tsb("prod1", [D, R, D])
                score_w = tsb("score_w", [D, 2, R])
                table1_v = table1.rearrange("(b p r) f -> b p (r f)", p=P, r=R)
                node_layer("l0", w0a, b0a, w0b, b0b, D, ACT.Gelu, mean_sum,
                        2 * HALF + R, ((0, HALF + R), (HALF + R, 2 * HALF + R)), nodes1, spread1,
                        dict(buffers=lambda tsb: (tsb("stage1", [P, BPB, 2 * HALF]), node1),
                             ones=lambda link, stage: None,
                             keep=keep1,
                             store=lambda sp, stage, block, b: sp.dma_start(
                                 table1_v[bass.ds(block, 1)].rearrange("o p f -> (o p) f"), stage[:, b])),
                        dict(load=w1_load, compute=w1_compute))

            target = lsb("target1", [P, 1, V])
            attend("a1", table1, idx1_tl, W1ROW, W1ROW + 1, D, 1, target,
                   lambda s: nc.vector.tensor_scalar(s, s, 0.0, None, ALU.max),
                   target_rows("l1", R, 1, nodes1, spread1, target, 2, True))


        def attention_mean(tag, y, count, at, heads, width):
            chain = Count(sem(f"mean_chain_{tag}"))
            with nc.Block() as block:
                @block.vector
                def _(dve):
                    link = linked(dve, chain)
                    link(nc.vector.tensor_scalar(count, at(agg), 1.0e-30, None, ALU.max))
                    link(nc.vector.reciprocal(count, count))
                    a4 = agg[:, :, 0:heads * width].rearrange("p b (h d) -> p b h d", h=heads)[:, :, :, 0:D // heads]
                    for h in range(heads):
                        link(nc.vector.tensor_tensor(y[:, :, h * (D // heads):(h + 1) * (D // heads)], a4[:, :, h],
                                                     along(count[:, h], D // heads), ALU.mult))
                    link(nc.vector.tensor_tensor(y[:], y[:], xcur[:], ALU.add))

        with ExitStack() as st:
            tsb, _ = fresh(nc, st)
            y = tsb("y1", [P, NB, D])
            tmp = tsb("tmp1", [P, NB, D])
            small = tsb("small1", [P, 4, NB])
            count = tsb("count1", [P, 1, NB])
            attention_mean("l1", y, count[:], lambda a: a[:, :, D + 1].unsqueeze(1), 1, W1ROW + 1)
            normalise("l1", y, tmp, small,
                      lambda sp, done: (sp.dma_start(node_rows(table2), xcur[:]).then_inc(done, 16), 16)[1])
        recycle()

        gather_sum("l2", table2)
        with ExitStack() as st:
            tsb, tps = fresh(nc, st)
            eps_in = sem("eps_in")
            eps_done = Count(sem("eps_done"))
            with nc.Block() as block:
                @block.sync
                def _(sp):
                    sp.dma_start(eps_s[:], eps2.partition_broadcast(P)).then_inc(eps_in, 16)

                @block.vector
                def _(dve):
                    dve.wait_ge(eps_in, 16)
                    linked(dve, eps_done)(nc.vector.tensor_scalar(eps_s[:], eps_s[:], 1.0, None, ALU.add))
        recycle()

        with ExitStack() as layer:
            lsb, _ = fresh(nc, layer)
            node3 = lsb("node3", [P, NB, H])
            KEY = H * (HD + 1)

            def w3_load(sp, loaded):
                sp.dma_start(wn_s[:], wn).then_inc(loaded, 16)
                for n, a in enumerate((ak, aq)):
                    sp.dma_start(att_s[:, n], a.rearrange("h d -> (h d)").partition_broadcast(P)).then_inc(loaded, 16)

            def w3_compute(dve, link, loaded, tsb, wsum):
                dve.wait_ge(loaded, 16 * 3)
                link(nc.vector.memset(wsum[:], 0.0))
                link(nc.vector.tensor_copy(wsum[:, 0:KEY].rearrange("p (h d) -> p h d", h=H)[:, :, 0:HD], wn_s[:].rearrange("p (h d) -> p h d", h=H)))
                for n in range(2):
                    link(nc.vector.tensor_tensor(prod3[0:D], wn_s[:], att_s[0:D, n], ALU.mult))
                    last = nc.vector.reduce_sum(wsum[:, KEY + n * H:KEY + (n + 1) * H], prod3[0:D].rearrange("p (h d) -> p h d", h=H), AX)
                    if n == 0:
                        link(last)
                return last

            def keep3(z, half, stage, node, block, b):
                heads = z[:, 0:KEY].rearrange("p (h d) -> p h d", h=H)
                nc.scalar.copy(stage[:, b, 0:KEY].rearrange("p (h d) -> p h d", h=H)[:, :, 0:HD], heads[:, :, 0:HD])
                nc.scalar.copy(node[:, bass.ds(block, 1), :], z[:, KEY + H:KEY + 2 * H].unsqueeze(1))
                return nc.scalar.copy(stage[:, b, KEY:KEY + H], z[:, KEY:KEY + H])

            def own_and_sum(h, g):
                return nc.vector.scalar_tensor_tensor(h[:], xcur[:, bass.ds(g * BPB, BPB), :], eps_s[:, 0:1],
                                                      agg[:, bass.ds(g * BPB, BPB), 0:D], ALU.mult, ALU.add)

            with ExitStack() as st:
                tsb, _ = fresh(nc, st)
                wn_s = tsb("wn_s", [D, D])
                att_s = tsb("att_s", [P, 2, D])
                prod3 = tsb("prod3", [P, D])
                table3_v = table3.rearrange("(b p) f -> b p f", p=P)
                node_layer("l2", w2a, b2a, w2b, b2b, w2a.shape[1], ACT.Relu, own_and_sum,
                        KEY + 2 * H, ((0, KEY + 2 * H),), nodes3, spread3,
                        dict(buffers=lambda tsb: (tsb("stage3", [P, BPB, W3ROW]), node3),
                             ones=lambda link, stage: link(nc.vector.memset(stage[:], 1.0)),
                             keep=keep3,
                             store=lambda sp, stage, block, b: sp.dma_start(
                                 table3_v[bass.ds(block, 1)].rearrange("o p f -> (o p) f"), stage[:, b])),
                        dict(load=w3_load, compute=w3_compute))

            target = lsb("target3", [P, H, V])
            attend("a3", table3, src_tl, W3ROW, W3ROW, KEY, H, target,
                   lambda s: nc.vector.scalar_tensor_tensor(s, s, 0.01, s, ALU.mult, ALU.max),
                   target_rows("l3", H, H, nodes3, spread3, target, 13, False), we_d)


        with ExitStack() as st:
            tsb, _ = fresh(nc, st)
            y = tsb("y3", [P, NB, D])
            tmp = tsb("tmp3", [P, NB, D])
            small = tsb("small3", [P, 4, NB])
            count = tsb("count3", [P, H, NB])
            bias_s = tsb("bias_s", [P, D])
            bias_in = sem("bias_in")
            chain = Count(sem("bias_chain"))
            attention_mean("l3", y, count[:], lambda a: a[:, :, 0:KEY].rearrange("p b (h d) -> p h b d", h=H)[:, :, :, HD], H, HD + 1)
            with nc.Block() as block:
                @block.sync
                def _(sp):
                    sp.dma_start(bias_s[:], bias3.partition_broadcast(P)).then_inc(bias_in, 16)

                @block.vector
                def _(dve):
                    link = linked(dve, chain)
                    link(nc.vector.tensor_tensor(y[:], y[:], xcur[:], ALU.add))
                    dve.wait_ge(bias_in, 16)
                    link(nc.vector.tensor_tensor(y[:], y[:], bias_s[:].unsqueeze(1).broadcast_to([P, NB, D]), ALU.add))

            def store(sp, done):
                sp.dma_start(out[0:(NB - 1) * P, :].rearrange("(b p) f -> p b f", p=P), xcur[:, 0:NB - 1, :]).then_inc(done, 16)
                sp.dma_start(out[(NB - 1) * P:N, :], xcur[0:NLAST, NB - 1, :]).then_inc(done, 16)
                return 32

            normalise("l3", y, tmp, small, store)


_INS = ["x", "src", "dst", "edge_attr_64", "edge_type_8", "L0_gnn_w1", "L0_gnn_b1", "L0_gnn_w2", "L0_gnn_b2",
        "L1_gnn_fc_weight", "L1_gnn_attn_weight", "L2_gnn_eps", "L2_gnn_W1", "L2_gnn_b1", "L2_gnn_W2", "L2_gnn_b2",
        "L3_gnn_W_node", "L3_gnn_W_edge", "L3_gnn_attn_query", "L3_gnn_attn_key", "L3_gnn_attn_edge", "L3_gnn_bias"]


def kernel(**inputs):
    import numpy as np
    import concourse.bacc as bacc
    from concourse.bass_utils import run_bass_kernel_spmd

    nc = bacc.Bacc("TRN2", target_bir_lowering=False, num_devices=1)
    arrays, args = {}, []
    for name in _INS:
        a = np.ascontiguousarray(inputs[name])
        arrays[name] = a
        args.append(nc.dram_tensor(name, a.shape, mybir.dt.from_np(a.dtype), kind="ExternalInput").ap())
    args.append(nc.dram_tensor("out", (N, D), F32, kind="ExternalOutput").ap())
    build(nc, *args)
    return run_bass_kernel_spmd(nc, [arrays], core_ids=[0]).results[0]["out"]
```
